# Optimizing a Trainium2 kernel written in Bass

```python
import numpy as np
import jax
import jax.numpy as jnp

def _softmax(x, axis=-1):
    return jax.nn.softmax(x, axis=axis)

def _gelu(x):
    return jax.nn.gelu(x, approximate=True)

def _silu(x):
    return jax.nn.silu(x)

def _sigmoid(x):
    return jax.nn.sigmoid(x)

def _layernorm(x, axis=-1, eps=1e-05):
    m = jnp.mean(x, axis=axis, keepdims=True)
    v = jnp.var(x, axis=axis, keepdims=True)
    return (x - m) / jnp.sqrt(v + eps)

def _scatter_add(tgt, idx, src, axis=0):
    return tgt.at[idx].add(src)

def _segment_sum(src, seg, n):
    return jax.ops.segment_sum(src, seg, n)
kernel_name = 'mk_decoder_preln_d1_seqx_r4_b651c7'

def setup_inputs(seed: int=0):
    np.random.seed(seed)
    _w = jnp.asarray

    def _rec_inputs():
        import jax
        import jax.numpy as jnp
        _rk = jax.random.key(seed)
        x = 0.0001212 + 1 * jax.random.normal(jax.random.fold_in(_rk, 1), (8, 256, 256), jnp.float32)
        _lenS = 256 - jax.random.randint(jax.random.fold_in(_rk, 7), (8,), 0, max(1, 256 // 4) + 1, jnp.int32)
        _lenS2 = 256 - jax.random.randint(jax.random.fold_in(_rk, 8), (8,), 0, max(1, 256 // 4) + 1, jnp.int32)
        _ctx_1024P = jax.random.normal(jax.random.fold_in(_rk, 11), (8, 16, 256), jnp.float32)
        _ctx_1024c = jax.random.dirichlet(jax.random.fold_in(_rk, 511), 0.3 * jnp.ones((16,), jnp.float32), (8, 256))
        _ctx_1024t = jnp.einsum('bsk,bkd->bsd', _ctx_1024c, _ctx_1024P)
        _ctx_1024t = _ctx_1024t * jax.lax.rsqrt(jnp.mean(jnp.square(_ctx_1024t)) + 1e-12) * 0.953939
        ctx_1024 = -0.000125008 + 0.999885 * (_ctx_1024t + 0.3 * jax.random.normal(jax.random.fold_in(_rk, 611), (8, 256, 256), jnp.float32))
        return (x, ctx_1024)
    x, ctx_1024 = _rec_inputs()

    def _L0_attn_setup():
        import jax, jax.numpy as jnp
        import numpy as np
        D_MODEL = 256
        NHEAD = 16
        D_HEAD = D_MODEL // NHEAD
        THETA = 10000.0

        def _apply_rope(Q, K):
            B, H, T, D = Q.shape
            qr, qi = (Q.reshape(B, H, T, D // 2, 2)[..., 0], Q.reshape(B, H, T, D // 2, 2)[..., 1])
            kr, ki = (K.reshape(B, H, T, D // 2, 2)[..., 0], K.reshape(B, H, T, D // 2, 2)[..., 1])
            freqs = jnp.arange(D // 2, dtype=jnp.float32) * (1.0 / THETA)
            angles = jnp.arange(T, dtype=jnp.float32)[:, None] * freqs[None, :]
            cos = jnp.cos(angles)[None, None]
            sin = jnp.sin(angles)[None, None]
            qr2 = qr * cos - qi * sin
            qi2 = qr * sin + qi * cos
            kr2 = kr * cos - ki * sin
            ki2 = kr * sin + ki * cos
            Q2 = jnp.stack([qr2, qi2], axis=-1).reshape(B, H, T, D)
            K2 = jnp.stack([kr2, ki2], axis=-1).reshape(B, H, T, D)
            return (Q2, K2)
        key = jax.random.key(seed)
        ks = jax.random.split(key, 9)
        B, T = (4, 512)
        s = 1.0 / np.sqrt(D_MODEL)
        inp = {'x': jax.random.normal(ks[0], (B, T, D_MODEL), dtype=jnp.float32), 'Wq': jax.random.normal(ks[1], (D_MODEL, D_MODEL), dtype=jnp.float32) * s, 'bq': jnp.zeros((D_MODEL,), dtype=jnp.float32), 'Wk': jax.random.normal(ks[2], (D_MODEL, D_MODEL), dtype=jnp.float32) * s, 'bk': jnp.zeros((D_MODEL,), dtype=jnp.float32), 'Wv': jax.random.normal(ks[3], (D_MODEL, D_MODEL), dtype=jnp.float32) * s, 'bv': jnp.zeros((D_MODEL,), dtype=jnp.float32), 'Wo': jax.random.normal(ks[4], (D_MODEL, D_MODEL), dtype=jnp.float32) * s, 'bo': jnp.zeros((D_MODEL,), dtype=jnp.float32)}
        return inp
    _L0_attn_all = _L0_attn_setup()
    _L0_attn_in = {k: v for k, v in _L0_attn_all.items() if k in ('Wq', 'bq', 'Wk', 'bk', 'Wv', 'bv', 'Wo', 'bo')}
    del _L0_attn_all

    def _L0_xattn_setup():
        import jax, jax.numpy as jnp
        import numpy as np
        B, L, D_MODEL, N_HEADS = (4, 2048, 256, 16)
        D_DEPTH = D_MODEL // N_HEADS

        def _split_heads(x):
            b, l, _ = x.shape
            return x.reshape(b, l, N_HEADS, D_DEPTH).transpose(0, 2, 1, 3)

        def _combine_heads(x):
            b, _, l, _ = x.shape
            return x.transpose(0, 2, 1, 3).reshape(b, l, D_MODEL)
        key = jax.random.key(seed)
        ks = jax.random.split(key, 8)
        s = 1.0 / np.sqrt(D_MODEL)
        return {'v': jax.random.normal(ks[0], (B, L, D_MODEL), dtype=jnp.float32), 'k': jax.random.normal(ks[1], (B, L, D_MODEL), dtype=jnp.float32), 'q': jax.random.normal(ks[2], (B, L, D_MODEL), dtype=jnp.float32), 'wq_w': jax.random.normal(ks[3], (D_MODEL, D_MODEL), dtype=jnp.float32) * s, 'wq_b': jnp.zeros((D_MODEL,), jnp.float32), 'wk_w': jax.random.normal(ks[4], (D_MODEL, D_MODEL), dtype=jnp.float32) * s, 'wk_b': jnp.zeros((D_MODEL,), jnp.float32), 'wv_w': jax.random.normal(ks[5], (D_MODEL, D_MODEL), dtype=jnp.float32) * s, 'wv_b': jnp.zeros((D_MODEL,), jnp.float32), 'wc_w': jax.random.normal(ks[6], (D_MODEL, D_MODEL), dtype=jnp.float32) * s, 'wc_b': jnp.zeros((D_MODEL,), jnp.float32)}
    _L0_xattn_all = _L0_xattn_setup()
    _L0_xattn_in = {k: v for k, v in _L0_xattn_all.items() if k in ('wq_w', 'wq_b', 'wk_w', 'wk_b', 'wv_w', 'wv_b', 'wc_w', 'wc_b')}
    del _L0_xattn_all

    def _L0_ffn_setup():
        import jax, jax.numpy as jnp
        import numpy as np
        B, S, D, DFF, E, TOPK = (4, 512, 256, 1024, 8, 2)
        key = jax.random.key(seed)
        ks = jax.random.split(key, 7)
        scale_r = 1.0 / np.sqrt(D)
        scale_1 = 1.0 / np.sqrt(D)
        scale_2 = 1.0 / np.sqrt(DFF)
        return {'x': jax.random.normal(ks[0], (B, S, D), dtype=jnp.float32), 'Wr': jax.random.normal(ks[1], (D, E), dtype=jnp.float32) * scale_r, 'br': jnp.zeros((E,), dtype=jnp.float32), 'W1': jax.random.normal(ks[2], (E, D, DFF), dtype=jnp.float32) * scale_1, 'b1': jnp.zeros((E, DFF), dtype=jnp.float32), 'W2': jax.random.normal(ks[3], (E, DFF, D), dtype=jnp.float32) * scale_2, 'b2': jnp.zeros((E, D), dtype=jnp.float32)}
    _L0_ffn_all = _L0_ffn_setup()
    _L0_ffn_in = {k: v for k, v in _L0_ffn_all.items() if k in ('Wr', 'br', 'W1', 'b1', 'W2', 'b2')}
    del _L0_ffn_all
    return {'x': x, 'ctx_1024': ctx_1024, 'L0_attn_Wq': _L0_attn_in['Wq'], 'L0_attn_bq': _L0_attn_in['bq'], 'L0_attn_Wk': _L0_attn_in['Wk'], 'L0_attn_bk': _L0_attn_in['bk'], 'L0_attn_Wv': _L0_attn_in['Wv'], 'L0_attn_bv': _L0_attn_in['bv'], 'L0_attn_Wo': _L0_attn_in['Wo'], 'L0_attn_bo': _L0_attn_in['bo'], 'L0_xattn_wq_w': _L0_xattn_in['wq_w'], 'L0_xattn_wq_b': _L0_xattn_in['wq_b'], 'L0_xattn_wk_w': _L0_xattn_in['wk_w'], 'L0_xattn_wk_b': _L0_xattn_in['wk_b'], 'L0_xattn_wv_w': _L0_xattn_in['wv_w'], 'L0_xattn_wv_b': _L0_xattn_in['wv_b'], 'L0_xattn_wc_w': _L0_xattn_in['wc_w'], 'L0_xattn_wc_b': _L0_xattn_in['wc_b'], 'L0_ffn_Wr': _L0_ffn_in['Wr'], 'L0_ffn_br': _L0_ffn_in['br'], 'L0_ffn_W1': _L0_ffn_in['W1'], 'L0_ffn_b1': _L0_ffn_in['b1'], 'L0_ffn_W2': _L0_ffn_in['W2'], 'L0_ffn_b2': _L0_ffn_in['b2']}

def reference(x, ctx_1024, L0_attn_Wq, L0_attn_bq, L0_attn_Wk, L0_attn_bk, L0_attn_Wv, L0_attn_bv, L0_attn_Wo, L0_attn_bo, L0_xattn_wq_w, L0_xattn_wq_b, L0_xattn_wk_w, L0_xattn_wk_b, L0_xattn_wv_w, L0_xattn_wv_b, L0_xattn_wc_w, L0_xattn_wc_b, L0_ffn_Wr, L0_ffn_br, L0_ffn_W1, L0_ffn_b1, L0_ffn_W2, L0_ffn_b2):
    import jax
    import jax.numpy as jnp

    def _L0_attn_ref(x, Wq, bq, Wk, bk, Wv, bv, Wo, bo):
        import jax, jax.numpy as jnp
        import numpy as np
        D_MODEL = 256
        NHEAD = 16
        D_HEAD = D_MODEL // NHEAD
        THETA = 10000.0

        def _apply_rope(Q, K):
            B, H, T, D = Q.shape
            qr, qi = (Q.reshape(B, H, T, D // 2, 2)[..., 0], Q.reshape(B, H, T, D // 2, 2)[..., 1])
            kr, ki = (K.reshape(B, H, T, D // 2, 2)[..., 0], K.reshape(B, H, T, D // 2, 2)[..., 1])
            freqs = jnp.arange(D // 2, dtype=jnp.float32) * (1.0 / THETA)
            angles = jnp.arange(T, dtype=jnp.float32)[:, None] * freqs[None, :]
            cos = jnp.cos(angles)[None, None]
            sin = jnp.sin(angles)[None, None]
            qr2 = qr * cos - qi * sin
            qi2 = qr * sin + qi * cos
            kr2 = kr * cos - ki * sin
            ki2 = kr * sin + ki * cos
            Q2 = jnp.stack([qr2, qi2], axis=-1).reshape(B, H, T, D)
            K2 = jnp.stack([kr2, ki2], axis=-1).reshape(B, H, T, D)
            return (Q2, K2)
        B, T, d_model = x.shape
        Q = x @ Wq.T + bq
        K = x @ Wk.T + bk
        V = x @ Wv.T + bv
        Q = Q.reshape(B, T, NHEAD, D_HEAD).transpose(0, 2, 1, 3)
        K = K.reshape(B, T, NHEAD, D_HEAD).transpose(0, 2, 1, 3)
        V = V.reshape(B, T, NHEAD, D_HEAD).transpose(0, 2, 1, 3)
        Q, K = _apply_rope(Q, K)
        scores = jnp.einsum('bhqd,bhkd->bhqk', Q, K) / jnp.sqrt(jnp.float32(D_HEAD))
        attn = jax.nn.softmax(scores, axis=-1)
        out = jnp.einsum('bhqk,bhkd->bhqd', attn, V)
        out = out.transpose(0, 2, 1, 3).reshape(B, T, d_model)
        return out @ Wo.T + bo

    def _L0_xattn_ref(v, k, q, wq_w, wq_b, wk_w, wk_b, wv_w, wv_b, wc_w, wc_b):
        import jax, jax.numpy as jnp
        import numpy as np
        B, L, D_MODEL, N_HEADS = (4, 2048, 256, 16)
        D_DEPTH = D_MODEL // N_HEADS

        def _split_heads(x):
            b, l, _ = x.shape
            return x.reshape(b, l, N_HEADS, D_DEPTH).transpose(0, 2, 1, 3)

        def _combine_heads(x):
            b, _, l, _ = x.shape
            return x.transpose(0, 2, 1, 3).reshape(b, l, D_MODEL)
        q_heads = jax.nn.elu(_split_heads(q @ wq_w + wq_b)) + 1.0
        k_heads = jax.nn.elu(_split_heads(k @ wk_w + wk_b)) + 1.0
        v_heads = _split_heads(v @ wv_w + wv_b)
        k_cumsum = jnp.cumsum(k_heads, axis=1)
        attn_free = q_heads * (k_heads / k_cumsum) * v_heads
        return _combine_heads(attn_free) @ wc_w + wc_b

    def _L0_ffn_ref(x, Wr, br, W1, b1, W2, b2):
        import jax, jax.numpy as jnp
        import numpy as np
        B, S, D, DFF, E, TOPK = (4, 512, 256, 1024, 8, 2)
        router_logits = jnp.einsum('bsd,de->bse', x, Wr) + br
        topk_w, topk_idx = jax.lax.top_k(router_logits, TOPK)
        topk_w = jax.nn.softmax(topk_w, axis=-1)
        one_hot = jax.nn.one_hot(topk_idx, E, dtype=x.dtype)
        gates = jnp.einsum('bsk,bske->bse', topk_w, one_hot)
        out = jnp.zeros_like(x)
        for e in range(E):
            h = jax.nn.gelu(jnp.einsum('bsd,df->bsf', x, W1[e]) + b1[e])
            y = jnp.einsum('bsf,fd->bsd', h, W2[e]) + b2[e]
            out = out + gates[:, :, e, None] * y
        return out
    x = x + _L0_attn_ref(_layernorm(x, axis=-1), L0_attn_Wq, L0_attn_bq, L0_attn_Wk, L0_attn_bk, L0_attn_Wv, L0_attn_bv, L0_attn_Wo, L0_attn_bo)
    x = x + _L0_xattn_ref(ctx_1024, ctx_1024, _layernorm(x, axis=-1), L0_xattn_wq_w, L0_xattn_wq_b, L0_xattn_wk_w, L0_xattn_wk_b, L0_xattn_wv_w, L0_xattn_wv_b, L0_xattn_wc_w, L0_xattn_wc_b)
    x = x + _L0_ffn_ref(_layernorm(x, axis=-1), L0_ffn_Wr, L0_ffn_br, L0_ffn_W1, L0_ffn_b1, L0_ffn_W2, L0_ffn_b2)
    return x

_drawn_inputs = setup_inputs


def setup_inputs(seed=0):
    import zlib

    import numpy as np

    out = dict(_drawn_inputs(seed))
    spreads = {'L0_attn_bq': (0.0, 0.1),
     'L0_attn_bk': (0.0, 0.1),
     'L0_attn_bv': (0.0, 0.1),
     'L0_attn_bo': (0.0, 0.1),
     'L0_xattn_wq_b': (0.0, 0.1),
     'L0_xattn_wk_b': (0.0, 0.1),
     'L0_xattn_wv_b': (0.0, 0.1),
     'L0_xattn_wc_b': (0.0, 0.1),
     'L0_ffn_br': (0.0, 0.1),
     'L0_ffn_b1': (0.0, 0.1),
     'L0_ffn_b2': (0.0, 0.1)}
    factors = {}
    for name, (base, spread) in spreads.items():
        noise = np.random.default_rng([zlib.crc32(name.encode()), seed]).standard_normal(out[name].shape)
        drawn = base * np.exp(spread * noise) if base else spread * noise
        out[name] = jnp.asarray(drawn.astype(out[name].dtype))
    for name, factor in factors.items():
        out[name] = (out[name] * factor).astype(out[name].dtype)
    return out
```

```python
from contextlib import ExitStack

import numpy as np

import concourse.bass as bass
from concourse import mybir

F32 = mybir.dt.float32
F16 = mybir.dt.float16
I32 = mybir.dt.int32
U32 = mybir.dt.uint32
ALU = mybir.AluOpType
ACT = mybir.ActivationFunctionType
AX = mybir.AxisListType

P = 128
BATCH, SEQ, D = 8, 256, 256
H, DH = 16, 16
KD = D // P
T = SEQ // P
NT = BATCH * T
PAIRS = H // 2
QUADS = H // 4
STACK = 64
E, TOP, DFF = 8, 2, 1024
KF = DFF // P
WSCALE = 256.0
TOKENS = BATCH * SEQ
NB = (TOKENS * TOP) // P + E - 1
ROWS = TOKENS + P
EPS = 1e-5
SCALE = float(DH) ** -0.5
THETA = 10000.0

ROW_MAX = 32

U_XNT, U_QK, U_V, S1_USES = 0, (1, 3), (2, 4), 5
U_QT, U_KT, U_SC, U_RT, S2_USES = (0, 1), (2, 3), 4, (20, 21), 22
U_WO, O_USES = 2, 3
GROUPS = QUADS * T


def rope_tables():
    freqs = np.arange(DH // 2, dtype=np.float32) * np.float32(1.0 / THETA)
    angles = np.arange(SEQ, dtype=np.float32)[:, None] * freqs[None, :]
    cos, sin = np.cos(angles), np.sin(angles)
    return (np.concatenate([cos, cos], 1).astype(np.float32),
            np.concatenate([-sin, sin], 1).astype(np.float32))


def head_cumsum_matrix():
    f = np.arange(D)
    same = (f[:, None] % DH) == (f[None, :] % DH)
    return (same & (f[:, None] // DH <= f[None, :] // DH)).astype(np.float32)


def routing_constants():
    e, p = np.arange(E), np.arange(P)[:, None]
    before = np.concatenate([e[None, :] < e[:, None], e[None, :] <= e[:, None]])
    columns = {
        "experts": e, "positions": np.arange(P), "blocks": np.arange(NB), "block_floors": P * np.arange(TOKENS // P),
        "before": before.reshape(-1),
        "tokens": P * np.arange(NT)[None, :] + p - 2 * TOKENS,
        "spare_row": p - TOKENS,
    }
    return {k: np.broadcast_to(v, (P, v.shape[-1])).astype(np.float32) for k, v in columns.items()}


def routing_columns():
    widths = {k: v.shape[1] for k, v in routing_constants().items()}
    starts = np.cumsum([0, *widths.values()]).tolist()
    return starts[-1], {k: (at, n) for (k, n), at in zip(widths.items(), starts)}


def rank_matrices():
    p = np.arange(P)
    return np.concatenate([p[:, None] < p[None, :], np.ones((P, P), bool)], 1).astype(np.float16)


def build(nc, x, ctxT, w_qkv, b_qkv, w_o, b_o, wx_q, wx_k, wx_v, wx_c, bx_q, bx_k, bx_v, bx_c,
          wr, br, w1, b1, w2, b2, cos, sin, cumsum_m, ident, rank_m, route_c, rows, out):
    with ExitStack() as ctx:
        scope = ctx

        def sb(name, shape, dt=F32):
            return scope.enter_context(nc.sbuf_tensor(name, shape, dt))

        def sem(name):
            return ctx.enter_context(nc.semaphore(name))

        X = sb("X", [P, (NT + T) * D])
        wxq_sb = sb("wxq_sb", [P, KD, D])
        wxk_sb = sb("wxk_sb", [P, KD, D])
        wxv_sb = sb("wxv_sb", [P, KD, D])
        wxc_sb = sb("wxc_sb", [P, KD, D])
        bxq_sb = sb("bxq_sb", [P, KD])
        bxk_sb = sb("bxk_sb", [P, KD])
        bxv_sb = sb("bxv_sb", [P, KD])
        bxc_sb = sb("bxc_sb", [P, D])
        cum_sb = sb("cum_sb", [P, KD, D])
        wr_sb = sb("wr_sb", [P, KD, E])
        br_sb = sb("br_sb", [P, E])
        b1_sb = sb("b1_sb", [P, E * KF])
        id_sb = sb("id_sb", [P, P])
        id16 = sb("id16", [P, P], F16)
        stats = sb("stats", [P, 4, 6])
        mv = sb("mv", [P, 4, 2])
        var_eps = sb("var_eps", [P, 4])
        minus_half = sb("minus_half", [P, 4])
        guess = sb("guess", [P, 4])
        newton = sb("newton", [P, 3, 4])
        rstd = sb("rstd", [P, 4])
        xn = sb("xn", [P, 4, D])
        top_v = sb("top_v", [P, TOP, NT])
        top_e = sb("top_e", [P, TOP, NT])
        W1 = sb("W1", [P, E, KD, 2, DFF], F16)
        staged = [sb(f"staged{i}", [P, DFF]) for i in range(2)]

        attention = ctx.enter_context(ExitStack())
        scope = attention
        wqkv_sb = sb("wqkv_sb", [P, KD, 3 * D])
        bqkv_sb = sb("bqkv_sb", [P, 3 * D])
        wo_sb = sb("wo_sb", [P, QUADS, D])
        bo_sb = sb("bo_sb", [P, D])
        cos_sb = sb("cos_sb", [P, T, DH])
        sin_sb = sb("sin_sb", [P, T, DH])
        xnT = sb("xnT", [P, KD, SEQ])
        qk = sb("qk", [P, T, 2 * D])
        rot_c = sb("rot_c", [P, T, 2 * D])
        rot_s = sb("rot_s", [P, T, 2 * D])
        roped = rot_c
        v_raw = sb("v_raw", [P, T, D])
        q_stack = [sb(f"q_stack{i}", [P, T, H, STACK], F16) for i in range(2)]
        k_stack = [sb(f"k_stack{i}", [P, T, H, STACK], F16) for i in range(2)]
        qT = sb("qT", [P, PAIRS, SEQ], F16)
        mx = sb("mx", [P, T, H])
        qmT = [sb(f"qmT{i}", [P, PAIRS, SEQ], F16) for i in range(2)]
        kT = [sb(f"kT{i}", [P, H, SEQ], F16) for i in range(2)]
        v1 = [sb(f"v1{i}", [P, T, H, 2 * DH]) for i in range(2)]
        probs = [sb(f"probs{i}", [P, 4, SEQ]) for i in range(2)]
        o_rows = sb("o_rows", [P, 2 * SEQ // 32, 32])
        rsums = sb("rsums", [P, 2 * SEQ // 32])
        oT = sb("oT", [P, QUADS, SEQ])
        attention.close()

        scope = ctx
        W2 = sb("W2", [P, E, KF, 2, D], F16)
        XC = 4 * P
        NC = TOKENS // XC
        TC = XC // P
        cross = ctx.enter_context(ExitStack())
        scope = cross
        ctx_sb = [sb(f"ctx_sb{i}", [P, KD, XC]) for i in range(2)]
        xT = sb("xT", [P, KD, XC])
        k_exp = sb("k_exp", [P, KD, XC])
        relu = sb("relu", [P, KD, XC])
        mix = sb("mix", [P, KD, XC])
        q_exp = sb("q_exp", [P, KD, XC])
        xn3 = sb("xn3", [P, TC, D])
        xs = sb("xs", [P, TC, 2 * D], F16)
        lg = sb("lg", [P, TC, E])
        best_v = sb("best_v", [P, TC, 8])
        best_e = sb("best_e", [P, TC, 8], U32)
        cross.close()

        scope = ctx
        b2_sb = sb("b2_sb", [P, E, D])
        xg = [sb(f"xg{i}", [P, 2 * D], F16) for i in range(2)]
        xgT = [sb(f"xgT{i}", [P, 2, KD, P], F16) for i in range(2)]
        RC, RC_AT = routing_columns()
        route_sb = sb("route_sb", [P, RC])
        rank_sb = sb("rank_sb", [P, 2 * P], F16)
        gates = sb("gates", [P, TOP, NT])
        block_gates = sb("block_gates", [P, NB])
        block_scales = sb("block_scales", [P, NB])
        block_rows = sb("block_rows", [P, NB], I32)
        block_expert = sb("block_expert", [P, NB], I32)
        gather_ids = [sb(f"gather_ids{i}", [P, 1], I32) for i in range(2)]
        add_ids = [sb(f"add_ids{i}", [P, 1], I32) for i in range(2)]
        routing = ctx.enter_context(ExitStack())
        scope = routing
        oh = sb("oh", [P, TOP, NT, E])
        oh_any = sb("oh_any", [P, NT + 1, E], F16)
        v_gap = sb("v_gap", [P, NT])
        v_exp = sb("v_exp", [P, NT])
        v_sum = sb("v_sum", [P, NT])
        above = sb("above", [P, E, TOKENS // P])
        expert_blocks = sb("expert_blocks", [P, E])
        bounds_of = sb("bounds_of", [P, 2 * E, E])
        bounds = sb("bounds", [P, 2 * E])
        place_of = sb("place_of", [P, NT, E])
        oh_place = sb("oh_place", [P, TOP, NT, E])
        place = sb("place", [P, TOP * NT])
        place_i = sb("place_i", [P, TOP * NT], I32)
        block_i = sb("block_i", [P, TOP * NT], I32)
        block_f = sb("block_f", [P, TOP * NT])
        pos = sb("pos", [P, TOP * NT])
        table = sb("table", [P, TOP * NT, 2, NB])
        reached = sb("reached", [P, NB, E])
        owner = sb("owner", [P, NB])
        spare_ids = sb("spare_ids", [P, NB])
        pos_oh = [s[:, :].rearrange("p (j q) -> p j q", q=P) for s in staged]
        routing.close()
        scope = ctx
        hid = [sb(f"hid{i}", [P, KF, P]) for i in range(2)]
        hid_hi = [sb(f"hid_hi{i}", [P, KF, P], F16) for i in range(2)]
        hid_lo = [sb(f"hid_lo{i}", [P, KF, P], F16) for i in range(2)]
        gated_b2 = [sb(f"gated_b2{i}", [P, D]) for i in range(2)]
        y = [sb(f"y{i}", [P, D]) for i in range(2)]

        def const(name):
            at_, n = RC_AT[name]
            return route_sb[:, at_:at_ + n]

        s1_ps = ctx.enter_context(nc.psum_tensor("s1_ps", [P, 512], F32))
        s2_ps = [ctx.enter_context(nc.psum_tensor(f"s2_ps{i}", [P, 512], F32)) for i in range(2)]
        o_ps = ctx.enter_context(nc.psum_tensor("o_ps", [P, 512], F32))
        s_ps = [ctx.enter_context(nc.psum_tensor(f"s_ps{i}", [P, 4, SEQ], F32)) for i in range(2)]
        s_halves = [s_ps[i][:, 2 * j:2 * j + 2, :].rearrange("p h s -> p (h s)") for i in range(2) for j in range(2)]
        xT_ps = [s1_ps[:, :], o_ps[:, :]]
        kv_ps = [s2_ps[0][:, :], s2_ps[1][:, :]]
        cq_ps, wc_ps = s_halves[0:2], s_halves[2:4]
        rank_ps = s2_ps[0][:, 0:(NT + 1) * E].rearrange("p (t e) -> p t e", e=E)
        table_ps = s2_ps[1][:, 0:2 * NB]
        xgT_ps = [bank[:, 0:D].bitcast(F16).rearrange("p (h k s) -> p h k s", h=2, k=KD) for bank in (s1_ps, o_ps)]
        hid_ps = [s_ps[i][:, :, :].rearrange("p h s -> p (h s)").rearrange("p (m s) -> p m s", s=P) for i in range(2)]
        y_ps = [bank[:, 0:D] for bank in s2_ps]

        x0_loaded = sem("x0_loaded")
        x_loaded = sem("x_loaded")
        wqkv_loaded = sem("wqkv_loaded")
        wo_loaded = sem("wo_loaded")
        cross_loaded = sem("cross_loaded")
        stacks_cleared = sem("stacks_cleared")
        consts_set = sem("consts_set")
        id16_ready = sem("id16_ready")
        ln_stats = sem("ln_stats")
        ln_mv = sem("ln_mv")
        var_ready = sem("var_ready")
        guess_ready = sem("guess_ready")
        newton_step = sem("newton_step")
        ln_rstd = sem("ln_rstd")
        xn_ready = sem("xn_ready")
        s1_done = sem("s1_done")
        s1_moved = sem("s1_moved")
        v_ready = sem("v_ready")
        s2_done = sem("s2_done")
        s2_moved = [sem(f"s2_moved{i}") for i in range(2)]
        rot_c_ready = sem("rot_c_ready")
        rot_s_ready = sem("rot_s_ready")
        roped_ready = sem("roped_ready")
        hi_ready = sem("hi_ready")
        lo_ready = sem("lo_ready")
        negm_ready = sem("negm_ready")
        xb_ready = sem("xb_ready")
        scores_ready = sem("scores_ready")
        exp_done = sem("exp_done")
        pv_done = sem("pv_done")
        o_scaled = sem("o_scaled")
        oT_ready = sem("oT_ready")
        rsums_ready = sem("rsums_ready")
        o_moved = sem("o_moved")
        wo_done = sem("wo_done")
        k_done = sem("k_done")
        k_moved = sem("k_moved")
        cum_done = sem("cum_done")
        cum_moved = sem("cum_moved")
        v_done = sem("v_done")
        v_moved = sem("v_moved")
        xnT_done = sem("xnT_done")
        xnT_moved = sem("xnT_moved")
        q_done = sem("q_done")
        q_moved = sem("q_moved")
        x3T_done = sem("x3T_done")
        x3T_moved = sem("x3T_moved")
        logits_done = sem("logits_done")
        logits_moved = sem("logits_moved")
        wc_done = sem("wc_done")
        wc_moved = sem("wc_moved")
        ctx_loaded = sem("ctx_loaded")
        xc_ready = sem("xc_ready")
        xc_normed = sem("xc_normed")
        x3_normed = sem("x3_normed")
        k_heads_ready = sem("k_heads_ready")
        ratio_ready = sem("ratio_ready")
        q_heads_ready = sem("q_heads_ready")
        mixed_ready = sem("mixed_ready")
        x3_high = sem("x3_high")
        x3_low = sem("x3_low")
        rows_stored = sem("rows_stored")
        x_stored = sem("x_stored")
        spare_stored = sem("spare_stored")
        best_found = sem("best_found")
        best_kept = sem("best_kept")
        route_loaded = sem("route_loaded")
        b2_loaded = sem("b2_loaded")
        zeros_set = sem("zeros_set")
        gap_ready = sem("gap_ready")
        gap_exp = sem("gap_exp")
        choices_ready = sem("choices_ready")
        ranks_done = sem("ranks_done")
        routed = sem("routed")
        table_ready = sem("table_ready")
        pos_ready = sem("pos_ready")
        pos_used = sem("pos_used")
        table_done = sem("table_done")
        experts_ready = sem("experts_ready")
        ids_ready = sem("ids_ready")
        ids_copied = sem("ids_copied")
        xg_transposed = sem("xg_transposed")
        xgT_moved = sem("xgT_moved")
        first_done = sem("first_done")
        gelu_done = sem("gelu_done")
        hi_split = sem("hi_split")
        lo_split = sem("lo_split")
        second_done = sem("second_done")
        gated_b2_ready = sem("gated_b2_ready")
        y_ready = sem("y_ready")
        added = sem("added")
        gathered = [sem(f"gathered{i}") for i in range(2)]
        w_loaded = [sem(f"w_loaded{i}") for i in range(2)]
        w_scaled = sem("w_scaled")
        w_high = sem("w_high")
        w_low = sem("w_low")

        def s2_slot(b, u):
            return u % 2, S2_USES // 2 * b + u // 2

        def at(eng, count):
            return count if isinstance(count, int) else eng.to_reg(count)

        def seq_rows(b):
            return X[:, bass.ds(b * T * D, T * D)].rearrange("p (t d) -> p t d", t=T)

        def iterations(eng, step):
            step(-2, 0, (True, False, False))
            step(-1, 1, (True, True, False))
            with eng.Fori(0, (BATCH - 2) // 2) as two:
                step(2 * two, 0, (True, True, True))
                step(2 * two + 1, 1, (True, True, True))
            step(BATCH - 2, 0, (False, True, True))
            step(BATCH - 1, 1, (False, False, True))

        def cross_steps(eng, step):
            step(0, 0, False, True)
            with eng.Fori(0, (NC - 2) // 2) as two:
                step(2 * two + 1, 1, True, True)
                step(2 * two + 2, 0, True, True)
            step(NC - 1, 1, True, False)

        def blocks_in_turn(eng, step):
            step(0, 0, 3)
            step(0, 1, 3)
            with eng.Fori(1, (NB - 3) // 2) as two:
                step(two, 0, 3)
                step(two, 1, 3)
            for i in range(NB - 3, NB):
                step(i // 2, i % 2, NB - 1 - i)

        XN0 = T * (BATCH + 1)

        block = ctx.enter_context(nc.Block())

        @block.sync
        def _(sp):
            xv = x.rearrange("(t p) d -> p t d", p=P)
            Xv = X[:, :].rearrange("p (t d) -> p t d", d=D)
            sp.dma_start(Xv[:, 0:T, :], xv[:, 0:T, :]).then_inc(x0_loaded, 16)
            sp.dma_start(id_sb[:, :], ident).then_inc(x0_loaded, 16)
            sp.dma_start(wqkv_sb[:, :, :], w_qkv.rearrange("(k p) n -> p k n", p=P)).then_inc(wqkv_loaded, 16)
            sp.dma_start(bqkv_sb[:, :], b_qkv.partition_broadcast(P)).then_inc(wqkv_loaded, 16)
            sp.dma_start(cos_sb[:, :, :], cos.rearrange("(t p) n -> p t n", p=P)).then_inc(wqkv_loaded, 16)
            sp.dma_start(sin_sb[:, :, :], sin.rearrange("(t p) n -> p t n", p=P)).then_inc(wqkv_loaded, 16)
            sp.dma_start(Xv[:, T:NT, :], xv[:, T:, :]).then_inc(x_loaded, 16)
            sp.dma_start(wo_sb[:, :, :], w_o.rearrange("(k p) n -> p k n", p=P)).then_inc(wo_loaded, 16)
            sp.dma_start(bo_sb[:, :], b_o.partition_broadcast(P)).then_inc(wo_loaded, 16)

            for k in range(KD):
                sp.dma_start(staged[k][:, :], w1[0, k * P:(k + 1) * P, :]).then_inc(w_loaded[k], 16)
            for dst, src in ((wxq_sb, wx_q), (wxk_sb, wx_k), (wxv_sb, wx_v), (wxc_sb, wx_c), (cum_sb, cumsum_m),
                             (wr_sb, wr)):
                sp.dma_start(dst[:, :, :], src.rearrange("(k p) n -> p k n", p=P)).then_inc(cross_loaded, 16)
            for dst, src in ((bxq_sb, bx_q), (bxk_sb, bx_k), (bxv_sb, bx_v), (b1_sb, b1)):
                sp.dma_start(dst[:, :], src.rearrange("(k p) -> p k", p=P),
                             allow_slow_non_contiguous=True).then_inc(cross_loaded, 16)
            for dst, src in ((bxc_sb, bx_c), (br_sb, br)):
                sp.dma_start(dst[:, :], src.partition_broadcast(P)).then_inc(cross_loaded, 16)
            sp.wait_ge(consts_set, 8)
            spare = X[:, NT * D:(NT + 1) * D]
            sp.dma_start(out[TOKENS:, :], spare).then_inc(spare_stored, 16)
            sp.dma_start(rows[TOKENS:, :], spare.bitcast(F16)).then_inc(spare_stored, 16)
            with sp.Fori(1, E) as e:
                for k in range(KD):
                    sp.wait_ge(w_low, 2 * e + k - 1)
                    sp.dma_start(staged[k][:, :], w1[bass.ds(e, 1), k * P:(k + 1) * P, :]
                                 .rearrange("e p n -> (e p) n")).then_inc(w_loaded[k], 16)

            def second_layer(c, u):
                sp.wait_ge(w_low, 2 * E + 4 * c + u - 1)
                half = KF // 2
                src = w2[bass.ds(2 * c + u // 2, 1), (u % 2) * half * P:(u % 2 + 1) * half * P, :]
                sp.dma_start(staged[u % 2][:, :].rearrange("p (k n) -> p k n", n=D),
                             src.rearrange("e (k p) n -> p (e k) n", p=P)).then_inc(w_loaded[u % 2], 16)

            def load_ctx(c, o):
                if not isinstance(c, int) or c > 0:
                    sp.wait_ge(ctx_loaded, 16 * c)
                sp.dma_start(ctx_sb[o][:, :, :], ctxT[:, bass.ds(c * XC, XC)].rearrange("(k p) n -> p k n", p=P)
                             ).then_inc(ctx_loaded, 16)

            def store_x(c):
                sp.wait_ge(wc_moved, 2 * c + 2)
                sp.dma_start(out[bass.ds(c * XC, XC), :].rearrange("(t p) d -> p t d", p=P),
                             X[:, bass.ds(c * TC * D, TC * D)].rearrange("p (t d) -> p t d", d=D)).then_inc(x_stored, 16)

            def store_rows(c):
                sp.wait_ge(x3_high, c + 1)
                sp.wait_ge(x3_low, c + 1)
                sp.dma_start(rows[bass.ds(c * XC, XC), :].rearrange("(t p) d -> p t d", p=P),
                             xs[:, :, :]).then_inc(rows_stored, 16)

            sp.wait_ge(o_moved, 1 + O_USES * BATCH)
            load_ctx(0, 0)
            load_ctx(1, 1)

            def cross_step(c, o, has_last, has_next):
                second_layer(c, 0)
                second_layer(c, 1)
                if has_last:
                    store_x(c - 1)
                    if has_next:
                        sp.wait_ge(k_done, KD * c + KD)
                        sp.wait_ge(v_done, KD * c)
                        load_ctx(c + 1, 1 - o)
                second_layer(c, 2)
                second_layer(c, 3)
                if has_last:
                    store_rows(c - 1)

            cross_steps(sp, cross_step)
            store_x(NC - 1)
            sp.dma_start(route_sb[:, :], route_c).then_inc(route_loaded, 16)
            sp.dma_start(rank_sb[:, :], rank_m).then_inc(route_loaded, 16)
            sp.dma_start(b2_sb[:, :, :].rearrange("p e n -> p (e n)"),
                         b2.rearrange("e n -> (e n)").partition_broadcast(P)).then_inc(b2_loaded, 16)
            store_rows(NC - 1)
            sp.wait_ge(spare_stored, 32)
            sp.wait_ge(x_stored, 16 * NC)
            sp.wait_ge(rows_stored, 16 * NC)
            sp.wait_ge(added, 16 * NB)

        CROSS_LOADS = 12 * 16

        @block.gpsimd
        def _(pool):
            for i in range(2):
                nc.gpsimd.memset(q_stack[i][:, :, :, :], 0.0).then_inc(stacks_cleared, 1)
                nc.gpsimd.memset(k_stack[i][:, :, :, :], 0.0).then_inc(stacks_cleared, 1)
            nc.gpsimd.memset(X[:, NT * D:], 0.0).then_inc(consts_set, 1)
            nc.gpsimd.memset(minus_half[:, :], -0.5).then_inc(consts_set, 1)
            pool.wait_ge(stacks_cleared, 4)
            for i in range(2):
                nc.gpsimd.memset(k_stack[i][:, :, :, ROW_MAX:ROW_MAX + 1], 1.0).then_inc(consts_set, 1)
                nc.gpsimd.memset(kT[i][:, :, :], 0.0).then_inc(consts_set, 1)
                nc.gpsimd.memset(v1[i][:, :, :, DH:], 1.0).then_inc(consts_set, 1)
            pool.wait_ge(consts_set, 8)

            def inverse_deviation(n, tiles, stats_done):
                c = slice(0, tiles)
                stats_done, halved = at(pool, stats_done), at(pool, 3 * n + 2)
                pool.wait_ge(stacks_cleared, 4)
                pool.wait_ge(ln_mv, stats_done)
                nc.gpsimd.tensor_scalar(var_eps[:, c], mv[:, c, 1], EPS, None, ALU.add).then_inc(var_ready, 1)
                pool.wait_ge(var_ready, n + 1)
                nc.gpsimd.tensor_tensor(guess[:, c], var_eps[:, c], minus_half[:, c], ALU.pow).then_inc(guess_ready, 1)
                pool.wait_ge(guess_ready, n + 1)
                nc.gpsimd.tensor_tensor(newton[:, 0, c], guess[:, c], guess[:, c], ALU.mult).then_inc(newton_step, 1)
                pool.wait_ge(newton_step, 3 * n + 1)
                nc.gpsimd.tensor_tensor(newton[:, 1, c], newton[:, 0, c], var_eps[:, c], ALU.mult).then_inc(newton_step, 1)
                pool.wait_ge(stacks_cleared, 4)
                pool.wait_ge(newton_step, halved)
                nc.gpsimd.tensor_scalar(newton[:, 2, c], newton[:, 1, c], -0.5, 1.5, ALU.mult, ALU.add).then_inc(newton_step, 1)
                pool.wait_ge(newton_step, 3 * n + 3)
                nc.gpsimd.tensor_tensor(rstd[:, c], guess[:, c], newton[:, 2, c], ALU.mult).then_inc(ln_rstd, 1)

            def values(b, o):
                for u in U_V:
                    pool.wait_ge(s1_moved, S1_USES * b + u + 1)
                if not isinstance(b, int) or b >= 2:
                    pool.wait_ge(pv_done, GROUPS * (b - 1) + 1)
                nc.gpsimd.tensor_tensor(v1[o][:, :, :, 0:DH], v_raw[:, :, :].rearrange("p t (h d) -> p t h d", d=DH),
                                        bqkv_sb[:, 2 * D:].rearrange("p (h d) -> p h d", d=DH).unsqueeze(1)
                                        .to_broadcast([P, T, H, DH]), ALU.add).then_inc(v_ready, 1)

            def low_parts(b):
                for k in range(KD):
                    high = at(pool, 2 * b + k + 1)
                    pool.wait_ge(stacks_cleared, 4)
                    pool.wait_ge(w_high, high)
                    dst = W1[:, bass.ds(b, 1), k, :, :]
                    nc.gpsimd.tensor_tensor(dst[:, 0, 1, :], staged[k][:, :], dst[:, 0, 0, :],
                                            ALU.subtract).then_inc(w_low, 1)

            def rotate(b, o):
                pool.wait_ge(xn_ready, T * b + T)
                rows = seq_rows(b)
                nc.gpsimd.tensor_tensor(rows, rows, bo_sb[:, :].unsqueeze(1).to_broadcast([P, T, D]),
                                        ALU.add).then_inc(xb_ready, 1)
                for t in range(T):
                    pool.wait_ge(s1_moved, S1_USES * b + U_QK[t] + 1)
                    nc.gpsimd.tensor_tensor(
                        rot_c[:, t, :].rearrange("p (h d) -> p h d", d=DH),
                        qk[:, t, :].rearrange("p (h d) -> p h d", d=DH),
                        cos_sb[:, t, :].unsqueeze(1).to_broadcast([P, 2 * H, DH]), ALU.mult).then_inc(rot_c_ready, 1)
                for t in range(T):
                    pool.wait_ge(rot_c_ready, T * b + t + 1)
                    pool.wait_ge(rot_s_ready, T * b + t + 1)
                    nc.gpsimd.tensor_tensor(roped[:, t, :], rot_c[:, t, :], rot_s[:, t, :], ALU.add).then_inc(roped_ready, 1)
                for t in range(T):
                    heads = roped[:, t, :].rearrange("p (w h d) -> p w h d", w=2, d=DH)
                    qs, ks = q_stack[o][:, t], k_stack[o][:, t]
                    high = at(pool, 2 * T * b + 2 * t + 2)
                    pool.wait_ge(stacks_cleared, 4)
                    pool.wait_ge(hi_ready, high)
                    nc.gpsimd.memset(qs[:, :, ROW_MAX:ROW_MAX + 1], 0.0).then_inc(lo_ready, 1)
                    nc.gpsimd.tensor_tensor(qs[:, :, 48:64], heads[:, 0], qs[:, :, 0:16], ALU.subtract).then_inc(lo_ready, 1)
                    nc.gpsimd.tensor_tensor(ks[:, :, 16:32], heads[:, 1], ks[:, :, 0:16], ALU.subtract).then_inc(lo_ready, 1)

            def shifts(b, o):
                for t in range(T):
                    last_two = [s2_slot(b, U_SC + g) for g in (PAIRS * t + PAIRS - 2, PAIRS * t + PAIRS - 1)]
                    moved = [at(pool, n + 1) for _, n in last_two]
                    pool.wait_ge(stacks_cleared, 4)
                    for (bank, _), n in zip(last_two, moved):
                        pool.wait_ge(s2_moved[bank], n)
                    nc.gpsimd.tensor_scalar(q_stack[o][:, t, :, ROW_MAX], mx[:, t, :], -1.0, None,
                                            ALU.mult).then_inc(negm_ready, 1)

            def step(j, o, stages):
                if stages[1]:
                    values(j + 1, 1 - o)
                if stages[0]:
                    rotate(j + 2, o)
                    low_parts(j + 2)
                    inverse_deviation(j + 3, T, T * (j + 3) + T)
                if stages[1]:
                    shifts(j + 1, 1 - o)

            inverse_deviation(0, T, T)
            pool.wait_ge(wqkv_loaded, 64)
            pool.wait_ge(wo_loaded, 32)
            iterations(pool, step)

            pool.wait_ge(cross_loaded, CROSS_LOADS)
            LN0 = BATCH + 1
            inverse_deviation(LN0, TC, XN0 + TC)

            def second_low(c, u):
                high = at(pool, 2 * E + 4 * c + u + 1)
                pool.wait_ge(stacks_cleared, 4)
                pool.wait_ge(w_high, high)
                dst = W2[:, bass.ds(2 * c + u // 2, 1), (u % 2) * KF // 2:(u % 2 + 1) * KF // 2, :, :]
                nc.gpsimd.tensor_tensor(dst[:, 0, :, 1, :], staged[u % 2][:, :].rearrange("p (k n) -> p k n", n=D),
                                        dst[:, 0, :, 0, :], ALU.subtract).then_inc(w_low, 1)

            def low_rows(c):
                pool.wait_ge(x3_high, c + 1)
                nc.gpsimd.tensor_tensor(xs[:, :, D:], xn3[:, :, :], xs[:, :, 0:D], ALU.subtract).then_inc(x3_low, 1)

            def cross_step(c, o, has_last, has_next):
                if has_last:
                    inverse_deviation(LN0 + 2 * c, TC, XN0 + TC * (2 * c + 1))
                second_low(c, 0)
                pool.wait_ge(xc_normed, TC * c + TC)
                chunk = X[:, bass.ds(c * TC * D, TC * D)].rearrange("p (t d) -> p t d", t=TC)
                nc.gpsimd.tensor_tensor(chunk, chunk, bxc_sb[:, :].unsqueeze(1).to_broadcast([P, TC, D]),
                                        ALU.add).then_inc(xc_ready, 1)
                for m in range(KD):
                    pool.wait_ge(cum_moved, KD * c + m + 1)
                    nc.gpsimd.tensor_tensor(mix[:, m, :], k_exp[:, m, :], mix[:, m, :], ALU.mult).then_inc(ratio_ready, 1)
                second_low(c, 1)
                if has_next:
                    inverse_deviation(LN0 + 2 * c + 1, TC, XN0 + TC * (2 * c + 2))
                for m in range(KD):
                    pool.wait_ge(q_heads_ready, KD * c + m + 1)
                    nc.gpsimd.tensor_tensor(mix[:, m, :], q_exp[:, m, :], mix[:, m, :], ALU.mult).then_inc(mixed_ready, 1)
                second_low(c, 2)
                if has_last:
                    low_rows(c - 1)
                second_low(c, 3)

            cross_steps(pool, cross_step)
            inverse_deviation(LN0 + 2 * NC - 1, TC, XN0 + TC * 2 * NC)
            low_rows(NC - 1)

            pool.wait_ge(b2_loaded, 16)
            pool.wait_ge(rows_stored, 16 * NC)
            pool.wait_ge(x_stored, 16 * NC)
            pool.wait_ge(spare_stored, 32)
            pool.wait_ge(experts_ready, 1)
            pool.wait_ge(ids_ready, 3)

            def gather(i, o, copies):
                if not isinstance(i, int) or i >= 2:
                    pool.wait_ge(stacks_cleared, 4)
                    pool.wait_ge(xg_transposed, at(pool, i - 1))
                nc.gpsimd.tensor_copy(gather_ids[o][:, :], block_rows[:, bass.ds(i, 1)]).then_inc(ids_copied, 1)
                copied = at(pool, copies + 1)
                pool.wait_ge(stacks_cleared, 4)
                pool.wait_ge(ids_copied, copied)
                nc.gpsimd.indirect_dma_start(xg[o][:, :], None, rows, bass.IndirectOffsetOnAxis(ap=gather_ids[o][:, :], axis=0)
                                             ).then_inc(gathered[o], 16)

            def gate_b2(i, o):
                e = pool.value_load(block_expert[0:1, bass.ds(i, 1)], min_val=0, max_val=E - 1)
                if not isinstance(i, int) or i >= 2:
                    pool.wait_ge(stacks_cleared, 4)
                    pool.wait_ge(y_ready, at(pool, i - 1))
                nc.gpsimd.tensor_tensor(gated_b2[o][:, :].unsqueeze(1), b2_sb[:, bass.ds(e, 1), :],
                                        block_gates[:, bass.ds(i, 1)].unsqueeze(2).to_broadcast([P, 1, D]),
                                        ALU.mult).then_inc(gated_b2_ready, 1)

            def add(i, o, copies):
                nc.gpsimd.tensor_copy(add_ids[o][:, :], block_rows[:, bass.ds(i, 1)]).then_inc(ids_copied, 1)
                copied, have, before = at(pool, copies + 1), at(pool, i + 1), at(pool, 16 * i)
                pool.wait_ge(stacks_cleared, 4)
                pool.wait_ge(ids_copied, copied)
                pool.wait_ge(y_ready, have)
                pool.wait_ge(added, before)
                nc.gpsimd.indirect_dma_start(out, bass.IndirectOffsetOnAxis(ap=add_ids[o][:, :], axis=0), y[o][:, :], None,
                                             compute_op=ALU.add).then_inc(added, 16)

            def block_step(two, o, ahead):
                i = 2 * two + o
                if ahead >= 3:
                    gather(i + 3, 1 - o, 3 + 2 * i)
                if ahead >= 1:
                    gate_b2(i + 1, 1 - o)
                add(i, o, 2 * i + 4 if ahead >= 3 else i + NB)

            for i in range(3):
                gather(i, i % 2, i)
            gate_b2(0, 0)
            blocks_in_turn(pool, block_step)

        @block.scalar
        def _(act):
            act.wait_ge(x0_loaded, 32)
            nc.scalar.copy(id16[:, :], id_sb[:, :]).then_inc(id16_ready, 1)

            def move_xnT(b):
                act.wait_ge(s1_done, S1_USES * b + U_XNT + 1)
                nc.scalar.copy(xnT[:, :, :], s1_ps[:, :].rearrange("p (k s) -> p k s", k=KD)).then_inc(s1_moved, 1)

            def move_v(b, t):
                act.wait_ge(s1_done, S1_USES * b + U_V[t] + 1)
                if t == 0 and (not isinstance(b, int) or b >= 1):
                    act.wait_ge(v_ready, b)
                nc.scalar.copy(v_raw[:, t, :], s1_ps[:, 0:D]).then_inc(s1_moved, 1)

            def high_parts(b, o, t):
                act.wait_ge(roped_ready, T * b + t + 1)
                heads = roped[:, t, :].rearrange("p (w h d) -> p w h d", w=2, d=DH)
                for w, dst in ((0, q_stack[o][:, t, :, 0:32].rearrange("p h (r d) -> p h r d", d=DH)),
                               (1, k_stack[o][:, t, :, :].rearrange("p h (r d) -> p h r d", d=DH)[:, :, 0:4:3, :])):
                    nc.scalar.copy(dst, heads[:, w].unsqueeze(2).to_broadcast([P, H, 2, DH])).then_inc(hi_ready, 1)

            def move_kT(b, o, r):
                bank, _ = s2_slot(b, U_KT[r])
                act.wait_ge(s2_done, S2_USES * b + U_KT[r] + 1)
                src = s2_ps[bank][:, :].bitcast(F16).rearrange("p (a s) -> p a s", s=SEQ)
                dst = kT[o][:, 8 * r:8 * r + 8, :].rearrange("p (a two) s -> p a two s", two=2)
                nc.scalar.copy(dst[0:64, :, 0, :], src[0:64])
                nc.scalar.copy(dst[64:128, :, 1, :], src[64:128]).then_inc(s2_moved[bank], 1)

            def move_qmT(b, o):
                for r in range(2):
                    bank, _ = s2_slot(b, U_RT[r])
                    act.wait_ge(s2_done, S2_USES * b + U_RT[r] + 1)
                    src = s2_ps[bank][:, :].bitcast(F16).rearrange("p (a s) -> p a s", s=SEQ)
                    nc.scalar.copy(qmT[o][:, 4 * r:4 * r + 4, :], src).then_inc(s2_moved[bank], 1)

            def exponentials(b, g):
                act.wait_ge(scores_ready, GROUPS * b + g + 1)
                if g >= 2:
                    act.wait_ge(pv_done, GROUPS * b + g - 1)
                nc.scalar.activation(probs[g % 2][:, :, :], s_ps[g % 2][:, :, :], ACT.Exp,
                                     scale=SCALE).then_inc(exp_done, 1)

            def high_weights(u, place, loads, dst):
                act.wait_ge(w_loaded[place], 16 * loads)
                nc.scalar.activation(staged[place][:, :], staged[place][:, :], ACT.Copy, scale=WSCALE).then_inc(w_scaled, 1)
                scaled = at(act, u + 1)
                act.wait_ge(consts_set, 8)
                act.wait_ge(w_scaled, scaled)
                nc.scalar.copy(dst, staged[place][:, :].rearrange("p (k n) -> p k n", n=dst.shape[-1])).then_inc(w_high, 1)

            def first_layer(b, k):
                high_weights(2 * b + k, k, b + 1, W1[:, bass.ds(b, 1), k, 0, :])

            def step(j, o, stages):
                def s3(*groups):
                    if stages[2]:
                        for g in groups:
                            exponentials(j, g)

                if stages[1]:
                    move_kT(j + 1, 1 - o, 0)
                if stages[0]:
                    move_xnT(j + 2)
                s3(0, 1)
                if stages[0]:
                    move_v(j + 2, 0)
                s3(2)
                if stages[0]:
                    first_layer(j + 2, 0)
                s3(3)
                if stages[0]:
                    move_v(j + 2, 1)
                s3(4)
                if stages[0]:
                    high_parts(j + 2, o, 0)
                s3(5)
                if stages[0]:
                    high_parts(j + 2, o, 1)
                s3(6)
                if stages[0]:
                    first_layer(j + 2, 1)
                s3(7)
                if stages[1]:
                    move_qmT(j + 1, 1 - o)

            act.wait_ge(consts_set, 8)
            iterations(act, step)

            act.wait_ge(cross_loaded, CROSS_LOADS)

            def elu_parts(m, src, bias, exp):
                nc.scalar.activation(exp[:, m, :], src, ACT.Exp, bias=bias[:, m:m + 1])
                return nc.scalar.activation(relu[:, m, :], src, ACT.Relu, bias=bias[:, m:m + 1])

            def key_parts(c):
                for m in range(KD):
                    act.wait_ge(k_done, KD * c + m + 1)
                    if not isinstance(c, int) or c > 0:
                        act.wait_ge(q_heads_ready, KD * c)
                        act.wait_ge(ratio_ready, KD * c)
                    elu_parts(m, kv_ps[m], bxk_sb, k_exp).then_inc(k_moved, 1)

            def second_layer(c, u):
                high_weights(2 * E + 4 * c + u, u % 2, E + 2 * c + u // 2 + 1,
                             W2[:, bass.ds(2 * c + u // 2, 1), (u % 2) * KF // 2:(u % 2 + 1) * KF // 2, 0, :]
                             .rearrange("p e k n -> p (e k) n"))

            def high_rows(c):
                act.wait_ge(x3_normed, TC * c + TC)
                if not isinstance(c, int) or c > 0:
                    act.wait_ge(rows_stored, 16 * c)
                nc.scalar.copy(xs[:, :, 0:D], xn3[:, :, :]).then_inc(x3_high, 1)

            def move_x3T(c):
                for k in range(KD):
                    act.wait_ge(x3T_done, KD * c + k + 1)
                    nc.scalar.copy(xT[:, k, :], xT_ps[k]).then_inc(x3T_moved, 1)

            def cross_step(c, o, has_last, has_next):
                for k in range(KD):
                    act.wait_ge(xnT_done, KD * c + k + 1)
                    nc.scalar.copy(xT[:, k, :], xT_ps[k]).then_inc(xnT_moved, 1)
                second_layer(c, 0)
                if has_last:
                    high_rows(c - 1)
                for m in range(KD):
                    act.wait_ge(q_done, KD * c + m + 1)
                    act.wait_ge(k_heads_ready, KD * c + KD)
                    elu_parts(m, cq_ps[m], bxq_sb, q_exp).then_inc(q_moved, 1)
                second_layer(c, 1)
                if has_last:
                    move_x3T(c - 1)
                second_layer(c, 2)
                if has_next:
                    key_parts(c + 1)
                second_layer(c, 3)

            key_parts(0)
            cross_steps(act, cross_step)
            high_rows(NC - 1)
            move_x3T(NC - 1)

            act.wait_ge(gap_ready, 1)
            nc.scalar.activation(v_exp[:, :], v_gap[:, :], ACT.Exp).then_inc(gap_exp, 1)

            act.wait_ge(experts_ready, 1)

            def hidden(i, o):
                e = act.value_load(block_expert[0:1, bass.ds(i, 1)], min_val=0, max_val=E - 1)
                for m in range(KF):
                    have = at(act, 2 * i + m // (KF // 2) + 1)
                    split = at(act, 2 * i - 2)
                    act.wait_ge(consts_set, 8)
                    act.wait_ge(first_done, have)
                    if m == 0 and (not isinstance(i, int) or i >= 2):
                        act.wait_ge(lo_split, split)
                    nc.scalar.activation(hid[o][:, m, :], hid_ps[o][:, m, :], ACT.Gelu_apprx_tanh,
                                         bias=b1_sb[:, bass.ds(e * KF + m, 1)], scale=1 / WSCALE).then_inc(gelu_done, 1)

            def block_step(two, o, ahead):
                if ahead >= 1:
                    hidden(2 * two + o + 1, 1 - o)

            hidden(0, 0)
            blocks_in_turn(act, block_step)

        @block.vector
        def _(dve):
            def normalise(b):
                rows = seq_rows(b)
                for t in range(T):
                    nc.vector.bn_stats(stats[:, t, :], rows[:, t, :]).then_inc(ln_stats, 1)
                for t in range(T):
                    have = at(dve, T * b + t + 1)
                    dve.wait_ge(x0_loaded, 32)
                    dve.wait_ge(ln_stats, have)
                    nc.vector.bn_aggr(mv[:, t, :], stats[:, t, :]).then_inc(ln_mv, 1)
                dve.wait_ge(ln_rstd, b + 1)
                for t in range(T):
                    nc.vector.tensor_scalar(xn[:, t, :], rows[:, t, :], mv[:, t, 0:1], rstd[:, t:t + 1],
                                            ALU.subtract, ALU.mult).then_inc(xn_ready, 1)

            def add_bias(b, t):
                dve.wait_ge(s1_done, S1_USES * b + U_QK[t] + 1)
                nc.vector.tensor_tensor(qk[:, t, :], s1_ps[:, :], bqkv_sb[:, 0:2 * D], ALU.add).then_inc(s1_moved, 1)

            def rotate_swapped(b, t):
                dve.wait_ge(s1_moved, S1_USES * b + U_QK[t] + 1)
                src = qk[:, t, :].rearrange("p (h two e) -> p h two e", two=2, e=DH // 2)
                dst = rot_s[:, t, :].rearrange("p (h two e) -> p h two e", two=2, e=DH // 2)
                sn = sin_sb[:, t, :].rearrange("p (two e) -> p two e", two=2)
                for half in range(2):
                    last = nc.vector.tensor_tensor(
                        dst[:, :, half, :], src[:, :, 1 - half, :],
                        sn[:, half, :].unsqueeze(1).to_broadcast([P, 2 * H, DH // 2]), ALU.mult)
                last.then_inc(rot_s_ready, 1)

            def move_qT(b, r):
                bank, _ = s2_slot(b, U_QT[r])
                dve.wait_ge(s2_done, S2_USES * b + U_QT[r] + 1)
                src = s2_ps[bank][:, :].bitcast(F16).rearrange("p (a s) -> p a s", s=SEQ)
                nc.vector.tensor_copy(qT[:, 4 * r:4 * r + 4, :], src).then_inc(s2_moved[bank], 1)

            def move_kT(b, o, r):
                bank, _ = s2_slot(b, U_KT[r])
                dve.wait_ge(s2_done, S2_USES * b + U_KT[r] + 1)
                src = s2_ps[bank][:, :].bitcast(F16).rearrange("p (a s) -> p a s", s=SEQ)
                dst = kT[o][:, 8 * r:8 * r + 8, :].rearrange("p (a two) s -> p a two s", two=2)
                nc.vector.tensor_copy(dst[0:64, :, 0, :], src[0:64])
                nc.vector.tensor_copy(dst[64:128, :, 1, :], src[64:128]).then_inc(s2_moved[bank], 1)

            def maxima(b, first, count):
                for g in range(first, first + count):
                    t, pair = divmod(g, PAIRS)
                    bank, _ = s2_slot(b, U_SC + g)
                    dve.wait_ge(s2_done, S2_USES * b + U_SC + g + 1)
                    nc.vector.reduce_max(mx[:, t, 2 * pair:2 * pair + 2],
                                         s2_ps[bank][:, :].rearrange("p (h s) -> p h s", h=2), AX.X).then_inc(s2_moved[bank], 1)

            def divide(b, half):
                dve.wait_ge(pv_done, GROUPS * b + 4 * half + 4)
                if half > 0:
                    dve.wait_ge(oT_ready, 2 * b + half)
                nc.vector.transpose(o_rows[:, :, :].rearrange("p c r -> p (c r)"), o_ps[:, :]).then_inc(o_moved, 1)
                dve.wait_ge(o_moved, 1 + O_USES * b + half + 1)
                nc.vector.reciprocal(rsums[:, :], o_rows[:, :, DH]).then_inc(rsums_ready, 1)
                dve.wait_ge(rsums_ready, 2 * b + half + 1)
                nc.vector.tensor_tensor(o_rows[:, :, 0:DH], o_rows[:, :, 0:DH],
                                        rsums[:, :].unsqueeze(2).to_broadcast([P, 2 * SEQ // 32, DH]),
                                        ALU.mult).then_inc(o_scaled, 1)
                dve.wait_ge(o_scaled, 2 * b + half + 1)
                nc.vector.transpose(oT[:, 2 * half:2 * half + 2, :].rearrange("p q s -> p (q s)"),
                                    o_rows[:, :, :].rearrange("p c r -> p (c r)")).then_inc(oT_ready, 1)

            def residual(b):
                dve.wait_ge(wo_done, b + 1)
                dve.wait_ge(xb_ready, b + 1)
                rows = seq_rows(b)
                nc.vector.tensor_tensor(rows, o_ps[:, :].rearrange("p (t d) -> p t d", t=T), rows,
                                        ALU.add).then_inc(o_moved, 1)

            def step(j, o, stages):
                def s2_max(first, count):
                    if stages[1]:
                        maxima(j + 1, first, count)

                if stages[1]:
                    move_qT(j + 1, 0)
                    move_qT(j + 1, 1)
                    move_kT(j + 1, 1 - o, 1)
                if stages[0]:
                    add_bias(j + 2, 0)
                s2_max(0, 2)
                if stages[0]:
                    rotate_swapped(j + 2, 0)
                s2_max(2, 2)
                if stages[0]:
                    add_bias(j + 2, 1)
                s2_max(4, 2)
                if stages[0]:
                    rotate_swapped(j + 2, 1)
                s2_max(6, 2)
                if stages[2]:
                    divide(j, 0)
                s2_max(8, 4)
                if stages[0]:
                    normalise(j + 3)
                s2_max(12, 4)
                if stages[2]:
                    divide(j, 1)
                    residual(j)

            dve.sem_inc(o_moved, 1)
            dve.wait_ge(x0_loaded, 32)
            normalise(0)
            dve.wait_ge(wqkv_loaded, 64)
            dve.wait_ge(x_loaded, 16)
            dve.wait_ge(consts_set, 8)
            iterations(dve, step)

            dve.wait_ge(cross_loaded, CROSS_LOADS)
            dve.wait_ge(o_moved, 1 + O_USES * BATCH)

            def normalise_chunk(c, n, dst, normed):
                chunk = X[:, bass.ds(c * TC * D, TC * D)].rearrange("p (t d) -> p t d", t=TC)
                for t in range(TC):
                    nc.vector.bn_stats(stats[:, t, :], chunk[:, t, :]).then_inc(ln_stats, 1)
                for t in range(TC):
                    have = at(dve, XN0 + TC * n + t + 1)
                    dve.wait_ge(x0_loaded, 32)
                    dve.wait_ge(ln_stats, have)
                    nc.vector.bn_aggr(mv[:, t, :], stats[:, t, :]).then_inc(ln_mv, 1)
                dve.wait_ge(ln_rstd, BATCH + 1 + n + 1)
                for t in range(TC):
                    nc.vector.tensor_scalar(dst[:, t, :], chunk[:, t, :], mv[:, t, 0:1], rstd[:, t:t + 1],
                                            ALU.subtract, ALU.mult).then_inc(normed, 1)

            def choose(c):
                dve.wait_ge(logits_done, c + 1)
                nc.vector.tensor_tensor(lg[:, :, :], wc_ps[0][:, 0:TC * E].rearrange("p (t e) -> p t e", e=E),
                                        br_sb[:, :].unsqueeze(1).to_broadcast([P, TC, E]), ALU.add).then_inc(logits_moved, 1)
                dve.wait_ge(logits_moved, c + 1)
                for t in range(TC):
                    nc.vector.max(best_v[:, t, :], lg[:, t, :]).then_inc(best_found, 1)
                for t in range(TC):
                    have = at(dve, 2 * TC * c + t + 1)
                    dve.wait_ge(x0_loaded, 32)
                    dve.wait_ge(best_found, have)
                    nc.vector.max_index(best_e[:, t, :], best_v[:, t, :], lg[:, t, :]).then_inc(best_found, 1)
                have = at(dve, 2 * TC * c + 2 * TC)
                dve.wait_ge(x0_loaded, 32)
                dve.wait_ge(best_found, have)
                nc.vector.tensor_copy(top_v[:, :, bass.ds(c * TC, TC)],
                                      best_v[:, :, 0:TOP].rearrange("p t k -> p k t")).then_inc(best_kept, 1)
                nc.vector.tensor_copy(top_e[:, :, bass.ds(c * TC, TC)],
                                      best_e[:, :, 0:TOP].rearrange("p t k -> p k t")).then_inc(best_kept, 1)

            def cross_step(c, o, has_last, has_next):
                for m in range(KD):
                    dve.wait_ge(k_moved, KD * c + m + 1)
                    nc.vector.scalar_tensor_tensor(k_exp[:, m, :], k_exp[:, m, :], 1.0, relu[:, m, :],
                                                   ALU.min, ALU.add).then_inc(k_heads_ready, 1)
                if has_last:
                    summed = at(dve, 2 * c)
                    dve.wait_ge(x0_loaded, 32)
                    dve.wait_ge(wc_moved, summed)
                    normalise_chunk(c - 1, 2 * c, xn3, x3_normed)
                for m in range(KD):
                    dve.wait_ge(cum_done, KD * c + m + 1)
                    nc.vector.reciprocal(mix[:, m, :], cq_ps[m]).then_inc(cum_moved, 1)
                for m in range(KD):
                    dve.wait_ge(v_done, KD * c + m + 1)
                    dve.wait_ge(ratio_ready, KD * c + m + 1)
                    nc.vector.scalar_tensor_tensor(mix[:, m, :], kv_ps[m], bxv_sb[:, m:m + 1], mix[:, m, :],
                                                   ALU.add, ALU.mult).then_inc(v_moved, 1)
                for m in range(KD):
                    dve.wait_ge(q_moved, KD * c + m + 1)
                    nc.vector.scalar_tensor_tensor(q_exp[:, m, :], q_exp[:, m, :], 1.0, relu[:, m, :],
                                                   ALU.min, ALU.add).then_inc(q_heads_ready, 1)
                if has_next:
                    normalise_chunk(c + 1, 2 * c + 1, xn, xc_normed)
                if has_last:
                    choose(c - 1)
                dve.wait_ge(xc_ready, c + 1)
                chunk = X[:, bass.ds(c * TC * D, TC * D)].rearrange("p (t d) -> p t d", t=TC)
                for half in range(2):
                    dve.wait_ge(wc_done, 2 * c + half + 1)
                    part = chunk[:, 2 * half:2 * half + 2, :]
                    nc.vector.tensor_tensor(part, wc_ps[half].rearrange("p (t d) -> p t d", t=2), part,
                                            ALU.add).then_inc(wc_moved, 1)

            normalise_chunk(0, 0, xn, xc_normed)
            cross_steps(dve, cross_step)
            dve.wait_ge(wc_moved, 2 * NC)
            normalise_chunk(NC - 1, 2 * NC - 1, xn3, x3_normed)
            choose(NC - 1)

            dve.wait_ge(route_loaded, 32)
            dve.wait_ge(best_kept, 2 * NC)
            by_choice = [P, TOP, NT, E]
            nc.vector.tensor_tensor(v_gap[:, :], top_v[:, 1, :], top_v[:, 0, :], ALU.subtract).then_inc(gap_ready, 1)
            nc.vector.memset(oh_any[:, NT, :], 0.0).then_inc(choices_ready, 1)
            nc.vector.tensor_tensor(oh[:, :, :, :], top_e[:, :, :].unsqueeze(3).to_broadcast(by_choice),
                                    const("experts").unsqueeze(1).unsqueeze(1).to_broadcast(by_choice),
                                    ALU.is_equal).then_inc(routed, 1)
            dve.wait_ge(routed, 1)
            nc.vector.tensor_tensor(oh_any[:, 0:NT, :], oh[:, 0], oh[:, 1], ALU.add).then_inc(choices_ready, 1)
            dve.wait_ge(gap_exp, 1)
            nc.vector.tensor_scalar(v_sum[:, :], v_exp[:, :], 1.0, None, ALU.add).then_inc(routed, 1)
            dve.wait_ge(routed, 2)
            nc.vector.reciprocal(gates[:, 0, :], v_sum[:, :]).then_inc(routed, 1)
            dve.wait_ge(routed, 3)
            nc.vector.tensor_tensor(gates[:, 1, :], v_exp[:, :], gates[:, 0, :], ALU.mult).then_inc(routed, 1)
            dve.wait_ge(ranks_done, 1)
            floors = [P, E, TOKENS // P]
            nc.vector.tensor_tensor(above[:, :, :], rank_ps[:, NT, :].unsqueeze(2).to_broadcast(floors),
                                    const("block_floors").unsqueeze(1).to_broadcast(floors), ALU.is_gt).then_inc(routed, 1)
            dve.wait_ge(routed, 5)
            nc.vector.reduce_sum(expert_blocks[:, :], above[:, :, :], AX.X).then_inc(routed, 1)
            dve.wait_ge(routed, 6)
            nc.vector.tensor_tensor(bounds_of[:, :, :], const("before").rearrange("p (w e) -> p w e", e=E),
                                    expert_blocks[:, :].unsqueeze(1).to_broadcast([P, 2 * E, E]), ALU.mult).then_inc(routed, 1)
            dve.wait_ge(routed, 7)
            nc.vector.reduce_sum(bounds[:, :], bounds_of[:, :, :], AX.X).then_inc(routed, 1)
            dve.wait_ge(routed, 8)
            nc.vector.scalar_tensor_tensor(place_of[:, :, :], bounds[:, 0:E].unsqueeze(1).to_broadcast([P, NT, E]), float(P),
                                           rank_ps[:, 0:NT, :], ALU.mult, ALU.add).then_inc(routed, 1)
            dve.wait_ge(routed, 9)
            nc.vector.tensor_tensor(oh_place[:, :, :, :], oh[:, :, :, :], place_of[:, :, :].unsqueeze(1).to_broadcast(by_choice),
                                    ALU.mult).then_inc(routed, 1)
            dve.wait_ge(routed, 10)
            nc.vector.reduce_sum(place[:, :], oh_place[:, :, :, :].rearrange("p k t e -> p (k t) e"), AX.X).then_inc(routed, 1)
            dve.wait_ge(routed, 11)
            nc.vector.tensor_copy(place_i[:, :], place[:, :]).then_inc(routed, 1)
            dve.wait_ge(routed, 12)
            nc.vector.tensor_scalar(block_i[:, :], place_i[:, :], P.bit_length() - 1, None,
                                    ALU.logical_shift_right).then_inc(routed, 1)
            dve.wait_ge(routed, 13)
            nc.vector.tensor_copy(block_f[:, :], block_i[:, :]).then_inc(routed, 1)
            dve.wait_ge(routed, 14)
            nc.vector.scalar_tensor_tensor(pos[:, :], block_f[:, :], float(-P), place[:, :], ALU.mult, ALU.add).then_inc(routed, 1)
            by_block = [P, TOP * NT, NB]
            dve.wait_ge(x3_low, NC)
            dve.wait_ge(rows_stored, 16 * NC)
            nc.vector.tensor_tensor(table[:, :, 0, :], const("blocks").unsqueeze(1).to_broadcast(by_block),
                                    block_f[:, :].unsqueeze(2).to_broadcast(by_block), ALU.is_equal).then_inc(routed, 1)
            dve.wait_ge(w_low, 4 * E)
            dve.wait_ge(routed, 16)

            def position_rows(q):
                j = slice(q * 8, q * 8 + 8)
                if q >= 2:
                    dve.wait_ge(pos_used, q - 1)
                nc.vector.tensor_tensor(pos_oh[q % 2], const("positions").unsqueeze(1).to_broadcast([P, 8, P]),
                                        pos[:, j].unsqueeze(2).to_broadcast([P, 8, P]), ALU.is_equal).then_inc(pos_ready, 1)

            position_rows(0)
            nc.vector.tensor_tensor(table[:, :, 1, :], table[:, :, 0, :],
                                    gates[:, :, :].rearrange("p k t -> p (k t)").unsqueeze(2).to_broadcast(by_block),
                                    ALU.mult).then_inc(routed, 1)
            dve.wait_ge(routed, 17)
            for k in range(TOP):
                tiles = table[:, k * NT:(k + 1) * NT, 0, :]
                nc.vector.tensor_tensor(tiles, tiles, const("tokens").unsqueeze(2).to_broadcast([P, NT, NB]),
                                        ALU.mult).then_inc(table_ready, 1)
            for q in range(1, TOP * NT // 8):
                position_rows(q)
            by_expert = [P, NB, E]
            nc.vector.tensor_tensor(reached[:, :, :], const("blocks").unsqueeze(2).to_broadcast(by_expert),
                                    bounds[:, E:].unsqueeze(1).to_broadcast(by_expert), ALU.is_ge).then_inc(routed, 1)
            dve.wait_ge(routed, 18)
            nc.vector.reduce_sum(owner[:, :], reached[:, :, :], AX.X).then_inc(routed, 1)
            dve.wait_ge(routed, 19)
            nc.vector.tensor_scalar(block_expert[:, :], owner[:, :], float(E - 1), None, ALU.min).then_inc(experts_ready, 1)
            dve.wait_ge(table_done, 1)
            nc.vector.tensor_scalar(spare_ids[:, :], table_ps[:, 0:NB], 0.0, const("spare_row"), ALU.is_ge,
                                    ALU.mult).then_inc(routed, 1)
            dve.wait_ge(routed, 20)
            nc.vector.scalar_tensor_tensor(block_rows[:, :], table_ps[:, 0:NB], float(2 * TOKENS), spare_ids[:, :],
                                           ALU.add, ALU.add).then_inc(ids_ready, 1)
            nc.vector.tensor_copy(block_gates[:, :], table_ps[:, NB:]).then_inc(ids_ready, 1)
            nc.vector.tensor_scalar(block_scales[:, :], table_ps[:, NB:], 1 / WSCALE, None, ALU.mult).then_inc(ids_ready, 1)

            dve.wait_ge(ids_ready, 3)

            def move_xgT(i, o):
                dve.wait_ge(xg_transposed, i + 1)
                nc.vector.tensor_copy(xgT[o][:, :, :, :], xgT_ps[o]).then_inc(xgT_moved, 1)

            def split_hidden(i, o, half):
                m = slice(half * KF // 2, (half + 1) * KF // 2)
                dve.wait_ge(gelu_done, KF * i + m.stop)
                nc.vector.tensor_copy(hid_hi[o][:, m, :], hid[o][:, m, :]).then_inc(hi_split, 1)
                dve.wait_ge(hi_split, 2 * i + half + 1)
                nc.vector.tensor_tensor(hid_lo[o][:, m, :], hid[o][:, m, :], hid_hi[o][:, m, :],
                                        ALU.subtract).then_inc(lo_split, 1)

            def gated_output(i, o):
                have, before = at(dve, i + 1), at(dve, 16 * i - 16)
                dve.wait_ge(x0_loaded, 32)
                dve.wait_ge(second_done, have)
                dve.wait_ge(gated_b2_ready, have)
                if not isinstance(i, int) or i >= 2:
                    dve.wait_ge(added, before)
                nc.vector.scalar_tensor_tensor(y[o][:, :], y_ps[o], block_scales[:, bass.ds(i, 1)], gated_b2[o][:, :],
                                               ALU.mult, ALU.add).then_inc(y_ready, 1)

            def block_step(two, o, ahead):
                i = 2 * two + o
                if ahead >= 1:
                    split_hidden(i + 1, 1 - o, 0)
                if ahead >= 2:
                    move_xgT(i + 2, o)
                if ahead >= 1:
                    split_hidden(i + 1, 1 - o, 1)
                gated_output(i, o)

            move_xgT(0, 0)
            move_xgT(1, 1)
            split_hidden(0, 0, 0)
            split_hidden(0, 0, 1)
            blocks_in_turn(dve, block_step)

        @block.tensor
        def _(pe):
            def s1_free(b, u):
                pe.wait_ge(s1_moved, S1_USES * b + u)

            def s2_free(b, u):
                bank, n = s2_slot(b, u)
                pe.wait_ge(s2_moved[bank], n)
                return bank

            def s2_arrived(b, u):
                bank, n = s2_slot(b, u)
                pe.wait_ge(s2_moved[bank], n + 1)

            def transpose_xn(b):
                pe.wait_ge(xn_ready, T * b + T)
                s1_free(b, U_XNT)
                for k in range(KD):
                    for t in range(T):
                        last = nc.tensor.transpose(s1_ps[:, k * SEQ + t * P:k * SEQ + (t + 1) * P],
                                                   xn[:, t, k * P:(k + 1) * P], id_sb[:, :])
                last.then_inc(s1_done, 1)

            def project(b, u, t, lo, n):
                s1_free(b, u)
                for k in range(KD):
                    last = nc.tensor.matmul(s1_ps[:, 0:n], xnT[:, k, t * P:(t + 1) * P],
                                            wqkv_sb[:, k, lo:lo + n], start=(k == 0), stop=(k == KD - 1))
                last.then_inc(s1_done, 1)

            def transpose_stack(b, stack, u, r):
                bank = s2_free(b, u)
                dst = s2_ps[bank][:, :].bitcast(F16).rearrange("p (a s) -> p a s", s=SEQ)
                for a in range(4):
                    for t in range(T):
                        pair = 4 * r + a
                        last = nc.tensor.transpose(
                            dst[:, a, t * P:(t + 1) * P],
                            stack[:, t, 2 * pair:2 * pair + 2, :].rearrange("p h r -> p (h r)"), id16[:, :])
                last.then_inc(s2_done, 1)

            def row_scores(b, o, first, count):
                if first == 0:
                    for u in (*U_QT, *U_KT):
                        s2_arrived(b, u)
                for g in range(first, first + count):
                    t, pair = divmod(g, PAIRS)
                    bank = s2_free(b, U_SC + g)
                    for h in range(2):
                        last = nc.tensor.matmul(s2_ps[bank][:, h * SEQ:(h + 1) * SEQ], qT[:, pair, t * P:(t + 1) * P],
                                                kT[o][:, 2 * pair + h, :], start=True, stop=True)
                    last.then_inc(s2_done, 1)

            def key_scores(b, o, g):
                quad, kt = divmod(g, T)
                if g == 0:
                    for u in U_RT:
                        s2_arrived(b, u)
                if g >= 2:
                    pe.wait_ge(exp_done, GROUPS * b + g - 1)
                for n in range(4):
                    h = 4 * quad + n
                    last = nc.tensor.matmul(s_ps[g % 2][:, n, :], kT[o][:, h, kt * P:(kt + 1) * P],
                                            qmT[o][:, h // 2, :], start=True, stop=True)
                last.then_inc(scores_ready, 1)

            def weigh_values(b, o, g):
                quad, kt = divmod(g, T)
                col = (quad % 2) * SEQ
                if g == 0:
                    pe.wait_ge(v_ready, b + 1)
                if g % 4 == 0:
                    pe.wait_ge(o_moved, 1 + O_USES * b + quad // 2)
                pe.wait_ge(exp_done, GROUPS * b + g + 1)
                for n in range(4):
                    last = nc.tensor.matmul(o_ps[32 * n:32 * n + 32, col:col + SEQ], v1[o][:, kt, 4 * quad + n, :],
                                            probs[g % 2][:, n, :], start=(kt == 0), stop=(kt == T - 1))
                last.then_inc(pv_done, 1)

            def project_out(b):
                pe.wait_ge(oT_ready, 2 * b + 2)
                pe.wait_ge(o_moved, 1 + O_USES * b + U_WO)
                for t in range(T):
                    for quad in range(QUADS):
                        last = nc.tensor.matmul(o_ps[:, t * D:(t + 1) * D], oT[:, quad, t * P:(t + 1) * P],
                                                wo_sb[:, quad, :], start=(quad == 0), stop=(quad == QUADS - 1))
                last.then_inc(wo_done, 1)

            def step(j, o, stages):
                s1, s2, s3 = stages
                qs, ks = q_stack[1 - o], k_stack[1 - o]

                def s3_scores(*groups):
                    for g in groups if s3 else ():
                        key_scores(j, o, g)

                def s3_values(*groups):
                    for g in groups if s3 else ():
                        weigh_values(j, o, g)

                def s2_scores(first, count):
                    if s2:
                        row_scores(j + 1, 1 - o, first, count)

                if s2:
                    pe.wait_ge(lo_ready, 3 * T * (j + 1) + 3 * T)
                    for r in range(2):
                        transpose_stack(j + 1, qs, U_QT[r], r)
                    for r in range(2):
                        transpose_stack(j + 1, ks, U_KT[r], r)
                if s1:
                    transpose_xn(j + 2)
                s3_scores(0, 1)
                if s1:
                    project(j + 2, U_QK[0], 0, 0, 2 * D)
                s3_values(0)
                s3_scores(2)
                if s1:
                    project(j + 2, U_V[0], 0, 2 * D, D)
                s2_scores(0, 2)
                s3_values(1)
                s3_scores(3)
                if s1:
                    project(j + 2, U_QK[1], 1, 0, 2 * D)
                s2_scores(2, 2)
                s3_values(2)
                s3_scores(4)
                if s1:
                    project(j + 2, U_V[1], 1, 2 * D, D)
                s2_scores(4, 2)
                s3_values(3)
                s3_scores(5)
                s2_scores(6, 3)
                s3_values(4)
                s3_scores(6)
                s2_scores(9, 3)
                s3_values(5)
                s3_scores(7)
                s2_scores(12, 2)
                s3_values(6)
                s2_scores(14, 2)
                s3_values(7)
                if s2:
                    pe.wait_ge(negm_ready, T * (j + 1) + T)
                    for r in range(2):
                        transpose_stack(j + 1, qs, U_RT[r], r)
                if s3:
                    project_out(j)

            pe.wait_ge(x0_loaded, 32)
            pe.wait_ge(consts_set, 8)
            pe.wait_ge(id16_ready, 1)
            pe.wait_ge(wqkv_loaded, 64)
            pe.wait_ge(wo_loaded, 32)
            iterations(pe, step)

            pe.wait_ge(cross_loaded, CROSS_LOADS)
            pe.wait_ge(o_moved, 1 + O_USES * BATCH)
            pe.wait_ge(exp_done, GROUPS * BATCH)
            for bank in range(2):
                pe.wait_ge(s2_moved[bank], S2_USES // 2 * BATCH)

            def transpose_rows(src, dst, done):
                for k in range(KD):
                    for t in range(TC):
                        last = nc.tensor.transpose(dst[k][:, t * P:(t + 1) * P], src[:, t, k * P:(k + 1) * P], id_sb[:, :])
                    last.then_inc(done, 1)

            def project_features(dst, m, w, rhs):
                for k in range(KD):
                    last = nc.tensor.matmul(dst, w[:, k, m * P:(m + 1) * P], rhs[:, k, :], start=(k == 0), stop=(k == KD - 1))
                return last

            def project_keys(c, o):
                pe.wait_ge(ctx_loaded, 16 * c + 16)
                for m in range(KD):
                    if not isinstance(c, int) or c > 0:
                        pe.wait_ge(v_moved, KD * c - KD + m + 1)
                    project_features(kv_ps[m], m, wxk_sb, ctx_sb[o]).then_inc(k_done, 1)

            def route(c):
                pe.wait_ge(x3_normed, TC * c + TC)
                transpose_rows(xn3, xT_ps, x3T_done)
                pe.wait_ge(x3T_moved, KD * c + KD)
                pe.wait_ge(wc_moved, 2 * c + 2)
                for t in range(TC):
                    for k in range(KD):
                        last = nc.tensor.matmul(wc_ps[0][:, t * E:(t + 1) * E], xT[:, k, t * P:(t + 1) * P],
                                                wr_sb[:, k, :], start=(k == 0), stop=(k == KD - 1))
                last.then_inc(logits_done, 1)

            def cross_step(c, o, has_last, has_next):
                pe.wait_ge(xc_normed, TC * c + TC)
                transpose_rows(xn, xT_ps, xnT_done)
                for m in range(KD):
                    pe.wait_ge(k_heads_ready, KD * c + m + 1)
                    if has_last:
                        pe.wait_ge(q_moved, KD * c - KD + m + 1)
                    for k in range(m + 1):
                        last = nc.tensor.matmul(cq_ps[m], cum_sb[:, k, m * P:(m + 1) * P], k_exp[:, k, :],
                                                start=(k == 0), stop=(k == m))
                    last.then_inc(cum_done, 1)
                for m in range(KD):
                    pe.wait_ge(k_moved, KD * c + m + 1)
                    project_features(kv_ps[m], m, wxv_sb, ctx_sb[o]).then_inc(v_done, 1)
                pe.wait_ge(xnT_moved, KD * c + KD)
                for m in range(KD):
                    pe.wait_ge(cum_moved, KD * c + m + 1)
                    project_features(cq_ps[m], m, wxq_sb, xT).then_inc(q_done, 1)
                if has_last:
                    route(c - 1)
                if has_next:
                    project_keys(c + 1, 1 - o)
                pe.wait_ge(mixed_ready, KD * c + KD)
                for half in range(2):
                    if has_last:
                        pe.wait_ge(logits_moved, c)
                        pe.wait_ge(wc_moved, 2 * c)
                    for t in range(2 * half, 2 * half + 2):
                        for k in range(KD):
                            last = nc.tensor.matmul(wc_ps[half][:, (t % 2) * D:(t % 2 + 1) * D], mix[:, k, t * P:(t + 1) * P],
                                                    wxc_sb[:, k, :], start=(k == 0), stop=(k == KD - 1))
                    last.then_inc(wc_done, 1)

            project_keys(0, 0)
            cross_steps(pe, cross_step)
            route(NC - 1)

            pe.wait_ge(route_loaded, 32)
            pe.wait_ge(choices_ready, 2)
            any_flat = oh_any[:, :, :].rearrange("p t e -> p (t e)")
            rank_flat = s2_ps[0][:, 0:(NT + 1) * E]
            nc.tensor.matmul(rank_flat, rank_sb[:, 0:P], any_flat, start=True, stop=False)
            for t in range(1, NT + 1):
                last = nc.tensor.matmul(rank_flat[:, t * E:], rank_sb[:, P:], any_flat[:, 0:(NT + 1 - t) * E],
                                        start=False, stop=(t == NT))
            last.then_inc(ranks_done, 1)
            pe.wait_ge(routed, 17)
            pe.wait_ge(table_ready, TOP)
            for j in range(TOP * NT):
                if j % 8 == 0:
                    pe.wait_ge(pos_ready, j // 8 + 1)
                last = nc.tensor.matmul(table_ps, pos_oh[j // 8 % 2][:, j % 8, :], table[:, j, :, :].rearrange("p w b -> p (w b)"),
                                        start=(j == 0), stop=(j == TOP * NT - 1))
                if j % 8 == 7 and j < TOP * NT - 1:
                    last.then_inc(pos_used, 1)
            last.then_inc(table_done, 1)

            pe.wait_ge(w_low, 4 * E)
            pe.wait_ge(experts_ready, 1)
            PASSES = ((0, 0), (0, 1), (1, 0))

            def transpose_block(two, o):
                i = 2 * two + o
                pe.wait_ge(gathered[o], 16 * two + 16)
                if not isinstance(i, int) or i >= 2:
                    pe.wait_ge(xgT_moved, i - 1)
                elif i == 0:
                    pe.wait_ge(ids_ready, 3)
                for h in range(2):
                    for k in range(KD):
                        last = nc.tensor.transpose(xgT_ps[o][:, h, k, :], xg[o][:, (h * KD + k) * P:(h * KD + k + 1) * P], id16[:, :])
                last.then_inc(xg_transposed, 1)

            def first_layer(i, o):
                e = pe.value_load(block_expert[0:1, bass.ds(i, 1)], min_val=0, max_val=E - 1)
                w = W1[:, bass.ds(e, 1), :, :, :]
                pe.wait_ge(xgT_moved, i + 1)
                if not isinstance(i, int) or i >= 2:
                    pe.wait_ge(gelu_done, KF * (i - 1))
                for m in range(KF):
                    for n, (wp, xp) in enumerate(PASSES):
                        for k in range(KD):
                            last = nc.tensor.matmul(hid_ps[o][:, m, :], w[:, 0, k, wp, m * P:(m + 1) * P], xgT[o][:, xp, k, :],
                                                    start=(n + k == 0), stop=(n == 2 and k == KD - 1))
                    if m % (KF // 2) == KF // 2 - 1:
                        last.then_inc(first_done, 1)

            def second_layer(i, o):
                e = pe.value_load(block_expert[0:1, bass.ds(i, 1)], min_val=0, max_val=E - 1)
                w = W2[:, bass.ds(e, 1), :, :, :]
                if not isinstance(i, int) or i >= 2:
                    pe.wait_ge(y_ready, i - 1)
                for k in range(KF):
                    if k % (KF // 2) == 0:
                        pe.wait_ge(lo_split, 2 * i + k // (KF // 2) + 1)
                    for n, (wp, hp) in enumerate(PASSES):
                        last = nc.tensor.matmul(y_ps[o], (hid_hi, hid_lo)[hp][o][:, k, :], w[:, 0, k, wp, :],
                                                start=(k + n == 0), stop=(n == 2 and k == KF - 1))
                last.then_inc(second_done, 1)

            def block_step(two, o, ahead):
                i = 2 * two + o
                if ahead >= 1:
                    first_layer(i + 1, 1 - o)
                if ahead >= 2:
                    transpose_block(two + 1, o)
                second_layer(i, o)

            transpose_block(0, 0)
            transpose_block(0, 1)
            first_layer(0, 0)
            blocks_in_turn(pe, block_step)


def head_halves():
    return np.concatenate([h * DH + np.concatenate([np.arange(0, DH, 2), np.arange(1, DH, 2)]) for h in range(H)])


def quad_rows(w):
    padded = np.zeros((H, 32, w.shape[1]), w.dtype)
    padded[:, :DH] = w.reshape(H, DH, -1)
    return padded.reshape(H * 32, -1)


def kernel(**inputs):
    import concourse.bacc as bacc
    from concourse.bass_utils import run_bass_kernel_spmd

    a = {k: np.asarray(v) for k, v in inputs.items()}
    halves = head_halves()
    cos, sin = rope_tables()
    laid = {
        "x": a["x"].reshape(BATCH * SEQ, D),
        "ctxT": a["ctx_1024"].reshape(BATCH * SEQ, D).T,
        "w_qkv": np.concatenate([a["L0_attn_Wq"].T[:, halves], a["L0_attn_Wk"].T[:, halves], a["L0_attn_Wv"].T], 1),
        "b_qkv": np.concatenate([a["L0_attn_bq"][halves], a["L0_attn_bk"][halves], a["L0_attn_bv"]]),
        "w_o": quad_rows(a["L0_attn_Wo"].T),
        "b_o": a["L0_attn_bo"],
        "wx_q": a["L0_xattn_wq_w"], "wx_k": a["L0_xattn_wk_w"], "wx_v": a["L0_xattn_wv_w"], "wx_c": a["L0_xattn_wc_w"],
        "bx_q": a["L0_xattn_wq_b"], "bx_k": a["L0_xattn_wk_b"], "bx_v": a["L0_xattn_wv_b"], "bx_c": a["L0_xattn_wc_b"],
        "wr": a["L0_ffn_Wr"], "br": a["L0_ffn_br"], "w1": a["L0_ffn_W1"], "b1": a["L0_ffn_b1"].reshape(-1),
        "w2": a["L0_ffn_W2"], "b2": a["L0_ffn_b2"],
        "rank_m": rank_matrices(), "route_c": np.concatenate(list(routing_constants().values()), 1),
        "cos": cos, "sin": sin, "cumsum_m": head_cumsum_matrix(), "ident": np.eye(P, dtype=np.float32),
    }
    nc = bacc.Bacc("TRN2", target_bir_lowering=False, num_devices=1)
    arrays, args = {}, {}
    for name, value in laid.items():
        value = np.ascontiguousarray(value)
        arrays[f"in_{name}"] = value
        args[name] = nc.dram_tensor(f"in_{name}", value.shape, mybir.dt.from_np(value.dtype), kind="ExternalInput").ap()
    rows = nc.dram_tensor("rows", (ROWS, 2 * D), F16, kind="Internal").ap()
    out = nc.dram_tensor("out_0", (ROWS, D), F32, kind="ExternalOutput").ap()
    build(nc, rows=rows, out=out, **args)
    got = run_bass_kernel_spmd(nc, [arrays], core_ids=[0]).results[0]["out_0"]
    return got[:TOKENS].reshape(BATCH, SEQ, D)
```

```python
from contextlib import ExitStack

import numpy as np

import concourse.bass as bass
from concourse import mybir

F32 = mybir.dt.float32
F16 = mybir.dt.float16
I32 = mybir.dt.int32
U32 = mybir.dt.uint32
ALU = mybir.AluOpType
ACT = mybir.ActivationFunctionType
AX = mybir.AxisListType

P = 128
BATCH, SEQ, D = 8, 256, 256
H, DH = 16, 16
KD = D // P
T = SEQ // P
NT = BATCH * T
PAIRS = H // 2
QUADS = H // 4
STACK = 64
E, TOP, DFF = 8, 2, 1024
KF = DFF // P
WSCALE = 256.0
TOKENS = BATCH * SEQ
NB = (TOKENS * TOP) // P + E - 1
ROWS = TOKENS + P
EPS = 1e-5
SCALE = float(DH) ** -0.5
THETA = 10000.0

ROW_MAX = 32

U_XNT, U_QK, U_V, S1_USES = 0, (1, 2), (3, 4), 5
U_QT, U_KT, U_RT, S2_USES = (0, 1), (2, 3), (18, 21), 22
U_SC = [u for u in range(4, S2_USES) if u not in U_RT]
U_WO, O_USES = 2, 3
GROUPS = QUADS * T


def rope_tables():
    freqs = np.arange(DH // 2, dtype=np.float32) * np.float32(1.0 / THETA)
    angles = np.arange(SEQ, dtype=np.float32)[:, None] * freqs[None, :]
    cos, sin = np.cos(angles), np.sin(angles)
    return (np.concatenate([cos, cos], 1).astype(np.float32),
            np.concatenate([-sin, sin], 1).astype(np.float32))


def head_cumsum_matrix():
    f = np.arange(D)
    same = (f[:, None] % DH) == (f[None, :] % DH)
    return (same & (f[:, None] // DH <= f[None, :] // DH)).astype(np.float32)


def routing_constants():
    e, p = np.arange(E), np.arange(P)[:, None]
    before = np.concatenate([e[None, :] < e[:, None], e[None, :] <= e[:, None]])
    columns = {
        "experts": e, "positions": np.arange(P), "blocks": np.arange(NB + 1), "block_floors": P * np.arange(TOKENS // P),
        "before": before.reshape(-1),
        "tokens": P * np.arange(NT)[None, :] + p - 2 * TOKENS,
        "spare_row": p - TOKENS,
    }
    return {k: np.broadcast_to(v, (P, v.shape[-1])).astype(np.float32) for k, v in columns.items()}


def routing_columns():
    widths = {k: v.shape[1] for k, v in routing_constants().items()}
    starts = np.cumsum([0, *widths.values()]).tolist()
    return starts[-1], {k: (at, n) for (k, n), at in zip(widths.items(), starts)}


def rank_matrices():
    p = np.arange(P)
    return np.concatenate([p[:, None] < p[None, :], np.ones((P, P), bool)], 1).astype(np.float16)


def build(nc, x, ctxT, w_qkv, b_qkv, w_o, b_o, wx_q, wx_k, wx_v, wx_c, bx_q, bx_k, bx_v, bx_c,
          wr, br, w1, b1, w2, b2, cos, sin, cumsum_m, ident, rank_m, route_c, rows, out):
    with ExitStack() as ctx:
        scope = ctx

        def sb(name, shape, dt=F32):
            return scope.enter_context(nc.sbuf_tensor(name, shape, dt))

        def sem(name):
            return ctx.enter_context(nc.semaphore(name))

        X = sb("X", [P, (NT + T) * D])
        wxq_sb = sb("wxq_sb", [P, KD, D])
        wxk_sb = sb("wxk_sb", [P, KD, D])
        wxv_sb = sb("wxv_sb", [P, KD, D])
        wxc_sb = sb("wxc_sb", [P, KD, D])
        bxq_sb = sb("bxq_sb", [P, KD])
        bxk_sb = sb("bxk_sb", [P, KD])
        bxv_sb = sb("bxv_sb", [P, KD])
        bxc_sb = sb("bxc_sb", [P, D])
        cum_sb = sb("cum_sb", [P, KD, D])
        wr_sb = sb("wr_sb", [P, KD, E])
        br_sb = sb("br_sb", [P, E])
        b1_sb = sb("b1_sb", [P, E * KF])
        id_sb = sb("id_sb", [P, P])
        id16 = sb("id16", [P, P], F16)
        stats = sb("stats", [P, 4, 6])
        mv = sb("mv", [P, 4, 2])
        var_eps = sb("var_eps", [P, 4])
        minus_half = sb("minus_half", [P, 4])
        guess = sb("guess", [P, 4])
        newton = sb("newton", [P, 3, 4])
        rstd = sb("rstd", [P, 4])
        xn = sb("xn", [P, 4, D])
        top_v = sb("top_v", [P, TOP, NT])
        top_e = sb("top_e", [P, TOP, NT])
        W1 = sb("W1", [P, E, KD, 2, DFF], F16)
        staged = [sb(f"staged{i}", [P, DFF]) for i in range(2)]

        attention = ctx.enter_context(ExitStack())
        scope = attention
        wqkv_sb = sb("wqkv_sb", [P, KD, 3 * D])
        bqkv_sb = sb("bqkv_sb", [P, 3 * D])
        wo_sb = sb("wo_sb", [P, QUADS, D])
        bo_sb = sb("bo_sb", [P, D])
        cos_sb = sb("cos_sb", [P, T, DH])
        sin_sb = sb("sin_sb", [P, T, DH])
        xnT = sb("xnT", [P, KD, SEQ])
        qk = sb("qk", [P, T, 2 * D])
        rot_c = sb("rot_c", [P, T, 2 * D])
        rot_s = sb("rot_s", [P, T, 2 * D])
        roped = rot_c
        v_raw = sb("v_raw", [P, T, D])
        q_stack = [sb(f"q_stack{i}", [P, T, H, STACK], F16) for i in range(2)]
        k_stack = [sb(f"k_stack{i}", [P, T, H, STACK], F16) for i in range(2)]
        qT = sb("qT", [P, PAIRS, SEQ], F16)
        mx = sb("mx", [P, T, H])
        qmT = [sb(f"qmT{i}", [P, PAIRS, SEQ], F16) for i in range(2)]
        kT = [sb(f"kT{i}", [P, H, SEQ], F16) for i in range(2)]
        v1 = [sb(f"v1{i}", [P, T, H, 2 * DH]) for i in range(2)]
        probs = [sb(f"probs{i}", [P, 4, SEQ]) for i in range(2)]
        o_rows = sb("o_rows", [P, 2 * SEQ // 32, 32])
        rsums = sb("rsums", [P, 2 * SEQ // 32])
        oT = sb("oT", [P, QUADS, SEQ])
        attention.close()

        scope = ctx
        W2 = sb("W2", [P, E, KF, 2, D], F16)
        XC = 4 * P
        NC = TOKENS // XC
        TC = XC // P
        cross = ctx.enter_context(ExitStack())
        scope = cross
        ctx_sb = [sb(f"ctx_sb{i}", [P, KD, XC]) for i in range(2)]
        xT = sb("xT", [P, KD, XC])
        k_exp = sb("k_exp", [P, KD, XC])
        relu = sb("relu", [P, KD, XC])
        mix = sb("mix", [P, KD, XC])
        q_exp = sb("q_exp", [P, KD, XC])
        xn3 = sb("xn3", [P, TC, D])
        xs = sb("xs", [P, TC, 2 * D], F16)
        lg = sb("lg", [P, TC, E])
        best_v = sb("best_v", [P, TC, 8])
        best_e = sb("best_e", [P, TC, 8], U32)
        cross.close()

        scope = ctx
        b2_sb = sb("b2_sb", [P, E, D])
        xg = [sb(f"xg{i}", [P, 2 * D], F16) for i in range(2)]
        xgT = [sb(f"xgT{i}", [P, 2, KD, P], F16) for i in range(2)]
        RC, RC_AT = routing_columns()
        route_sb = sb("route_sb", [P, RC])
        rank_sb = sb("rank_sb", [P, 2 * P], F16)
        gates = sb("gates", [P, TOP, NT])
        block_gates = sb("block_gates", [P, NB])
        block_scales = sb("block_scales", [P, NB])
        block_rows = sb("block_rows", [P, NB], I32)
        block_expert = sb("block_expert", [P, NB + 1], I32)
        expert_pairs = sb("expert_pairs", [P, (NB + 1) // 2], I32)
        gather_ids = [sb(f"gather_ids{i}", [P, 1], I32) for i in range(2)]
        add_ids = [sb(f"add_ids{i}", [P, 1], I32) for i in range(2)]
        routing = ctx.enter_context(ExitStack())
        scope = routing
        oh = sb("oh", [P, TOP, NT, E])
        oh_any = sb("oh_any", [P, NT + 1, E], F16)
        v_gap = sb("v_gap", [P, NT])
        v_exp = sb("v_exp", [P, NT])
        v_sum = sb("v_sum", [P, NT])
        above = sb("above", [P, E, TOKENS // P])
        expert_blocks = sb("expert_blocks", [P, E])
        bounds_of = sb("bounds_of", [P, 2 * E, E])
        bounds = sb("bounds", [P, 2 * E])
        place_of = sb("place_of", [P, NT, E])
        oh_place = sb("oh_place", [P, TOP, NT, E])
        place = sb("place", [P, TOP * NT])
        place_i = sb("place_i", [P, TOP * NT], I32)
        block_i = sb("block_i", [P, TOP * NT], I32)
        block_f = sb("block_f", [P, TOP * NT])
        pos = sb("pos", [P, TOP * NT])
        table = sb("table", [P, TOP * NT, 2, NB])
        reached = sb("reached", [P, NB + 1, E])
        owner = sb("owner", [P, NB + 1])
        spare_ids = sb("spare_ids", [P, NB])
        pos_oh = [s[:, :].rearrange("p (j q) -> p j q", q=P) for s in staged]
        routing.close()
        scope = ctx
        hid = [sb(f"hid{i}", [P, KF, P]) for i in range(2)]
        hid_hi = [sb(f"hid_hi{i}", [P, KF, P], F16) for i in range(2)]
        hid_lo = [sb(f"hid_lo{i}", [P, KF, P], F16) for i in range(2)]
        gated_b2 = [sb(f"gated_b2{i}", [P, D]) for i in range(2)]
        y = [sb(f"y{i}", [P, D]) for i in range(2)]
        w1_now = [X[:, i * KD * DFF:(i + 1) * KD * DFF].bitcast(F16).rearrange("p (k h n) -> p k h n", k=KD, h=2) for i in range(2)]

        def const(name):
            at_, n = RC_AT[name]
            return route_sb[:, at_:at_ + n]

        s1_ps = ctx.enter_context(nc.psum_tensor("s1_ps", [P, 512], F32))
        s2_ps = [ctx.enter_context(nc.psum_tensor(f"s2_ps{i}", [P, 512], F32)) for i in range(2)]
        o_ps = ctx.enter_context(nc.psum_tensor("o_ps", [P, 512], F32))
        s_ps = [ctx.enter_context(nc.psum_tensor(f"s_ps{i}", [P, 4, SEQ], F32)) for i in range(2)]
        s_halves = [s_ps[i][:, 2 * j:2 * j + 2, :].rearrange("p h s -> p (h s)") for i in range(2) for j in range(2)]
        xT_ps = [s1_ps[:, :], o_ps[:, :]]
        kv_ps = [s2_ps[0][:, :], s2_ps[1][:, :]]
        cq_ps, wc_ps = s_halves[0:2], s_halves[2:4]
        rank_ps = s2_ps[0][:, 0:(NT + 1) * E].rearrange("p (t e) -> p t e", e=E)
        table_ps = s2_ps[1][:, 0:2 * NB]
        xgT_ps = [bank[:, 0:D].bitcast(F16).rearrange("p (h k s) -> p h k s", h=2, k=KD) for bank in (s1_ps, o_ps)]
        hid_ps = [s_ps[i][:, :, :].rearrange("p h s -> p (h s)").rearrange("p (m s) -> p m s", s=P) for i in range(2)]
        y_ps = [bank[:, 0:D] for bank in s2_ps]

        x0_loaded = sem("x0_loaded")
        x_loaded = sem("x_loaded")
        wqkv_loaded = sem("wqkv_loaded")
        wo_loaded = sem("wo_loaded")
        cross_loaded = sem("cross_loaded")
        stacks_cleared = sem("stacks_cleared")
        consts_set = sem("consts_set")
        half_set = sem("half_set")
        keys_cleared = sem("keys_cleared")
        id16_ready = sem("id16_ready")
        ln_stats = sem("ln_stats")
        ln_mv = sem("ln_mv")
        var_ready = sem("var_ready")
        guess_ready = sem("guess_ready")
        newton_step = sem("newton_step")
        ln_rstd = sem("ln_rstd")
        xn_ready = sem("xn_ready")
        s1_done = sem("s1_done")
        s1_moved = sem("s1_moved")
        v_ready = sem("v_ready")
        s2_done = sem("s2_done")
        s2_moved = [sem(f"s2_moved{i}") for i in range(2)]
        rot_c_ready = sem("rot_c_ready")
        rot_s_ready = sem("rot_s_ready")
        roped_ready = sem("roped_ready")
        hi_ready = sem("hi_ready")
        lo_ready = sem("lo_ready")
        even_kT_moved = sem("even_kT_moved")
        negm_ready = sem("negm_ready")
        xb_ready = sem("xb_ready")
        scores_ready = sem("scores_ready")
        exp_done = sem("exp_done")
        pv_done = sem("pv_done")
        o_scaled = sem("o_scaled")
        oT_ready = sem("oT_ready")
        rsums_ready = sem("rsums_ready")
        o_moved = sem("o_moved")
        wo_done = sem("wo_done")
        k_done = sem("k_done")
        k_moved = sem("k_moved")
        cum_done = sem("cum_done")
        cum_moved = sem("cum_moved")
        v_done = sem("v_done")
        v_moved = sem("v_moved")
        xnT_done = sem("xnT_done")
        xnT_moved = sem("xnT_moved")
        q_done = sem("q_done")
        q_moved = sem("q_moved")
        x3T_done = sem("x3T_done")
        x3T_moved = sem("x3T_moved")
        logits_done = sem("logits_done")
        logits_moved = sem("logits_moved")
        wc_done = sem("wc_done")
        wc_moved = sem("wc_moved")
        ctx_loaded = sem("ctx_loaded")
        xc_ready = sem("xc_ready")
        xc_normed = sem("xc_normed")
        x3_normed = sem("x3_normed")
        k_heads_ready = sem("k_heads_ready")
        ratio_ready = sem("ratio_ready")
        q_heads_ready = sem("q_heads_ready")
        mixed_ready = sem("mixed_ready")
        x3_high = sem("x3_high")
        x3_low = sem("x3_low")
        rows_stored = sem("rows_stored")
        x_stored = sem("x_stored")
        spare_stored = sem("spare_stored")
        best_found = sem("best_found")
        best_kept = sem("best_kept")
        route_loaded = sem("route_loaded")
        b2_loaded = sem("b2_loaded")
        zeros_set = sem("zeros_set")
        gap_ready = sem("gap_ready")
        gap_exp = sem("gap_exp")
        choices_ready = sem("choices_ready")
        ranks_done = sem("ranks_done")
        routed = sem("routed")
        table_ready = sem("table_ready")
        pos_ready = sem("pos_ready")
        pos_used = sem("pos_used")
        table_done = sem("table_done")
        experts_ready = sem("experts_ready")
        ids_ready = sem("ids_ready")
        ids_copied = sem("ids_copied")
        xg_transposed = sem("xg_transposed")
        xgT_moved = sem("xgT_moved")
        first_done = sem("first_done")
        gelu_done = sem("gelu_done")
        hi_split = sem("hi_split")
        lo_split = sem("lo_split")
        second_done = sem("second_done")
        gated_b2_ready = sem("gated_b2_ready")
        y_ready = sem("y_ready")
        added = sem("added")
        w1_copied = sem("w1_copied")
        gathered = [sem(f"gathered{i}") for i in range(2)]
        w_loaded = [sem(f"w_loaded{i}") for i in range(2)]
        w_scaled = sem("w_scaled")
        w_high = sem("w_high")
        w_low = sem("w_low")

        def s2_slot(b, u):
            return u % 2, S2_USES // 2 * b + u // 2

        def at(eng, count):
            return count if isinstance(count, int) else eng.to_reg(count)

        def seq_rows(b):
            return X[:, bass.ds(b * T * D, T * D)].rearrange("p (t d) -> p t d", t=T)

        def iterations(eng, step):
            step(-2, 0, (True, False, False))
            step(-1, 1, (True, True, False))
            with eng.Fori(0, (BATCH - 2) // 2) as two:
                step(2 * two, 0, (True, True, True))
                step(2 * two + 1, 1, (True, True, True))
            step(BATCH - 2, 0, (False, True, True))
            step(BATCH - 1, 1, (False, False, True))

        def cross_steps(eng, step):
            step(0, 0, False, True)
            with eng.Fori(0, (NC - 2) // 2) as two:
                step(2 * two + 1, 1, True, True)
                step(2 * two + 2, 0, True, True)
            step(NC - 1, 1, True, False)

        def expert_pair(eng, two):
            pair = eng.value_load(expert_pairs[0:1, bass.ds(two, 1)], min_val=0, max_val=E * E - 1)
            return pair % E, pair // E

        def blocks_in_turn(eng, step, experts_of=None):
            def pair(two):
                return (None, None) if experts_of is None else expert_pair(eng, two + experts_of // 2)

            def steps(two):
                e = pair(two)
                step(two, 0, 3, e[0])
                step(two, 1, 3, e[1])

            steps(0)
            with eng.Fori(1, (NB - 3) // 2) as two:
                steps(two)
            last = (NB - 3) // 2
            e = pair(last)
            step(last, 0, 2, e[0])
            step(last, 1, 1, e[1])
            e = pair(last + 1) if experts_of == 0 else e
            step(last + 1, 0, 0, e[0])

        XN0 = T * (BATCH + 1)

        block = ctx.enter_context(nc.Block())

        @block.sync
        def _(sp):
            xv = x.rearrange("(t p) d -> p t d", p=P)
            Xv = X[:, :].rearrange("p (t d) -> p t d", d=D)
            sp.dma_start(Xv[:, 0:T, :], xv[:, 0:T, :]).then_inc(x0_loaded, 16)
            sp.dma_start(id_sb[:, :], ident).then_inc(x0_loaded, 16)
            sp.dma_start(wqkv_sb[:, :, :], w_qkv.rearrange("(k p) n -> p k n", p=P)).then_inc(wqkv_loaded, 16)
            sp.dma_start(bqkv_sb[:, :], b_qkv.partition_broadcast(P)).then_inc(wqkv_loaded, 16)
            sp.dma_start(cos_sb[:, :, :], cos.rearrange("(t p) n -> p t n", p=P)).then_inc(wqkv_loaded, 16)
            sp.dma_start(sin_sb[:, :, :], sin.rearrange("(t p) n -> p t n", p=P)).then_inc(wqkv_loaded, 16)
            sp.dma_start(Xv[:, T:NT, :], xv[:, T:, :]).then_inc(x_loaded, 16)
            sp.dma_start(wo_sb[:, :, :], w_o.rearrange("(k p) n -> p k n", p=P)).then_inc(wo_loaded, 16)
            sp.dma_start(bo_sb[:, :], b_o.partition_broadcast(P)).then_inc(wo_loaded, 16)

            for k in range(KD):
                sp.dma_start(staged[k][:, :], w1[0, k * P:(k + 1) * P, :]).then_inc(w_loaded[k], 16)
            for dst, src in ((wxq_sb, wx_q), (wxk_sb, wx_k), (wxv_sb, wx_v), (wxc_sb, wx_c), (cum_sb, cumsum_m),
                             (wr_sb, wr)):
                sp.dma_start(dst[:, :, :], src.rearrange("(k p) n -> p k n", p=P)).then_inc(cross_loaded, 16)
            for dst, src in ((bxq_sb, bx_q), (bxk_sb, bx_k), (bxv_sb, bx_v), (b1_sb, b1)):
                sp.dma_start(dst[:, :], src.rearrange("(k p) -> p k", p=P),
                             allow_slow_non_contiguous=True).then_inc(cross_loaded, 16)
            for dst, src in ((bxc_sb, bx_c), (br_sb, br)):
                sp.dma_start(dst[:, :], src.partition_broadcast(P)).then_inc(cross_loaded, 16)
            sp.wait_ge(consts_set, 5)
            spare = X[:, NT * D:(NT + 1) * D]
            sp.dma_start(out[TOKENS:, :], spare).then_inc(spare_stored, 16)
            sp.dma_start(rows[TOKENS:, :], spare.bitcast(F16)).then_inc(spare_stored, 16)
            with sp.Fori(1, E) as e:
                for k in range(KD):
                    sp.wait_ge(w_low, 2 * e + k - 1)
                    sp.dma_start(staged[k][:, :], w1[bass.ds(e, 1), k * P:(k + 1) * P, :]
                                 .rearrange("e p n -> (e p) n")).then_inc(w_loaded[k], 16)

            def second_layer(c, u):
                sp.wait_ge(w_low, 2 * E + 4 * c + u - 1)
                half = KF // 2
                src = w2[bass.ds(2 * c + u // 2, 1), (u % 2) * half * P:(u % 2 + 1) * half * P, :]
                sp.dma_start(staged[u % 2][:, :].rearrange("p (k n) -> p k n", n=D),
                             src.rearrange("e (k p) n -> p (e k) n", p=P)).then_inc(w_loaded[u % 2], 16)

            def load_ctx(c, o):
                if not isinstance(c, int) or c > 0:
                    sp.wait_ge(ctx_loaded, 16 * c)
                sp.dma_start(ctx_sb[o][:, :, :], ctxT[:, bass.ds(c * XC, XC)].rearrange("(k p) n -> p k n", p=P)
                             ).then_inc(ctx_loaded, 16)

            def store_x(c):
                sp.wait_ge(wc_moved, 2 * c + 2)
                sp.dma_start(out[bass.ds(c * XC, XC), :].rearrange("(t p) d -> p t d", p=P),
                             X[:, bass.ds(c * TC * D, TC * D)].rearrange("p (t d) -> p t d", d=D)).then_inc(x_stored, 16)

            def store_rows(c):
                sp.wait_ge(x3_high, c + 1)
                sp.wait_ge(x3_low, c + 1)
                sp.dma_start(rows[bass.ds(c * XC, XC), :].rearrange("(t p) d -> p t d", p=P),
                             xs[:, :, :]).then_inc(rows_stored, 16)

            sp.wait_ge(o_moved, 1 + O_USES * BATCH)
            load_ctx(0, 0)
            load_ctx(1, 1)

            def cross_step(c, o, has_last, has_next):
                second_layer(c, 0)
                second_layer(c, 1)
                if has_last:
                    store_x(c - 1)
                    if has_next:
                        sp.wait_ge(k_done, KD * c + KD)
                        sp.wait_ge(v_done, KD * c)
                        load_ctx(c + 1, 1 - o)
                second_layer(c, 2)
                second_layer(c, 3)
                if has_last:
                    store_rows(c - 1)

            cross_steps(sp, cross_step)
            store_x(NC - 1)
            sp.dma_start(route_sb[:, :], route_c).then_inc(route_loaded, 16)
            sp.dma_start(rank_sb[:, :], rank_m).then_inc(route_loaded, 16)
            sp.dma_start(b2_sb[:, :, :].rearrange("p e n -> p (e n)"),
                         b2.rearrange("e n -> (e n)").partition_broadcast(P)).then_inc(b2_loaded, 16)
            store_rows(NC - 1)
            sp.wait_ge(spare_stored, 32)
            sp.wait_ge(x_stored, 16 * NC)
            sp.wait_ge(rows_stored, 16 * NC)
            sp.wait_ge(added, 16 * NB)

        CROSS_LOADS = 12 * 16

        @block.gpsimd
        def _(pool):
            nc.gpsimd.memset(minus_half[:, :], -0.5).then_inc(half_set, 1)
            pool.wait_ge(half_set, 1)
            def inverse_deviation(n, tiles, stats_done):
                c = slice(0, tiles)
                stats_done, halved = at(pool, stats_done), at(pool, 3 * n + 2)
                pool.wait_ge(half_set, 1)
                pool.wait_ge(ln_mv, stats_done)
                nc.gpsimd.tensor_scalar(var_eps[:, c], mv[:, c, 1], EPS, None, ALU.add).then_inc(var_ready, 1)
                pool.wait_ge(var_ready, n + 1)
                nc.gpsimd.tensor_tensor(guess[:, c], var_eps[:, c], minus_half[:, c], ALU.pow).then_inc(guess_ready, 1)
                pool.wait_ge(guess_ready, n + 1)
                nc.gpsimd.tensor_tensor(newton[:, 0, c], guess[:, c], guess[:, c], ALU.mult).then_inc(newton_step, 1)
                pool.wait_ge(newton_step, 3 * n + 1)
                nc.gpsimd.tensor_tensor(newton[:, 1, c], newton[:, 0, c], var_eps[:, c], ALU.mult).then_inc(newton_step, 1)
                pool.wait_ge(half_set, 1)
                pool.wait_ge(newton_step, halved)
                nc.gpsimd.tensor_scalar(newton[:, 2, c], newton[:, 1, c], -0.5, 1.5, ALU.mult, ALU.add).then_inc(newton_step, 1)
                pool.wait_ge(newton_step, 3 * n + 3)
                nc.gpsimd.tensor_tensor(rstd[:, c], guess[:, c], newton[:, 2, c], ALU.mult).then_inc(ln_rstd, 1)

            def values(b, o):
                for u in U_V:
                    pool.wait_ge(s1_moved, S1_USES * b + u + 1)
                if not isinstance(b, int) or b >= 2:
                    pool.wait_ge(pv_done, GROUPS * (b - 1) + 1)
                nc.gpsimd.tensor_tensor(v1[o][:, :, :, 0:DH], v_raw[:, :, :].rearrange("p t (h d) -> p t h d", d=DH),
                                        bqkv_sb[:, 2 * D:].rearrange("p (h d) -> p h d", d=DH).unsqueeze(1)
                                        .to_broadcast([P, T, H, DH]), ALU.add).then_inc(v_ready, 1)

            def low_parts(b, k):
                high = at(pool, 2 * b + k + 1)
                pool.wait_ge(half_set, 1)
                pool.wait_ge(w_high, high)
                dst = W1[:, bass.ds(b, 1), k, :, :]
                nc.gpsimd.tensor_tensor(dst[:, 0, 1, :], staged[k][:, :], dst[:, 0, 0, :],
                                        ALU.subtract).then_inc(w_low, 1)

            def add_output_bias(b):
                pool.wait_ge(wo_loaded, 32)
                pool.wait_ge(xn_ready, T * b + T)
                rows = seq_rows(b)
                nc.gpsimd.tensor_tensor(rows, rows, bo_sb[:, :].unsqueeze(1).to_broadcast([P, T, D]),
                                        ALU.add).then_inc(xb_ready, 1)

            def rotate(b, t):
                pool.wait_ge(s1_moved, S1_USES * b + U_QK[t] + 1)
                nc.gpsimd.tensor_tensor(
                    rot_c[:, t, :].rearrange("p (h d) -> p h d", d=DH),
                    qk[:, t, :].rearrange("p (h d) -> p h d", d=DH),
                    cos_sb[:, t, :].unsqueeze(1).to_broadcast([P, 2 * H, DH]), ALU.mult).then_inc(rot_c_ready, 1)
                pool.wait_ge(rot_c_ready, T * b + t + 1)
                pool.wait_ge(rot_s_ready, T * b + t + 1)
                nc.gpsimd.tensor_tensor(roped[:, t, :], rot_c[:, t, :], rot_s[:, t, :], ALU.add).then_inc(roped_ready, 1)

            def low_stacks(b, o, t):
                heads = roped[:, t, :].rearrange("p (w h d) -> p w h d", w=2, d=DH)
                qs, ks = q_stack[o][:, t], k_stack[o][:, t]
                high = at(pool, 2 * T * b + 2 * t + 2)
                pool.wait_ge(half_set, 1)
                pool.wait_ge(hi_ready, high)
                nc.gpsimd.memset(qs[:, :, ROW_MAX:ROW_MAX + 1], 0.0).then_inc(lo_ready, 1)
                nc.gpsimd.tensor_tensor(qs[:, :, 48:64], heads[:, 0], qs[:, :, 0:16], ALU.subtract).then_inc(lo_ready, 1)
                nc.gpsimd.tensor_tensor(ks[:, :, 16:32], heads[:, 1], ks[:, :, 0:16], ALU.subtract).then_inc(lo_ready, 1)

            def shift(b, o, t):
                last_two = [s2_slot(b, U_SC[g]) for g in (PAIRS * t + PAIRS - 2, PAIRS * t + PAIRS - 1)]
                moved = [at(pool, n + 1) for _, n in last_two]
                pool.wait_ge(half_set, 1)
                for (bank, _), n in zip(last_two, moved):
                    pool.wait_ge(s2_moved[bank], n)
                nc.gpsimd.tensor_scalar(q_stack[o][:, t, :, ROW_MAX], mx[:, t, :], -1.0, None,
                                        ALU.mult).then_inc(negm_ready, 1)

            def step(j, o, stages):
                if stages[1]:
                    values(j + 1, 1 - o)
                    low_parts(j + 1, 1)
                if stages[0]:
                    rotate(j + 2, 0)
                    low_stacks(j + 2, o, 0)
                    rotate(j + 2, 1)
                if stages[1]:
                    shift(j + 1, 1 - o, 0)
                if stages[0]:
                    low_stacks(j + 2, o, 1)
                    add_output_bias(j + 2)
                    low_parts(j + 2, 0)
                if stages[1]:
                    shift(j + 1, 1 - o, 1)
                if stages[0]:
                    inverse_deviation(j + 3, T, T * (j + 3) + T)

            inverse_deviation(0, T, T)
            for i in range(2):
                nc.gpsimd.memset(q_stack[i][:, :, :, ROW_MAX:ROW_MAX + DH], 0.0).then_inc(stacks_cleared, 1)
                nc.gpsimd.memset(k_stack[i][:, :, :, ROW_MAX:ROW_MAX + DH], 0.0).then_inc(stacks_cleared, 1)
            nc.gpsimd.memset(X[:, NT * D:], 0.0).then_inc(consts_set, 1)
            pool.wait_ge(stacks_cleared, 4)
            for i in range(2):
                nc.gpsimd.memset(k_stack[i][:, :, :, ROW_MAX:ROW_MAX + 1], 1.0).then_inc(consts_set, 1)
                nc.gpsimd.memset(v1[i][:, :, :, DH:], 1.0).then_inc(consts_set, 1)
            pool.wait_ge(consts_set, 5)
            pool.wait_ge(wqkv_loaded, 64)
            iterations(pool, step)

            pool.wait_ge(cross_loaded, CROSS_LOADS)
            LN0 = BATCH + 1
            inverse_deviation(LN0, TC, XN0 + TC)

            def second_low(c, u):
                high = at(pool, 2 * E + 4 * c + u + 1)
                pool.wait_ge(half_set, 1)
                pool.wait_ge(w_high, high)
                dst = W2[:, bass.ds(2 * c + u // 2, 1), (u % 2) * KF // 2:(u % 2 + 1) * KF // 2, :, :]
                nc.gpsimd.tensor_tensor(dst[:, 0, :, 1, :], staged[u % 2][:, :].rearrange("p (k n) -> p k n", n=D),
                                        dst[:, 0, :, 0, :], ALU.subtract).then_inc(w_low, 1)

            def low_rows(c):
                pool.wait_ge(x3_high, c + 1)
                nc.gpsimd.tensor_tensor(xs[:, :, D:], xn3[:, :, :], xs[:, :, 0:D], ALU.subtract).then_inc(x3_low, 1)

            def cross_step(c, o, has_last, has_next):
                if has_last:
                    inverse_deviation(LN0 + 2 * c, TC, XN0 + TC * (2 * c + 1))
                second_low(c, 0)
                pool.wait_ge(xc_normed, TC * c + TC)
                chunk = X[:, bass.ds(c * TC * D, TC * D)].rearrange("p (t d) -> p t d", t=TC)
                nc.gpsimd.tensor_tensor(chunk, chunk, bxc_sb[:, :].unsqueeze(1).to_broadcast([P, TC, D]),
                                        ALU.add).then_inc(xc_ready, 1)
                for m in range(KD):
                    pool.wait_ge(cum_moved, KD * c + m + 1)
                    nc.gpsimd.tensor_tensor(mix[:, m, :], k_exp[:, m, :], mix[:, m, :], ALU.mult).then_inc(ratio_ready, 1)
                second_low(c, 1)
                if has_next:
                    inverse_deviation(LN0 + 2 * c + 1, TC, XN0 + TC * (2 * c + 2))
                for m in range(KD):
                    pool.wait_ge(q_heads_ready, KD * c + m + 1)
                    nc.gpsimd.tensor_tensor(mix[:, m, :], q_exp[:, m, :], mix[:, m, :], ALU.mult).then_inc(mixed_ready, 1)
                second_low(c, 2)
                if has_last:
                    low_rows(c - 1)
                second_low(c, 3)

            cross_steps(pool, cross_step)
            inverse_deviation(LN0 + 2 * NC - 1, TC, XN0 + TC * 2 * NC)
            low_rows(NC - 1)

            pool.wait_ge(b2_loaded, 16)
            pool.wait_ge(rows_stored, 16 * NC)
            pool.wait_ge(x_stored, 16 * NC)
            pool.wait_ge(spare_stored, 32)
            pool.wait_ge(experts_ready, 2)
            pool.wait_ge(ids_ready, 3)

            def gather(i, o, copies):
                if not isinstance(i, int) or i >= 2:
                    pool.wait_ge(half_set, 1)
                    pool.wait_ge(xg_transposed, at(pool, i - 1))
                nc.gpsimd.tensor_copy(gather_ids[o][:, :], block_rows[:, bass.ds(i, 1)]).then_inc(ids_copied, 1)
                copied = at(pool, copies + 1)
                pool.wait_ge(half_set, 1)
                pool.wait_ge(ids_copied, copied)
                nc.gpsimd.indirect_dma_start(xg[o][:, :], None, rows, bass.IndirectOffsetOnAxis(ap=gather_ids[o][:, :], axis=0)
                                             ).then_inc(gathered[o], 16)

            def gate_b2(i, o):
                e = pool.value_load(block_expert[0:1, bass.ds(i, 1)], min_val=0, max_val=E - 1)
                if not isinstance(i, int) or i >= 2:
                    pool.wait_ge(half_set, 1)
                    pool.wait_ge(y_ready, at(pool, i - 1))
                nc.gpsimd.tensor_tensor(gated_b2[o][:, :].unsqueeze(1), b2_sb[:, bass.ds(e, 1), :],
                                        block_gates[:, bass.ds(i, 1)].unsqueeze(2).to_broadcast([P, 1, D]),
                                        ALU.mult).then_inc(gated_b2_ready, 1)

            def add(i, o, copies):
                nc.gpsimd.tensor_copy(add_ids[o][:, :], block_rows[:, bass.ds(i, 1)]).then_inc(ids_copied, 1)
                copied, have, before = at(pool, copies + 1), at(pool, i + 1), at(pool, 16 * i)
                pool.wait_ge(half_set, 1)
                pool.wait_ge(ids_copied, copied)
                pool.wait_ge(y_ready, have)
                pool.wait_ge(added, before)
                nc.gpsimd.indirect_dma_start(out, bass.IndirectOffsetOnAxis(ap=add_ids[o][:, :], axis=0), y[o][:, :], None,
                                             compute_op=ALU.add).then_inc(added, 16)

            def block_step(two, o, ahead, e):
                i = 2 * two + o
                if ahead >= 3:
                    gather(i + 3, 1 - o, 3 + 2 * i)
                if ahead >= 1:
                    gate_b2(i + 1, 1 - o)
                add(i, o, 2 * i + 4 if ahead >= 3 else i + NB)

            for i in range(3):
                gather(i, i % 2, i)
            gate_b2(0, 0)
            blocks_in_turn(pool, block_step)

        @block.scalar
        def _(act):
            act.wait_ge(x0_loaded, 32)
            nc.scalar.copy(id16[:, :], id_sb[:, :]).then_inc(id16_ready, 1)

            def move_xnT(b):
                act.wait_ge(s1_done, S1_USES * b + U_XNT + 1)
                nc.scalar.copy(xnT[:, :, :], s1_ps[:, :].rearrange("p (k s) -> p k s", k=KD)).then_inc(s1_moved, 1)

            def move_v(b, t):
                act.wait_ge(s1_done, S1_USES * b + U_V[t] + 1)
                if t == 0 and (not isinstance(b, int) or b >= 1):
                    act.wait_ge(v_ready, b)
                nc.scalar.copy(v_raw[:, t, :], s1_ps[:, 0:D]).then_inc(s1_moved, 1)

            def high_parts(b, o, t):
                act.wait_ge(roped_ready, T * b + t + 1)
                heads = roped[:, t, :].rearrange("p (w h d) -> p w h d", w=2, d=DH)
                for w, dst in ((0, q_stack[o][:, t, :, 0:32].rearrange("p h (r d) -> p h r d", d=DH)),
                               (1, k_stack[o][:, t, :, :].rearrange("p h (r d) -> p h r d", d=DH)[:, :, 0:4:3, :])):
                    nc.scalar.copy(dst, heads[:, w].unsqueeze(2).to_broadcast([P, H, 2, DH])).then_inc(hi_ready, 1)

            def move_even_kT(b, o, r):
                bank, _ = s2_slot(b, U_KT[r])
                act.wait_ge(s2_done, S2_USES * b + U_KT[r] + 1)
                src = s2_ps[bank][:, :].bitcast(F16).rearrange("p (a s) -> p a s", s=SEQ)
                dst = kT[o][:, 8 * r:8 * r + 8, :].rearrange("p (a two) s -> p a two s", two=2)
                nc.scalar.copy(dst[0:64, :, 0, :], src[0:64]).then_inc(even_kT_moved, 1)

            def move_qmT(b, o, t):
                bank, _ = s2_slot(b, U_RT[t])
                act.wait_ge(s2_done, S2_USES * b + U_RT[t] + 1)
                src = s2_ps[bank][:, :].bitcast(F16).rearrange("p (a s) -> p a s", s=P)
                nc.scalar.copy(qmT[o][:, :, t * P:(t + 1) * P], src).then_inc(s2_moved[bank], 1)

            def exponentials(b, g):
                act.wait_ge(scores_ready, GROUPS * b + g + 1)
                if g >= 2:
                    act.wait_ge(pv_done, GROUPS * b + g - 1)
                nc.scalar.activation(probs[g % 2][:, :, :], s_ps[g % 2][:, :, :], ACT.Exp,
                                     scale=SCALE).then_inc(exp_done, 1)

            def high_weights(u, place, loads, dst):
                act.wait_ge(w_loaded[place], 16 * loads)
                nc.scalar.activation(staged[place][:, :], staged[place][:, :], ACT.Copy, scale=WSCALE).then_inc(w_scaled, 1)
                scaled = at(act, u + 1)
                act.wait_ge(consts_set, 5)
                act.wait_ge(w_scaled, scaled)
                nc.scalar.copy(dst, staged[place][:, :].rearrange("p (k n) -> p k n", n=dst.shape[-1])).then_inc(w_high, 1)

            def first_layer(b, k):
                high_weights(2 * b + k, k, b + 1, W1[:, bass.ds(b, 1), k, 0, :])

            def step(j, o, stages):
                def s3(*groups):
                    if stages[2]:
                        for g in groups:
                            exponentials(j, g)

                if stages[0]:
                    move_xnT(j + 2)
                if stages[1]:
                    move_even_kT(j + 1, 1 - o, 1)
                s3(0, 1)
                if stages[0]:
                    first_layer(j + 2, 0)
                s3(2, 3, 4)
                if stages[0]:
                    high_parts(j + 2, o, 0)
                s3(5, 6, 7)
                if stages[0]:
                    high_parts(j + 2, o, 1)
                if stages[1]:
                    move_qmT(j + 1, 1 - o, 0)
                if stages[0]:
                    move_v(j + 2, 0)
                    move_v(j + 2, 1)
                    first_layer(j + 2, 1)
                if stages[1]:
                    move_qmT(j + 1, 1 - o, 1)
                if stages[0]:
                    move_even_kT(j + 2, o, 0)

            act.wait_ge(consts_set, 5)
            iterations(act, step)

            act.wait_ge(cross_loaded, CROSS_LOADS)

            def elu_parts(m, src, bias, exp):
                nc.scalar.activation(exp[:, m, :], src, ACT.Exp, bias=bias[:, m:m + 1])
                return nc.scalar.activation(relu[:, m, :], src, ACT.Relu, bias=bias[:, m:m + 1])

            def key_parts(c):
                for m in range(KD):
                    act.wait_ge(k_done, KD * c + m + 1)
                    if not isinstance(c, int) or c > 0:
                        act.wait_ge(q_heads_ready, KD * c)
                        act.wait_ge(ratio_ready, KD * c)
                    elu_parts(m, kv_ps[m], bxk_sb, k_exp).then_inc(k_moved, 1)

            def second_layer(c, u):
                high_weights(2 * E + 4 * c + u, u % 2, E + 2 * c + u // 2 + 1,
                             W2[:, bass.ds(2 * c + u // 2, 1), (u % 2) * KF // 2:(u % 2 + 1) * KF // 2, 0, :]
                             .rearrange("p e k n -> p (e k) n"))

            def high_rows(c):
                act.wait_ge(x3_normed, TC * c + TC)
                if not isinstance(c, int) or c > 0:
                    act.wait_ge(rows_stored, 16 * c)
                nc.scalar.copy(xs[:, :, 0:D], xn3[:, :, :]).then_inc(x3_high, 1)

            def move_x3T(c):
                for k in range(KD):
                    act.wait_ge(x3T_done, KD * c + k + 1)
                    nc.scalar.copy(xT[:, k, :], xT_ps[k]).then_inc(x3T_moved, 1)

            def cross_step(c, o, has_last, has_next):
                for k in range(KD):
                    act.wait_ge(xnT_done, KD * c + k + 1)
                    nc.scalar.copy(xT[:, k, :], xT_ps[k]).then_inc(xnT_moved, 1)
                second_layer(c, 0)
                if has_last:
                    high_rows(c - 1)
                for m in range(KD):
                    act.wait_ge(q_done, KD * c + m + 1)
                    act.wait_ge(k_heads_ready, KD * c + KD)
                    elu_parts(m, cq_ps[m], bxq_sb, q_exp).then_inc(q_moved, 1)
                second_layer(c, 1)
                if has_last:
                    move_x3T(c - 1)
                second_layer(c, 2)
                if has_next:
                    key_parts(c + 1)
                second_layer(c, 3)

            key_parts(0)
            cross_steps(act, cross_step)
            high_rows(NC - 1)
            move_x3T(NC - 1)

            act.wait_ge(gap_ready, 1)
            nc.scalar.activation(v_exp[:, :], v_gap[:, :], ACT.Exp).then_inc(gap_exp, 1)

            act.wait_ge(experts_ready, 2)

            def hidden(i, o):
                e = act.value_load(block_expert[0:1, bass.ds(i, 1)], min_val=0, max_val=E - 1)
                for m in range(KF):
                    have = at(act, 2 * i + m // (KF // 2) + 1)
                    split = at(act, 2 * i - 2)
                    act.wait_ge(consts_set, 5)
                    act.wait_ge(first_done, have)
                    if m == 0 and (not isinstance(i, int) or i >= 2):
                        act.wait_ge(lo_split, split)
                    nc.scalar.activation(hid[o][:, m, :], hid_ps[o][:, m, :], ACT.Gelu_apprx_tanh,
                                         bias=b1_sb[:, bass.ds(e * KF + m, 1)], scale=1 / WSCALE).then_inc(gelu_done, 1)

            def block_step(two, o, ahead, e):
                if ahead >= 1:
                    hidden(2 * two + o + 1, 1 - o)

            hidden(0, 0)
            blocks_in_turn(act, block_step)

        @block.vector
        def _(dve):
            def statistics(b):
                rows = seq_rows(b)
                if not isinstance(b, int) or b > 0:
                    dve.wait_ge(x_loaded, 16)
                for t in range(T):
                    nc.vector.bn_stats(stats[:, t, :], rows[:, t, :]).then_inc(ln_stats, 1)
                for t in range(T):
                    have = at(dve, T * b + t + 1)
                    dve.wait_ge(x0_loaded, 32)
                    dve.wait_ge(ln_stats, have)
                    nc.vector.bn_aggr(mv[:, t, :], stats[:, t, :]).then_inc(ln_mv, 1)

            def normalise(b):
                rows = seq_rows(b)
                dve.wait_ge(ln_rstd, b + 1)
                for t in range(T):
                    nc.vector.tensor_scalar(xn[:, t, :], rows[:, t, :], mv[:, t, 0:1], rstd[:, t:t + 1],
                                            ALU.subtract, ALU.mult).then_inc(xn_ready, 1)

            def add_bias(b, t):
                dve.wait_ge(s1_done, S1_USES * b + U_QK[t] + 1)
                nc.vector.tensor_tensor(qk[:, t, :], s1_ps[:, :], bqkv_sb[:, 0:2 * D], ALU.add).then_inc(s1_moved, 1)

            def rotate_swapped(b, t):
                dve.wait_ge(s1_moved, S1_USES * b + U_QK[t] + 1)
                src = qk[:, t, :].rearrange("p (h two e) -> p h two e", two=2, e=DH // 2)
                dst = rot_s[:, t, :].rearrange("p (h two e) -> p h two e", two=2, e=DH // 2)
                sn = sin_sb[:, t, :].rearrange("p (two e) -> p two e", two=2)
                for half in range(2):
                    last = nc.vector.tensor_tensor(
                        dst[:, :, half, :], src[:, :, 1 - half, :],
                        sn[:, half, :].unsqueeze(1).to_broadcast([P, 2 * H, DH // 2]), ALU.mult)
                last.then_inc(rot_s_ready, 1)

            def move_qT(b, r):
                bank, _ = s2_slot(b, U_QT[r])
                dve.wait_ge(s2_done, S2_USES * b + U_QT[r] + 1)
                src = s2_ps[bank][:, :].bitcast(F16).rearrange("p (a s) -> p a s", s=SEQ)
                nc.vector.tensor_copy(qT[:, 4 * r:4 * r + 4, :], src).then_inc(s2_moved[bank], 1)

            def move_odd_kT(b, o, r):
                bank, _ = s2_slot(b, U_KT[r])
                dve.wait_ge(s2_done, S2_USES * b + U_KT[r] + 1)
                src = s2_ps[bank][:, :].bitcast(F16).rearrange("p (a s) -> p a s", s=SEQ)
                dst = kT[o][:, 8 * r:8 * r + 8, :].rearrange("p (a two) s -> p a two s", two=2)
                nc.vector.tensor_copy(dst[64:128, :, 1, :], src[64:128]).then_inc(s2_moved[bank], 1)

            def maxima(b, first, count):
                for g in range(first, first + count):
                    t, pair = divmod(g, PAIRS)
                    bank, _ = s2_slot(b, U_SC[g])
                    dve.wait_ge(s2_done, S2_USES * b + U_SC[g] + 1)
                    nc.vector.reduce_max(mx[:, t, 2 * pair:2 * pair + 2],
                                         s2_ps[bank][:, :].rearrange("p (h s) -> p h s", h=2), AX.X).then_inc(s2_moved[bank], 1)

            def divide(b, half):
                dve.wait_ge(pv_done, GROUPS * b + 4 * half + 4)
                if half > 0:
                    dve.wait_ge(oT_ready, 2 * b + half)
                nc.vector.transpose(o_rows[:, :, :].rearrange("p c r -> p (c r)"), o_ps[:, :]).then_inc(o_moved, 1)
                dve.wait_ge(o_moved, 1 + O_USES * b + half + 1)
                nc.vector.reciprocal(rsums[:, :], o_rows[:, :, DH]).then_inc(rsums_ready, 1)
                dve.wait_ge(rsums_ready, 2 * b + half + 1)
                nc.vector.tensor_tensor(o_rows[:, :, 0:DH], o_rows[:, :, 0:DH],
                                        rsums[:, :].unsqueeze(2).to_broadcast([P, 2 * SEQ // 32, DH]),
                                        ALU.mult).then_inc(o_scaled, 1)
                dve.wait_ge(o_scaled, 2 * b + half + 1)
                nc.vector.transpose(oT[:, 2 * half:2 * half + 2, :].rearrange("p q s -> p (q s)"),
                                    o_rows[:, :, :].rearrange("p c r -> p (c r)")).then_inc(oT_ready, 1)

            def residual(b):
                dve.wait_ge(wo_done, b + 1)
                dve.wait_ge(xb_ready, b + 1)
                rows = seq_rows(b)
                nc.vector.tensor_tensor(rows, o_ps[:, :].rearrange("p (t d) -> p t d", t=T), rows,
                                        ALU.add).then_inc(o_moved, 1)

            def step(j, o, stages):
                def s2_max(first, count):
                    if stages[1]:
                        maxima(j + 1, first, count)

                if stages[1]:
                    move_odd_kT(j + 1, 1 - o, 1)
                s2_max(0, 2)
                if stages[0]:
                    add_bias(j + 2, 0)
                s2_max(2, 2)
                if stages[0]:
                    rotate_swapped(j + 2, 0)
                s2_max(4, 3)
                if stages[2]:
                    divide(j, 0)
                s2_max(7, 1)
                if stages[0]:
                    add_bias(j + 2, 1)
                s2_max(8, 1)
                if stages[0]:
                    rotate_swapped(j + 2, 1)
                s2_max(9, 5)
                if stages[2]:
                    divide(j, 1)
                s2_max(14, 2)
                if stages[0]:
                    statistics(j + 3)
                    move_qT(j + 2, 0)
                    normalise(j + 3)
                if stages[2]:
                    residual(j)
                if stages[0]:
                    move_qT(j + 2, 1)
                    move_odd_kT(j + 2, o, 0)

            for i in range(2):
                heads = kT[i][:, :, :].rearrange("p h s -> p (h s)").bitcast(F32).rearrange("p (a two s) -> p a two s", two=2, a=PAIRS)
                nc.vector.memset(heads[0:64, :, 1, :], 0.0).then_inc(keys_cleared, 1)
                nc.vector.memset(heads[64:128, :, 0, :], 0.0).then_inc(keys_cleared, 1)
            dve.sem_inc(o_moved, 1)
            dve.wait_ge(x0_loaded, 32)
            statistics(0)
            normalise(0)
            dve.wait_ge(wqkv_loaded, 64)
            dve.wait_ge(consts_set, 5)
            iterations(dve, step)

            dve.wait_ge(cross_loaded, CROSS_LOADS)
            dve.wait_ge(o_moved, 1 + O_USES * BATCH)

            def normalise_chunk(c, n, dst, normed):
                chunk = X[:, bass.ds(c * TC * D, TC * D)].rearrange("p (t d) -> p t d", t=TC)
                for t in range(TC):
                    nc.vector.bn_stats(stats[:, t, :], chunk[:, t, :]).then_inc(ln_stats, 1)
                for t in range(TC):
                    have = at(dve, XN0 + TC * n + t + 1)
                    dve.wait_ge(x0_loaded, 32)
                    dve.wait_ge(ln_stats, have)
                    nc.vector.bn_aggr(mv[:, t, :], stats[:, t, :]).then_inc(ln_mv, 1)
                dve.wait_ge(ln_rstd, BATCH + 1 + n + 1)
                for t in range(TC):
                    nc.vector.tensor_scalar(dst[:, t, :], chunk[:, t, :], mv[:, t, 0:1], rstd[:, t:t + 1],
                                            ALU.subtract, ALU.mult).then_inc(normed, 1)

            def choose(c):
                dve.wait_ge(logits_done, c + 1)
                nc.vector.tensor_tensor(lg[:, :, :], wc_ps[0][:, 0:TC * E].rearrange("p (t e) -> p t e", e=E),
                                        br_sb[:, :].unsqueeze(1).to_broadcast([P, TC, E]), ALU.add).then_inc(logits_moved, 1)
                dve.wait_ge(logits_moved, c + 1)
                for t in range(TC):
                    nc.vector.max(best_v[:, t, :], lg[:, t, :]).then_inc(best_found, 1)
                for t in range(TC):
                    have = at(dve, 2 * TC * c + t + 1)
                    dve.wait_ge(x0_loaded, 32)
                    dve.wait_ge(best_found, have)
                    nc.vector.max_index(best_e[:, t, :], best_v[:, t, :], lg[:, t, :]).then_inc(best_found, 1)
                have = at(dve, 2 * TC * c + 2 * TC)
                dve.wait_ge(x0_loaded, 32)
                dve.wait_ge(best_found, have)
                nc.vector.tensor_copy(top_v[:, :, bass.ds(c * TC, TC)],
                                      best_v[:, :, 0:TOP].rearrange("p t k -> p k t")).then_inc(best_kept, 1)
                nc.vector.tensor_copy(top_e[:, :, bass.ds(c * TC, TC)],
                                      best_e[:, :, 0:TOP].rearrange("p t k -> p k t")).then_inc(best_kept, 1)

            def cross_step(c, o, has_last, has_next):
                for m in range(KD):
                    dve.wait_ge(k_moved, KD * c + m + 1)
                    nc.vector.scalar_tensor_tensor(k_exp[:, m, :], k_exp[:, m, :], 1.0, relu[:, m, :],
                                                   ALU.min, ALU.add).then_inc(k_heads_ready, 1)
                if has_last:
                    summed = at(dve, 2 * c)
                    dve.wait_ge(x0_loaded, 32)
                    dve.wait_ge(wc_moved, summed)
                    normalise_chunk(c - 1, 2 * c, xn3, x3_normed)
                for m in range(KD):
                    dve.wait_ge(cum_done, KD * c + m + 1)
                    nc.vector.reciprocal(mix[:, m, :], cq_ps[m]).then_inc(cum_moved, 1)
                for m in range(KD):
                    dve.wait_ge(v_done, KD * c + m + 1)
                    dve.wait_ge(ratio_ready, KD * c + m + 1)
                    nc.vector.scalar_tensor_tensor(mix[:, m, :], kv_ps[m], bxv_sb[:, m:m + 1], mix[:, m, :],
                                                   ALU.add, ALU.mult).then_inc(v_moved, 1)
                for m in range(KD):
                    dve.wait_ge(q_moved, KD * c + m + 1)
                    nc.vector.scalar_tensor_tensor(q_exp[:, m, :], q_exp[:, m, :], 1.0, relu[:, m, :],
                                                   ALU.min, ALU.add).then_inc(q_heads_ready, 1)
                if has_next:
                    normalise_chunk(c + 1, 2 * c + 1, xn, xc_normed)
                if has_last:
                    choose(c - 1)
                dve.wait_ge(xc_ready, c + 1)
                chunk = X[:, bass.ds(c * TC * D, TC * D)].rearrange("p (t d) -> p t d", t=TC)
                for half in range(2):
                    dve.wait_ge(wc_done, 2 * c + half + 1)
                    part = chunk[:, 2 * half:2 * half + 2, :]
                    nc.vector.tensor_tensor(part, wc_ps[half].rearrange("p (t d) -> p t d", t=2), part,
                                            ALU.add).then_inc(wc_moved, 1)

            normalise_chunk(0, 0, xn, xc_normed)
            cross_steps(dve, cross_step)
            dve.wait_ge(wc_moved, 2 * NC)
            normalise_chunk(NC - 1, 2 * NC - 1, xn3, x3_normed)
            choose(NC - 1)

            dve.wait_ge(route_loaded, 32)
            dve.wait_ge(best_kept, 2 * NC)
            by_choice = [P, TOP, NT, E]
            nc.vector.tensor_tensor(v_gap[:, :], top_v[:, 1, :], top_v[:, 0, :], ALU.subtract).then_inc(gap_ready, 1)
            nc.vector.memset(oh_any[:, NT, :], 0.0).then_inc(choices_ready, 1)
            nc.vector.tensor_tensor(oh[:, :, :, :], top_e[:, :, :].unsqueeze(3).to_broadcast(by_choice),
                                    const("experts").unsqueeze(1).unsqueeze(1).to_broadcast(by_choice),
                                    ALU.is_equal).then_inc(routed, 1)
            dve.wait_ge(routed, 1)
            nc.vector.tensor_tensor(oh_any[:, 0:NT, :], oh[:, 0], oh[:, 1], ALU.add).then_inc(choices_ready, 1)
            dve.wait_ge(gap_exp, 1)
            nc.vector.tensor_scalar(v_sum[:, :], v_exp[:, :], 1.0, None, ALU.add).then_inc(routed, 1)
            dve.wait_ge(routed, 2)
            nc.vector.reciprocal(gates[:, 0, :], v_sum[:, :]).then_inc(routed, 1)
            dve.wait_ge(routed, 3)
            nc.vector.tensor_tensor(gates[:, 1, :], v_exp[:, :], gates[:, 0, :], ALU.mult).then_inc(routed, 1)
            dve.wait_ge(ranks_done, 1)
            floors = [P, E, TOKENS // P]
            nc.vector.tensor_tensor(above[:, :, :], rank_ps[:, NT, :].unsqueeze(2).to_broadcast(floors),
                                    const("block_floors").unsqueeze(1).to_broadcast(floors), ALU.is_gt).then_inc(routed, 1)
            dve.wait_ge(routed, 5)
            nc.vector.reduce_sum(expert_blocks[:, :], above[:, :, :], AX.X).then_inc(routed, 1)
            dve.wait_ge(routed, 6)
            nc.vector.tensor_tensor(bounds_of[:, :, :], const("before").rearrange("p (w e) -> p w e", e=E),
                                    expert_blocks[:, :].unsqueeze(1).to_broadcast([P, 2 * E, E]), ALU.mult).then_inc(routed, 1)
            dve.wait_ge(routed, 7)
            nc.vector.reduce_sum(bounds[:, :], bounds_of[:, :, :], AX.X).then_inc(routed, 1)
            dve.wait_ge(routed, 8)
            nc.vector.scalar_tensor_tensor(place_of[:, :, :], bounds[:, 0:E].unsqueeze(1).to_broadcast([P, NT, E]), float(P),
                                           rank_ps[:, 0:NT, :], ALU.mult, ALU.add).then_inc(routed, 1)
            dve.wait_ge(routed, 9)
            nc.vector.tensor_tensor(oh_place[:, :, :, :], oh[:, :, :, :], place_of[:, :, :].unsqueeze(1).to_broadcast(by_choice),
                                    ALU.mult).then_inc(routed, 1)
            dve.wait_ge(routed, 10)
            nc.vector.reduce_sum(place[:, :], oh_place[:, :, :, :].rearrange("p k t e -> p (k t) e"), AX.X).then_inc(routed, 1)
            dve.wait_ge(routed, 11)
            nc.vector.tensor_copy(place_i[:, :], place[:, :]).then_inc(routed, 1)
            dve.wait_ge(routed, 12)
            nc.vector.tensor_scalar(block_i[:, :], place_i[:, :], P.bit_length() - 1, None,
                                    ALU.logical_shift_right).then_inc(routed, 1)
            dve.wait_ge(routed, 13)
            nc.vector.tensor_copy(block_f[:, :], block_i[:, :]).then_inc(routed, 1)
            dve.wait_ge(routed, 14)
            nc.vector.scalar_tensor_tensor(pos[:, :], block_f[:, :], float(-P), place[:, :], ALU.mult, ALU.add).then_inc(routed, 1)
            by_block = [P, TOP * NT, NB]
            dve.wait_ge(x3_low, NC)
            dve.wait_ge(rows_stored, 16 * NC)
            nc.vector.tensor_tensor(table[:, :, 0, :], const("blocks")[:, 0:NB].unsqueeze(1).to_broadcast(by_block),
                                    block_f[:, :].unsqueeze(2).to_broadcast(by_block), ALU.is_equal).then_inc(routed, 1)
            dve.wait_ge(w_low, 4 * E)
            dve.wait_ge(routed, 16)

            def position_rows(q):
                j = slice(q * 8, q * 8 + 8)
                if q >= 2:
                    dve.wait_ge(pos_used, q - 1)
                nc.vector.tensor_tensor(pos_oh[q % 2], const("positions").unsqueeze(1).to_broadcast([P, 8, P]),
                                        pos[:, j].unsqueeze(2).to_broadcast([P, 8, P]), ALU.is_equal).then_inc(pos_ready, 1)

            position_rows(0)
            nc.vector.tensor_tensor(table[:, :, 1, :], table[:, :, 0, :],
                                    gates[:, :, :].rearrange("p k t -> p (k t)").unsqueeze(2).to_broadcast(by_block),
                                    ALU.mult).then_inc(routed, 1)
            dve.wait_ge(routed, 17)
            for k in range(TOP):
                tiles = table[:, k * NT:(k + 1) * NT, 0, :]
                nc.vector.tensor_tensor(tiles, tiles, const("tokens").unsqueeze(2).to_broadcast([P, NT, NB]),
                                        ALU.mult).then_inc(table_ready, 1)
            for q in range(1, TOP * NT // 8):
                position_rows(q)
            by_expert = [P, NB + 1, E]
            nc.vector.tensor_tensor(reached[:, :, :], const("blocks").unsqueeze(2).to_broadcast(by_expert),
                                    bounds[:, E:].unsqueeze(1).to_broadcast(by_expert), ALU.is_ge).then_inc(routed, 1)
            dve.wait_ge(routed, 18)
            nc.vector.reduce_sum(owner[:, :], reached[:, :, :], AX.X).then_inc(routed, 1)
            dve.wait_ge(routed, 19)
            nc.vector.tensor_scalar(owner[:, :], owner[:, :], float(E - 1), None, ALU.min).then_inc(routed, 1)
            dve.wait_ge(routed, 20)
            nc.vector.tensor_copy(block_expert[:, :], owner[:, :]).then_inc(experts_ready, 1)
            two_by_two = owner[:, :].rearrange("p (b two) -> p b two", two=2)
            nc.vector.scalar_tensor_tensor(expert_pairs[:, :], two_by_two[:, :, 1], float(E), two_by_two[:, :, 0],
                                           ALU.mult, ALU.add).then_inc(experts_ready, 1)
            dve.wait_ge(table_done, 1)
            nc.vector.tensor_scalar(spare_ids[:, :], table_ps[:, 0:NB], 0.0, const("spare_row"), ALU.is_ge,
                                    ALU.mult).then_inc(routed, 1)
            dve.wait_ge(routed, 21)
            nc.vector.scalar_tensor_tensor(block_rows[:, :], table_ps[:, 0:NB], float(2 * TOKENS), spare_ids[:, :],
                                           ALU.add, ALU.add).then_inc(ids_ready, 1)
            nc.vector.tensor_copy(block_gates[:, :], table_ps[:, NB:]).then_inc(ids_ready, 1)
            nc.vector.tensor_scalar(block_scales[:, :], table_ps[:, NB:], 1 / WSCALE, None, ALU.mult).then_inc(ids_ready, 1)

            dve.wait_ge(ids_ready, 3)
            dve.wait_ge(experts_ready, 2)
            dve.wait_ge(w_low, 4 * E)

            def copy_w1(i, o, e):
                done = at(dve, 2 * i - 2)
                if not isinstance(i, int) or i >= 2:
                    dve.wait_ge(x0_loaded, 32)
                    dve.wait_ge(first_done, done)
                nc.vector.tensor_copy(w1_now[o], W1[:, bass.ds(e, 1), :, :, :].rearrange("p e k h n -> p (e k) h n")
                                      ).then_inc(w1_copied, 1)

            def move_xgT(i, o):
                dve.wait_ge(xg_transposed, i + 1)
                nc.vector.tensor_copy(xgT[o][:, :, :, :], xgT_ps[o]).then_inc(xgT_moved, 1)

            def split_hidden(i, o, half):
                m = slice(half * KF // 2, (half + 1) * KF // 2)
                dve.wait_ge(gelu_done, KF * i + m.stop)
                nc.vector.tensor_copy(hid_hi[o][:, m, :], hid[o][:, m, :]).then_inc(hi_split, 1)
                dve.wait_ge(hi_split, 2 * i + half + 1)
                nc.vector.tensor_tensor(hid_lo[o][:, m, :], hid[o][:, m, :], hid_hi[o][:, m, :],
                                        ALU.subtract).then_inc(lo_split, 1)

            def gated_output(i, o):
                have, before = at(dve, i + 1), at(dve, 16 * i - 16)
                dve.wait_ge(x0_loaded, 32)
                dve.wait_ge(second_done, have)
                dve.wait_ge(gated_b2_ready, have)
                if not isinstance(i, int) or i >= 2:
                    dve.wait_ge(added, before)
                nc.vector.scalar_tensor_tensor(y[o][:, :], y_ps[o], block_scales[:, bass.ds(i, 1)], gated_b2[o][:, :],
                                               ALU.mult, ALU.add).then_inc(y_ready, 1)

            def block_step(two, o, ahead, e):
                i = 2 * two + o
                if ahead >= 2:
                    copy_w1(i + 2, o, e)
                if ahead >= 1:
                    split_hidden(i + 1, 1 - o, 0)
                if ahead >= 2:
                    move_xgT(i + 2, o)
                if ahead >= 1:
                    split_hidden(i + 1, 1 - o, 1)
                gated_output(i, o)

            dve.wait_ge(x_stored, 16 * NC)
            for i, e in enumerate(expert_pair(dve, 0)):
                copy_w1(i, i, e)
            move_xgT(0, 0)
            move_xgT(1, 1)
            split_hidden(0, 0, 0)
            split_hidden(0, 0, 1)
            blocks_in_turn(dve, block_step, experts_of=2)

        @block.tensor
        def _(pe):
            def s1_free(b, u):
                pe.wait_ge(s1_moved, S1_USES * b + u)

            def s2_free(b, u):
                bank, n = s2_slot(b, u)
                pe.wait_ge(s2_moved[bank], n)
                return bank

            def s2_arrived(b, u):
                bank, n = s2_slot(b, u)
                pe.wait_ge(s2_moved[bank], n + 1)

            def transpose_xn(b):
                pe.wait_ge(xn_ready, T * b + T)
                s1_free(b, U_XNT)
                for k in range(KD):
                    for t in range(T):
                        last = nc.tensor.transpose(s1_ps[:, k * SEQ + t * P:k * SEQ + (t + 1) * P],
                                                   xn[:, t, k * P:(k + 1) * P], id_sb[:, :])
                last.then_inc(s1_done, 1)

            def project(b, u, t, lo, n):
                pe.wait_ge(wqkv_loaded, 64)
                s1_free(b, u)
                for k in range(KD):
                    last = nc.tensor.matmul(s1_ps[:, 0:n], xnT[:, k, t * P:(t + 1) * P],
                                            wqkv_sb[:, k, lo:lo + n], start=(k == 0), stop=(k == KD - 1))
                last.then_inc(s1_done, 1)

            def transpose_stack(b, stack, u, r):
                bank = s2_free(b, u)
                dst = s2_ps[bank][:, :].bitcast(F16).rearrange("p (a s) -> p a s", s=SEQ)
                for a in range(4):
                    for t in range(T):
                        pair = 4 * r + a
                        last = nc.tensor.transpose(
                            dst[:, a, t * P:(t + 1) * P],
                            stack[:, t, 2 * pair:2 * pair + 2, :].rearrange("p h r -> p (h r)"), id16[:, :])
                last.then_inc(s2_done, 1)

            def transpose_shifted(b, o, t):
                pe.wait_ge(negm_ready, T * b + t + 1)
                bank = s2_free(b, U_RT[t])
                dst = s2_ps[bank][:, :].bitcast(F16).rearrange("p (a s) -> p a s", s=P)
                for pair in range(PAIRS):
                    last = nc.tensor.transpose(
                        dst[:, pair, :], q_stack[o][:, t, 2 * pair:2 * pair + 2, :].rearrange("p h r -> p (h r)"), id16[:, :])
                last.then_inc(s2_done, 1)

            def row_scores(b, o, first, count):
                for g in range(first, first + count):
                    t, pair = divmod(g, PAIRS)
                    if g in (0, PAIRS // 2):
                        s2_arrived(b, U_QT[g // (PAIRS // 2)])
                        s2_arrived(b, U_KT[g // (PAIRS // 2)])
                    bank = s2_free(b, U_SC[g])
                    if g < 2:
                        pe.wait_ge(even_kT_moved, 2 * b + g + 1)
                    for h in range(2):
                        last = nc.tensor.matmul(s2_ps[bank][:, h * SEQ:(h + 1) * SEQ], qT[:, pair, t * P:(t + 1) * P],
                                                kT[o][:, 2 * pair + h, :], start=True, stop=True)
                    last.then_inc(s2_done, 1)

            def key_scores(b, o, g):
                quad, kt = divmod(g, T)
                if g == 0:
                    for u in U_RT:
                        s2_arrived(b, u)
                if g >= 2:
                    pe.wait_ge(exp_done, GROUPS * b + g - 1)
                for n in range(4):
                    h = 4 * quad + n
                    last = nc.tensor.matmul(s_ps[g % 2][:, n, :], kT[o][:, h, kt * P:(kt + 1) * P],
                                            qmT[o][:, h // 2, :], start=True, stop=True)
                last.then_inc(scores_ready, 1)

            def weigh_values(b, o, g):
                quad, kt = divmod(g, T)
                col = (quad % 2) * SEQ
                if g == 0:
                    pe.wait_ge(v_ready, b + 1)
                if g % 4 == 0:
                    pe.wait_ge(o_moved, 1 + O_USES * b + quad // 2)
                pe.wait_ge(exp_done, GROUPS * b + g + 1)
                for n in range(4):
                    last = nc.tensor.matmul(o_ps[32 * n:32 * n + 32, col:col + SEQ], v1[o][:, kt, 4 * quad + n, :],
                                            probs[g % 2][:, n, :], start=(kt == 0), stop=(kt == T - 1))
                last.then_inc(pv_done, 1)

            def project_out(b, t):
                if t == 0:
                    pe.wait_ge(wo_loaded, 32)
                    pe.wait_ge(oT_ready, 2 * b + 2)
                    pe.wait_ge(o_moved, 1 + O_USES * b + U_WO)
                for quad in range(QUADS):
                    last = nc.tensor.matmul(o_ps[:, t * D:(t + 1) * D], oT[:, quad, t * P:(t + 1) * P],
                                            wo_sb[:, quad, :], start=(quad == 0), stop=(quad == QUADS - 1))
                if t == T - 1:
                    last.then_inc(wo_done, 1)

            def step(j, o, stages):
                s1, s2, s3 = stages

                def probabilities(g):
                    if s3:
                        weigh_values(j, o, g)
                        if g + 2 < GROUPS:
                            key_scores(j, o, g + 2)

                def s2_scores(first, count):
                    if s2:
                        row_scores(j + 1, 1 - o, first, count)

                if s1:
                    transpose_xn(j + 2)
                if s3:
                    key_scores(j, o, 0)
                if s2:
                    transpose_stack(j + 1, k_stack[1 - o], U_KT[1], 1)
                if s3:
                    key_scores(j, o, 1)
                s2_scores(0, 2)
                if s1:
                    project(j + 2, U_QK[0], 0, 0, 2 * D)
                probabilities(0)
                s2_scores(2, 2)
                probabilities(1)
                s2_scores(4, 2)
                probabilities(2)
                s2_scores(6, 1)
                probabilities(3)
                s2_scores(7, 1)
                if s1:
                    project(j + 2, U_QK[1], 1, 0, 2 * D)
                s2_scores(8, 1)
                probabilities(4)
                s2_scores(9, 2)
                probabilities(5)
                s2_scores(11, 2)
                probabilities(6)
                s2_scores(13, 1)
                probabilities(7)
                if s2:
                    transpose_shifted(j + 1, 1 - o, 0)
                if s1:
                    project(j + 2, U_V[0], 0, 2 * D, D)
                    project(j + 2, U_V[1], 1, 2 * D, D)
                s2_scores(14, 2)
                if s3:
                    project_out(j, 0)
                if s2:
                    transpose_shifted(j + 1, 1 - o, 1)
                if s1:
                    pe.wait_ge(lo_ready, 3 * T * (j + 2) + 3 * T)
                    transpose_stack(j + 2, q_stack[o], U_QT[0], 0)
                if s3:
                    project_out(j, 1)
                if s1:
                    transpose_stack(j + 2, q_stack[o], U_QT[1], 1)
                    transpose_stack(j + 2, k_stack[o], U_KT[0], 0)

            pe.wait_ge(keys_cleared, 4)
            pe.wait_ge(x0_loaded, 32)
            pe.wait_ge(id16_ready, 1)
            iterations(pe, step)

            pe.wait_ge(cross_loaded, CROSS_LOADS)
            pe.wait_ge(o_moved, 1 + O_USES * BATCH)
            pe.wait_ge(exp_done, GROUPS * BATCH)
            for bank in range(2):
                pe.wait_ge(s2_moved[bank], S2_USES // 2 * BATCH)

            def transpose_rows(src, dst, done):
                for k in range(KD):
                    for t in range(TC):
                        last = nc.tensor.transpose(dst[k][:, t * P:(t + 1) * P], src[:, t, k * P:(k + 1) * P], id_sb[:, :])
                    last.then_inc(done, 1)

            def project_features(dst, m, w, rhs):
                for k in range(KD):
                    last = nc.tensor.matmul(dst, w[:, k, m * P:(m + 1) * P], rhs[:, k, :], start=(k == 0), stop=(k == KD - 1))
                return last

            def project_keys(c, o):
                pe.wait_ge(ctx_loaded, 16 * c + 16)
                for m in range(KD):
                    if not isinstance(c, int) or c > 0:
                        pe.wait_ge(v_moved, KD * c - KD + m + 1)
                    project_features(kv_ps[m], m, wxk_sb, ctx_sb[o]).then_inc(k_done, 1)

            def route(c):
                pe.wait_ge(x3_normed, TC * c + TC)
                transpose_rows(xn3, xT_ps, x3T_done)
                pe.wait_ge(x3T_moved, KD * c + KD)
                pe.wait_ge(wc_moved, 2 * c + 2)
                for t in range(TC):
                    for k in range(KD):
                        last = nc.tensor.matmul(wc_ps[0][:, t * E:(t + 1) * E], xT[:, k, t * P:(t + 1) * P],
                                                wr_sb[:, k, :], start=(k == 0), stop=(k == KD - 1))
                last.then_inc(logits_done, 1)

            def cross_step(c, o, has_last, has_next):
                pe.wait_ge(xc_normed, TC * c + TC)
                transpose_rows(xn, xT_ps, xnT_done)
                for m in range(KD):
                    pe.wait_ge(k_heads_ready, KD * c + m + 1)
                    if has_last:
                        pe.wait_ge(q_moved, KD * c - KD + m + 1)
                    for k in range(m + 1):
                        last = nc.tensor.matmul(cq_ps[m], cum_sb[:, k, m * P:(m + 1) * P], k_exp[:, k, :],
                                                start=(k == 0), stop=(k == m))
                    last.then_inc(cum_done, 1)
                for m in range(KD):
                    pe.wait_ge(k_moved, KD * c + m + 1)
                    project_features(kv_ps[m], m, wxv_sb, ctx_sb[o]).then_inc(v_done, 1)
                pe.wait_ge(xnT_moved, KD * c + KD)
                for m in range(KD):
                    pe.wait_ge(cum_moved, KD * c + m + 1)
                    project_features(cq_ps[m], m, wxq_sb, xT).then_inc(q_done, 1)
                if has_last:
                    route(c - 1)
                if has_next:
                    project_keys(c + 1, 1 - o)
                pe.wait_ge(mixed_ready, KD * c + KD)
                for half in range(2):
                    if has_last:
                        pe.wait_ge(logits_moved, c)
                        pe.wait_ge(wc_moved, 2 * c)
                    for t in range(2 * half, 2 * half + 2):
                        for k in range(KD):
                            last = nc.tensor.matmul(wc_ps[half][:, (t % 2) * D:(t % 2 + 1) * D], mix[:, k, t * P:(t + 1) * P],
                                                    wxc_sb[:, k, :], start=(k == 0), stop=(k == KD - 1))
                    last.then_inc(wc_done, 1)

            project_keys(0, 0)
            cross_steps(pe, cross_step)
            route(NC - 1)

            pe.wait_ge(route_loaded, 32)
            pe.wait_ge(choices_ready, 2)
            any_flat = oh_any[:, :, :].rearrange("p t e -> p (t e)")
            rank_flat = s2_ps[0][:, 0:(NT + 1) * E]
            nc.tensor.matmul(rank_flat, rank_sb[:, 0:P], any_flat, start=True, stop=False)
            for t in range(1, NT + 1):
                last = nc.tensor.matmul(rank_flat[:, t * E:], rank_sb[:, P:], any_flat[:, 0:(NT + 1 - t) * E],
                                        start=False, stop=(t == NT))
            last.then_inc(ranks_done, 1)
            pe.wait_ge(routed, 17)
            pe.wait_ge(table_ready, TOP)
            for j in range(TOP * NT):
                if j % 8 == 0:
                    pe.wait_ge(pos_ready, j // 8 + 1)
                last = nc.tensor.matmul(table_ps, pos_oh[j // 8 % 2][:, j % 8, :], table[:, j, :, :].rearrange("p w b -> p (w b)"),
                                        start=(j == 0), stop=(j == TOP * NT - 1))
                if j % 8 == 7 and j < TOP * NT - 1:
                    last.then_inc(pos_used, 1)
            last.then_inc(table_done, 1)

            pe.wait_ge(w_low, 4 * E)
            pe.wait_ge(experts_ready, 2)
            PASSES = ((0, 0), (0, 1), (1, 0))

            def transpose_block(two, o):
                i = 2 * two + o
                pe.wait_ge(gathered[o], 16 * two + 16)
                if not isinstance(i, int) or i >= 2:
                    pe.wait_ge(xgT_moved, i - 1)
                elif i == 0:
                    pe.wait_ge(ids_ready, 3)
                for h in range(2):
                    for k in range(KD):
                        last = nc.tensor.transpose(xgT_ps[o][:, h, k, :], xg[o][:, (h * KD + k) * P:(h * KD + k + 1) * P], id16[:, :])
                last.then_inc(xg_transposed, 1)

            def first_layer(i, o):
                pe.wait_ge(xgT_moved, i + 1)
                pe.wait_ge(w1_copied, i + 1)
                if not isinstance(i, int) or i >= 2:
                    pe.wait_ge(gelu_done, KF * (i - 1))
                for m in range(KF):
                    for n, (wp, xp) in enumerate(PASSES):
                        for k in range(KD):
                            last = nc.tensor.matmul(hid_ps[o][:, m, :], w1_now[o][:, k, wp, m * P:(m + 1) * P], xgT[o][:, xp, k, :],
                                                    start=(n + k == 0), stop=(n == 2 and k == KD - 1))
                    if m % (KF // 2) == KF // 2 - 1:
                        last.then_inc(first_done, 1)

            def second_layer(i, o, e):
                w = W2[:, bass.ds(e, 1), :, :, :]
                if not isinstance(i, int) or i >= 2:
                    pe.wait_ge(y_ready, i - 1)
                for k in range(KF):
                    if k % (KF // 2) == 0:
                        pe.wait_ge(lo_split, 2 * i + k // (KF // 2) + 1)
                    for n, (wp, hp) in enumerate(PASSES):
                        last = nc.tensor.matmul(y_ps[o], (hid_hi, hid_lo)[hp][o][:, k, :], w[:, 0, k, wp, :],
                                                start=(k + n == 0), stop=(n == 2 and k == KF - 1))
                last.then_inc(second_done, 1)

            def block_step(two, o, ahead, e):
                i = 2 * two + o
                if ahead >= 1:
                    first_layer(i + 1, 1 - o)
                if ahead >= 2:
                    transpose_block(two + 1, o)
                second_layer(i, o, e)

            transpose_block(0, 0)
            transpose_block(0, 1)
            first_layer(0, 0)
            blocks_in_turn(pe, block_step, experts_of=0)


def head_halves():
    return np.concatenate([h * DH + np.concatenate([np.arange(0, DH, 2), np.arange(1, DH, 2)]) for h in range(H)])


def quad_rows(w):
    padded = np.zeros((H, 32, w.shape[1]), w.dtype)
    padded[:, :DH] = w.reshape(H, DH, -1)
    return padded.reshape(H * 32, -1)


def kernel(**inputs):
    import concourse.bacc as bacc
    from concourse.bass_utils import run_bass_kernel_spmd

    a = {k: np.asarray(v) for k, v in inputs.items()}
    halves = head_halves()
    cos, sin = rope_tables()
    laid = {
        "x": a["x"].reshape(BATCH * SEQ, D),
        "ctxT": a["ctx_1024"].reshape(BATCH * SEQ, D).T,
        "w_qkv": np.concatenate([a["L0_attn_Wq"].T[:, halves], a["L0_attn_Wk"].T[:, halves], a["L0_attn_Wv"].T], 1),
        "b_qkv": np.concatenate([a["L0_attn_bq"][halves], a["L0_attn_bk"][halves], a["L0_attn_bv"]]),
        "w_o": quad_rows(a["L0_attn_Wo"].T),
        "b_o": a["L0_attn_bo"],
        "wx_q": a["L0_xattn_wq_w"], "wx_k": a["L0_xattn_wk_w"], "wx_v": a["L0_xattn_wv_w"], "wx_c": a["L0_xattn_wc_w"],
        "bx_q": a["L0_xattn_wq_b"], "bx_k": a["L0_xattn_wk_b"], "bx_v": a["L0_xattn_wv_b"], "bx_c": a["L0_xattn_wc_b"],
        "wr": a["L0_ffn_Wr"], "br": a["L0_ffn_br"], "w1": a["L0_ffn_W1"], "b1": a["L0_ffn_b1"].reshape(-1),
        "w2": a["L0_ffn_W2"], "b2": a["L0_ffn_b2"],
        "rank_m": rank_matrices(), "route_c": np.concatenate(list(routing_constants().values()), 1),
        "cos": cos, "sin": sin, "cumsum_m": head_cumsum_matrix(), "ident": np.eye(P, dtype=np.float32),
    }
    nc = bacc.Bacc("TRN2", target_bir_lowering=False, num_devices=1)
    arrays, args = {}, {}
    for name, value in laid.items():
        value = np.ascontiguousarray(value)
        arrays[f"in_{name}"] = value
        args[name] = nc.dram_tensor(f"in_{name}", value.shape, mybir.dt.from_np(value.dtype), kind="ExternalInput").ap()
    rows = nc.dram_tensor("rows", (ROWS, 2 * D), F16, kind="Internal").ap()
    out = nc.dram_tensor("out_0", (ROWS, D), F32, kind="ExternalOutput").ap()
    build(nc, rows=rows, out=out, **args)
    got = run_bass_kernel_spmd(nc, [arrays], core_ids=[0]).results[0]["out_0"]
    return got[:TOKENS].reshape(BATCH, SEQ, D)
```

```python
from contextlib import ExitStack

import numpy as np

import concourse.bass as bass
from concourse import mybir

F32 = mybir.dt.float32
F16 = mybir.dt.float16
I32 = mybir.dt.int32
U32 = mybir.dt.uint32
ALU = mybir.AluOpType
ACT = mybir.ActivationFunctionType
AX = mybir.AxisListType

P = 128
BATCH, SEQ, D = 8, 256, 256
H, DH = 16, 16
KD = D // P
T = SEQ // P
NT = BATCH * T
PAIRS = H // 2
QUADS = H // 4
STACK = 64
E, TOP, DFF = 8, 2, 1024
KF = DFF // P
WSCALE = 256.0
GSCALE = 4096.0
TOKENS = BATCH * SEQ
NB = (TOKENS * TOP) // P + E - 1
ROWS = TOKENS + P
EPS = 1e-5
SCALE = float(DH) ** -0.5
THETA = 10000.0

ROW_MAX = 32

U_XNT, U_QK, U_V, S1_USES = 0, (1, 2), (3, 4), 5
U_QT, U_KT, U_RT, S2_USES = (0, 1), (2, 3), (18, 21), 22
U_SC = [u for u in range(4, S2_USES) if u not in U_RT]
U_WO, O_USES = 2, 3
LN_SETS = 3
GROUPS = QUADS * T


def rope_tables():
    freqs = np.arange(DH // 2, dtype=np.float32) * np.float32(1.0 / THETA)
    angles = np.arange(SEQ, dtype=np.float32)[:, None] * freqs[None, :]
    cos, sin = np.cos(angles), np.sin(angles)
    return (np.concatenate([cos, cos], 1).astype(np.float32),
            np.concatenate([-sin, sin], 1).astype(np.float32))


def head_cumsum_matrix():
    f = np.arange(D)
    same = (f[:, None] % DH) == (f[None, :] % DH)
    return (same & (f[:, None] // DH <= f[None, :] // DH)).astype(np.float32)


def routing_constants():
    e, p = np.arange(E), np.arange(P)[:, None]
    before = np.concatenate([e[None, :] < e[:, None], e[None, :] <= e[:, None]])
    columns = {
        "experts": e, "positions": np.arange(P), "blocks": np.arange(NB + 1), "block_floors": P * np.arange(TOKENS // P),
        "before": before.reshape(-1),
        "tokens": P * np.arange(NT)[None, :] + p - TOKENS,
        "spare_row": p,
    }
    return {k: np.broadcast_to(v, (P, v.shape[-1])).astype(np.float32) for k, v in columns.items()}


def routing_columns():
    widths = {k: v.shape[1] for k, v in routing_constants().items()}
    starts = np.cumsum([0, *widths.values()]).tolist()
    return starts[-1], {k: (at, n) for (k, n), at in zip(widths.items(), starts)}


def rank_matrices():
    p = np.arange(P)
    return np.concatenate([p[:, None] < p[None, :], np.ones((P, P), bool)], 1).astype(np.float16)


def build(nc, x, ctxT, w_qkv, b_qkv, w_o, b_o, wx_q, wx_k, wx_v, wx_c, bx_q, bx_k, bx_v, bx_c,
          wr, br, w1, b1, w2, b2, cos, sin, cumsum_m, ident, rank_m, route_c, spare_x, spare_rows, rows, out):
    with ExitStack() as ctx:
        scope = ctx

        def sb(name, shape, dt=F32):
            return scope.enter_context(nc.sbuf_tensor(name, shape, dt))

        def sem(name):
            return ctx.enter_context(nc.semaphore(name))

        X = sb("X", [P, NT * D])
        wxq_sb = sb("wxq_sb", [P, KD, D])
        wxkv_sb = sb("wxkv_sb", [P, 2, KD, D])
        wxc_sb = sb("wxc_sb", [P, KD, D])
        bxq_sb = sb("bxq_sb", [P, KD])
        bxk_sb = sb("bxk_sb", [P, KD])
        bxv_sb = sb("bxv_sb", [P, KD])
        bxc_sb = sb("bxc_sb", [P, D])
        cum_sb = sb("cum_sb", [P, KD, D])
        wr_sb = sb("wr_sb", [P, KD, E])
        br_sb = sb("br_sb", [P, E])
        b1_sb = sb("b1_sb", [P, E * KF])
        gelu_table = sb("gelu_table", [P, 1])
        id_sb = sb("id_sb", [P, P])
        id16 = sb("id16", [P, P], F16)
        stats = sb("stats", [P, 4, 6])
        mv = sb("mv", [P, LN_SETS * 4, 2])
        var_eps = sb("var_eps", [P, 4])
        minus_half = sb("minus_half", [P, 4])
        guess = sb("guess", [P, 4])
        newton = sb("newton", [P, 3, 4])
        rstd = sb("rstd", [P, LN_SETS * 4])
        top_v = sb("top_v", [P, TOP, NT])
        top_e = sb("top_e", [P, TOP, NT])
        W1 = sb("W1", [P, E, KD, 2, DFF], F16)
        staged = [sb(f"staged{i}", [P, DFF]) for i in range(2)]

        XC = 4 * P
        NC = TOKENS // XC
        TC = XC // P
        PIECES = [*((c * TC, TC) for c in range(NC - 1)), *((NT - n * T, T) for n in (2, 1))]
        NP = len(PIECES)
        below = ctx.enter_context(ExitStack())
        scope = below
        kv = sb("kv", [P, NC, KD, XC])
        weights_in = [*staged, *(kv[:, c].rearrange("p k s -> p (k s)") for c in range(2))]
        attention = ctx.enter_context(ExitStack())
        scope = attention
        xn = sb("xn", [P, T, D])
        xnT = sb("xnT", [P, KD, SEQ])
        qk = sb("qk", [P, T, 2 * D])
        rot_c = sb("rot_c", [P, T, 2 * D])
        rot_s = sb("rot_s", [P, T, 2 * D])
        roped = rot_c
        wqkv_sb = sb("wqkv_sb", [P, KD, 3 * D])
        bqkv_sb = sb("bqkv_sb", [P, 3 * D])
        v_raw = sb("v_raw", [P, T, D])
        k_stack = sb("k_stack", [P, T, H, STACK], F16)
        cos_sb = sb("cos_sb", [P, T, DH])
        sin_sb = sb("sin_sb", [P, T, DH])
        q_stack = [sb(f"q_stack{i}", [P, T, H, STACK], F16) for i in range(2)]
        qT = sb("qT", [P, PAIRS, SEQ], F16)
        mx = sb("mx", [P, T, H])
        wo_sb = sb("wo_sb", [P, QUADS, D])
        bo_sb = sb("bo_sb", [P, D])
        qmT = sb("qmT", [P, PAIRS, SEQ], F16)
        kT = [sb(f"kT{i}", [P, H, SEQ], F16) for i in range(2)]
        v1 = [sb(f"v1{i}", [P, T, H, 2 * DH]) for i in range(2)]
        probs = [sb(f"probs{i}", [P, 4, SEQ]) for i in range(2)]
        o_rows = sb("o_rows", [P, 2 * SEQ // 32, 32])
        rsums = sb("rsums", [P, 2 * SEQ // 32])
        oT = sb("oT", [P, QUADS, SEQ])
        attention.close()

        early = W1[:, E // 2:, :, :, :].rearrange("p e k h n -> p (e k h n)").bitcast(F32).rearrange(
            "p (b k s) -> p b k s", k=KD, s=XC)
        ctx_sb = [early[:, c] for c in range(NC)]
        k_exp = [early[:, NC + i] for i in range(2)]
        k_relu = [early[:, NC + 2 + i] for i in range(2)]
        x3T = wxkv_sb[:, :, :, :].rearrange("p w k n -> p (w k n)").rearrange("p (k s) -> p k s", s=XC)

        cross = ctx.enter_context(ExitStack())
        scope = cross
        xn2 = sb("xn2", [P, TC, D])
        xT = sb("xT", [P, KD, XC])
        q_exp = sb("q_exp", [P, KD, XC])
        q_relu = sb("q_relu", [P, KD, XC])
        xn3 = sb("xn3", [P, TC, D])
        xs = sb("xs", [P, TC, 2 * D], F16)
        lg = sb("lg", [P, TC, E])
        best_v = sb("best_v", [P, TC, 8])
        best_e = sb("best_e", [P, TC, 8], U32)
        cross.close()
        below.close()

        late = ctx.enter_context(ExitStack())
        scope = late
        RC, RC_AT = routing_columns()
        b2_sb = sb("b2_sb", [P, E, D])
        route_sb = sb("route_sb", [P, RC])
        rank_sb = sb("rank_sb", [P, 2 * P], F16)
        xg = [sb(f"xg{i}", [P, 2 * D], F16) for i in range(2)]
        xgT = [sb(f"xgT{i}", [P, 2, KD, P], F16) for i in range(2)]
        gates = sb("gates", [P, TOP, NT])
        block_gates = sb("block_gates", [P, NB])
        block_scales = sb("block_scales", [P, NB])
        block_rows = sb("block_rows", [P, NB], I32)
        block_expert = sb("block_expert", [P, NB + 1], I32)
        expert_pairs = sb("expert_pairs", [P, (NB + 1) // 2], I32)
        gather_ids = [sb(f"gather_ids{i}", [P, 1], I32) for i in range(2)]
        add_ids = [sb(f"add_ids{i}", [P, 1], I32) for i in range(2)]
        routing = ctx.enter_context(ExitStack())
        scope = routing
        oh = sb("oh", [P, TOP, NT, E])
        oh_any = sb("oh_any", [P, NT + 1, E], F16)
        v_gap = sb("v_gap", [P, NT])
        v_exp = sb("v_exp", [P, NT])
        v_sum = sb("v_sum", [P, NT])
        above = sb("above", [P, E, TOKENS // P])
        expert_blocks = sb("expert_blocks", [P, E])
        bounds_of = sb("bounds_of", [P, 2 * E, E])
        bounds = sb("bounds", [P, 2 * E])
        place_of = sb("place_of", [P, NT, E])
        oh_place = sb("oh_place", [P, TOP, NT, E])
        place = sb("place", [P, TOP * NT])
        place_i = sb("place_i", [P, TOP * NT], I32)
        block_i = sb("block_i", [P, TOP * NT], I32)
        block_f = sb("block_f", [P, TOP * NT])
        pos = sb("pos", [P, TOP * NT])
        gate_parts = sb("gate_parts", [P, 2, TOP * NT], F16)
        table = sb("table", [P, TOP * NT, 3, NB], F16)
        reached = sb("reached", [P, NB + 1, E])
        owner = sb("owner", [P, NB + 1])
        spare_ids = sb("spare_ids", [P, NB])
        pos_oh = [X[:, i * 4 * P:(i + 1) * 4 * P].bitcast(F16).rearrange("p (j q) -> p j q", q=P) for i in range(TOP * NT // 8)]
        routing.close()
        scope = late
        hid = [sb(f"hid{i}", [P, KF, P]) for i in range(2)]
        hid_hi = [sb(f"hid_hi{i}", [P, KF, P], F16) for i in range(2)]
        hid_lo = [sb(f"hid_lo{i}", [P, KF, P], F16) for i in range(2)]
        gated_b2 = [sb(f"gated_b2{i}", [P, D]) for i in range(2)]
        y = [sb(f"y{i}", [P, D]) for i in range(2)]
        late.close()
        scope = ctx
        sb("before_w2", [P, (NC + 3) * KD * XC + 3 * TC * D + TC * (E + 2 * 8)])
        W2 = sb("W2", [P, E, KF, 2, D], F16)
        w1_now = [X[:, i * KD * DFF:(i + 1) * KD * DFF].bitcast(F16).rearrange("p (k h n) -> p k h n", k=KD, h=2) for i in range(2)]

        def const(name):
            at_, n = RC_AT[name]
            return route_sb[:, at_:at_ + n]

        s1_ps = ctx.enter_context(nc.psum_tensor("s1_ps", [P, 512], F32))
        s2_ps = [ctx.enter_context(nc.psum_tensor(f"s2_ps{i}", [P, 512], F32)) for i in range(2)]
        o_ps = ctx.enter_context(nc.psum_tensor("o_ps", [P, 512], F32))
        s_ps = [ctx.enter_context(nc.psum_tensor(f"s_ps{i}", [P, 4, SEQ], F32)) for i in range(2)]
        s_halves = [s_ps[i][:, 2 * j:2 * j + 2, :].rearrange("p h s -> p (h s)") for i in range(2) for j in range(2)]
        key_ps = [s_halves[0:2], s_halves[2:4]]
        x_ps = [s1_ps[:, :], s2_ps[0][:, :], s2_ps[1][:, :], *s_halves]
        rank_ps = s2_ps[0][:, 0:(NT + 1) * E].rearrange("p (t e) -> p t e", e=E)
        table_ps = s2_ps[1][:, 0:3 * NB]
        xgT_ps = [bank[:, 0:D].bitcast(F16).rearrange("p (h k s) -> p h k s", h=2, k=KD) for bank in (s1_ps, o_ps)]
        hid_ps = [s_ps[i][:, :, :].rearrange("p h s -> p (h s)").rearrange("p (m s) -> p m s", s=P) for i in range(2)]
        y_ps = [bank[:, 0:D] for bank in s2_ps]

        x0_loaded = sem("x0_loaded")
        x_loaded = sem("x_loaded")
        wqkv_loaded = sem("wqkv_loaded")
        wo_loaded = sem("wo_loaded")
        cross_loaded = sem("cross_loaded")
        stacks_cleared = sem("stacks_cleared")
        consts_set = sem("consts_set")
        half_set = sem("half_set")
        keys_cleared = sem("keys_cleared")
        id16_ready = sem("id16_ready")
        ln_stats = sem("ln_stats")
        ln_mv = sem("ln_mv")
        var_ready = sem("var_ready")
        guess_ready = sem("guess_ready")
        newton_step = sem("newton_step")
        ln_rstd = sem("ln_rstd")
        xn_ready = sem("xn_ready")
        s1_done = sem("s1_done")
        s1_moved = sem("s1_moved")
        v_ready = sem("v_ready")
        s2_done = sem("s2_done")
        s2_moved = [sem(f"s2_moved{i}") for i in range(2)]
        rot_c_ready = sem("rot_c_ready")
        rot_s_ready = sem("rot_s_ready")
        roped_ready = sem("roped_ready")
        hi_ready = sem("hi_ready")
        lo_ready = sem("lo_ready")
        even_kT_moved = sem("even_kT_moved")
        negm_ready = sem("negm_ready")
        xb_ready = sem("xb_ready")
        scores_ready = sem("scores_ready")
        exp_done = sem("exp_done")
        pv_done = sem("pv_done")
        o_scaled = sem("o_scaled")
        oT_ready = sem("oT_ready")
        rsums_ready = sem("rsums_ready")
        o_moved = sem("o_moved")
        wo_done = sem("wo_done")
        k_done = sem("k_done")
        k_moved = sem("k_moved")
        cum_done = sem("cum_done")
        cum_moved = sem("cum_moved")
        v_done = sem("v_done")
        v_moved = sem("v_moved")
        x_done = sem("x_done")
        x_moved = [sem(f"x_moved{i}") for i in range(len(x_ps))]
        keys_loaded = sem("keys_loaded")
        ctx_loaded = [sem(f"ctx_loaded{i}") for i in range(NC)]
        xc_ready = sem("xc_ready")
        xc_normed = sem("xc_normed")
        x3_normed = sem("x3_normed")
        k_heads_ready = sem("k_heads_ready")
        ratio_ready = sem("ratio_ready")
        q_heads_ready = sem("q_heads_ready")
        mixed_ready = sem("mixed_ready")
        x3_high = sem("x3_high")
        x3_low = sem("x3_low")
        rows_stored = sem("rows_stored")
        x_stored = sem("x_stored")
        spare_stored = sem("spare_stored")
        best_found = sem("best_found")
        best_kept = sem("best_kept")
        route_loaded = sem("route_loaded")
        b2_loaded = sem("b2_loaded")
        gap_ready = sem("gap_ready")
        gap_exp = sem("gap_exp")
        choices_ready = sem("choices_ready")
        ranks_done = sem("ranks_done")
        routed = sem("routed")
        gates_split = sem("gates_split")
        table_ready = sem("table_ready")
        high_gates = sem("high_gates")
        pos_ready = sem("pos_ready")
        table_done = sem("table_done")
        experts_ready = sem("experts_ready")
        ids_ready = sem("ids_ready")
        ids_copied = sem("ids_copied")
        xg_transposed = [sem(f"xg_transposed{i}") for i in range(2)]
        first_xg_transposed = sem("first_xg_transposed")
        xgT_moved = sem("xgT_moved")
        first_done = sem("first_done")
        gelu_done = sem("gelu_done")
        hi_split = sem("hi_split")
        lo_split = sem("lo_split")
        second_done = sem("second_done")
        gated_b2_ready = sem("gated_b2_ready")
        y_ready = sem("y_ready")
        added = sem("added")
        w1_copied = sem("w1_copied")
        gathered = [sem(f"gathered{i}") for i in range(2)]
        w_loaded = [sem(f"w_loaded{i}") for i in range(4)]
        w_scaled = sem("w_scaled")
        w_high = sem("w_high")
        w_low = sem("w_low")
        second_low_dve = sem("second_low_dve")

        X_ORDER = [("xT", 0, 0, 0), ("xT", 0, 1, 0), ("q", 0, 0, 0), ("q", 0, 1, 0), ("xT", 1, 0, 0), ("xT", 1, 1, 0),
                   ("q", 1, 0, 0), ("q", 1, 1, 0), ("xT", 2, 0, 1), ("xT", 2, 1, 2), ("wc", 0, 0, 0), ("wc", 0, 1, 1),
                   ("q", 2, 0, 2), ("q", 2, 1, 0), ("wc", 1, 0, 1), ("wc", 1, 1, 2), ("x3T", 0, 0, 0), ("x3T", 0, 1, 1),
                   ("xT", 3, 0, 3), ("xT", 3, 1, 4), ("logits", 0, 0, 5), ("q", 3, 0, 6), ("q", 3, 1, 2), ("wc", 2, 0, 0),
                   ("wc", 2, 1, 1), ("xT", 4, 0, 3), ("xT", 4, 1, 4), ("q", 4, 0, 5), ("q", 4, 1, 6), ("x3T", 1, 0, 2),
                   ("x3T", 1, 1, 0), ("wc", 3, 0, 1), ("logits", 1, 0, 3), ("wc", 4, 0, 4), ("x3T", 2, 0, 5),
                   ("x3T", 2, 1, 6), ("logits", 2, 0, 2), ("x3T", 3, 0, 0), ("x3T", 3, 1, 1), ("logits", 3, 0, 3),
                   ("x3T", 4, 0, 4), ("x3T", 4, 1, 5), ("logits", 4, 0, 6)]

        def x_use(what, c, part=0):
            n = [u[:3] for u in X_ORDER].index((what, c, part))
            bank = X_ORDER[n][3]
            return n, bank, sum(u[3] == bank for u in X_ORDER[:n])

        def x_arrived(eng, what, c, part=0):
            n, bank, _ = x_use(what, c, part)
            eng.wait_ge(x_done, n + 1)
            return x_ps[bank], x_moved[bank]

        def x_left(eng, what, c, part=0):
            _, bank, before = x_use(what, c, part)
            eng.wait_ge(x_moved[bank], before + 1)

        LN_ORDER = [(2, 0), (2, 1), (2, 2), (2, 3), (3, 0), (3, 1), (2, 4), (3, 2), (3, 3), (3, 4)]

        def ln_use(which, c):
            n = LN_ORDER.index((which, c))
            base, before = n % LN_SETS * 4, sum(PIECES[p][1] for _, p in LN_ORDER[:n])
            return n, before, slice(base, base + PIECES[c][1])

        def tiles_to(c):
            return sum(PIECES[c])

        def beside(c):
            n = PIECES[c][1]
            return slice(n, 2 * n) if c == NP - 1 else slice(0, n)

        def tokens_beside(c):
            return slice(beside(c).start * P, beside(c).stop * P)

        WHOLE = NC - 1

        def normalised(which, c):
            return xn2[:, beside(c), :] if which == 2 or c == WHOLE - 1 else xn3[:, beside(c), :]

        def row_parts(c):
            return q_relu[:, :, :].rearrange("p k s -> p (k s)").bitcast(F16).rearrange(
                "p (t d) -> p t d", t=TC) if c == WHOLE - 1 else xs[:, beside(c), :]

        def chunk_rows(c):
            first, n = PIECES[c]
            return X[:, first * D:(first + n) * D].rearrange("p (t d) -> p t d", d=D)

        def dram_rows(array, c):
            first, n = PIECES[c]
            return array[first * P:(first + n) * P, :].rearrange("(t p) d -> p t d", p=P)

        def mixture(c, m):
            first, n = PIECES[c]
            return kv[:, first // TC, m, first % TC * P:(first % TC + n) * P]

        def halves(c):
            return range(PIECES[c][1] // 2)

        def s2_slot(b, u):
            return u % 2, S2_USES // 2 * b + u // 2

        def at(eng, count):
            return count if isinstance(count, int) else eng.to_reg(count)

        def seq_rows(b):
            return X[:, bass.ds(b % BATCH * (T * D), T * D)].rearrange("p (t d) -> p t d", t=T)

        def nothing(n):
            pass

        def iterations(eng, step, keys=(nothing, nothing), mixing=(nothing, nothing)):
            step(-2, 0, (True, False, False), keys[0])
            step(-1, 1, (True, True, False), keys[1])
            with eng.Fori(0, (BATCH - 2) // 2) as two:
                step(2 * two, 0, (True, True, True), nothing)
                step(2 * two + 1, 1, (True, True, True), nothing)
            step(BATCH - 2, 0, (False, True, True), mixing[0])
            step(BATCH - 1, 1, (False, False, True), mixing[1])

        def expert_pair(eng, two):
            pair = eng.value_load(expert_pairs[0:1, bass.ds(two, 1)], min_val=0, max_val=E * E - 1)
            return pair % E, pair // E

        def blocks_in_turn(eng, step, experts_of=None):
            def pair(two):
                return (None, None) if experts_of is None else expert_pair(eng, two + experts_of // 2)

            def steps(two):
                e = pair(two)
                step(two, 0, 3, e[0])
                step(two, 1, 3, e[1])

            steps(0)
            with eng.Fori(1, (NB - 3) // 2) as two:
                steps(two)
            last = (NB - 3) // 2
            e = pair(last)
            step(last, 0, 2, e[0])
            step(last, 1, 1, e[1])
            e = pair(last + 1) if experts_of == 0 else e
            step(last + 1, 0, 0, e[0])

        def second_place(u):
            return u % len(weights_in)

        def second_loads(u):
            return u // len(weights_in) + 1 + (E if second_place(u) < KD else 0)

        DVE_HALVES = (1, 3, 12, 13, 14, 15)

        def pool_halves(u):
            return u - sum(d < u for d in DVE_HALVES)

        def second_split(eng, u):
            if u in DVE_HALVES:
                eng.wait_ge(second_low_dve, DVE_HALVES.index(u) + 1)
            else:
                eng.wait_ge(w_low, 2 * E + pool_halves(u) + 1)

        def second_half(weights, u):
            return weights[:, u // 2, (u % 2) * KF // 2:(u % 2 + 1) * KF // 2]

        def loaded_half(u):
            return weights_in[second_place(u)][:, :].rearrange("p (k n) -> p k n", n=D)

        LN0, XN0 = BATCH + 1, T * (BATCH + 1)

        block = ctx.enter_context(nc.Block())

        @block.sync
        def _(sp):
            xv = x.rearrange("(t p) d -> p t d", p=P)
            Xv = X[:, :].rearrange("p (t d) -> p t d", d=D)
            sp.dma_start(Xv[:, 0:T, :], xv[:, 0:T, :]).then_inc(x0_loaded, 16)
            sp.dma_start(id_sb[:, :], ident).then_inc(x0_loaded, 16)
            sp.dma_start(wqkv_sb[:, :, :], w_qkv.rearrange("(k p) n -> p k n", p=P)).then_inc(wqkv_loaded, 16)
            sp.dma_start(bqkv_sb[:, :], b_qkv.partition_broadcast(P)).then_inc(wqkv_loaded, 16)
            sp.dma_start(cos_sb[:, :, :], cos.rearrange("(t p) n -> p t n", p=P)).then_inc(wqkv_loaded, 16)
            sp.dma_start(sin_sb[:, :, :], sin.rearrange("(t p) n -> p t n", p=P)).then_inc(wqkv_loaded, 16)

            def load_context(c):
                sp.dma_start(ctx_sb[c], ctxT[:, c * XC:(c + 1) * XC].rearrange("(k p) n -> p k n", p=P)
                             ).then_inc(ctx_loaded[c], 16)

            for dst, src in ((wxkv_sb[:, 0], wx_k), (cum_sb[:, :, :], cumsum_m), (wxkv_sb[:, 1], wx_v)):
                sp.dma_start(dst, src.rearrange("(k p) n -> p k n", p=P)).then_inc(keys_loaded, 16)
            for dst, src in ((bxk_sb, bx_k), (bxv_sb, bx_v)):
                sp.dma_start(dst[:, :], src.rearrange("(k p) -> p k", p=P),
                             allow_slow_non_contiguous=True).then_inc(keys_loaded, 16)
            load_context(0)
            load_context(1)
            sp.dma_start(Xv[:, T:NT, :], xv[:, T:, :]).then_inc(x_loaded, 16)
            sp.dma_start(bo_sb[:, :], b_o.partition_broadcast(P)).then_inc(wo_loaded, 16)
            for k in range(KD):
                sp.dma_start(staged[k][:, :], w1[0, k * P:(k + 1) * P, :]).then_inc(w_loaded[k], 16)
            for c in range(2, NC):
                load_context(c)
            sp.dma_start(wo_sb[:, :, :], w_o.rearrange("(k p) n -> p k n", p=P)).then_inc(wo_loaded, 16)
            for dst, src in ((wxq_sb, wx_q), (wxc_sb, wx_c), (wr_sb, wr)):
                sp.dma_start(dst[:, :, :], src.rearrange("(k p) n -> p k n", p=P)).then_inc(cross_loaded, 16)
            for dst, src in ((bxq_sb, bx_q), (b1_sb, b1)):
                sp.dma_start(dst[:, :], src.rearrange("(k p) -> p k", p=P),
                             allow_slow_non_contiguous=True).then_inc(cross_loaded, 16)
            for dst, src in ((bxc_sb, bx_c), (br_sb, br)):
                sp.dma_start(dst[:, :], src.partition_broadcast(P)).then_inc(cross_loaded, 16)
            sp.dma_start(out[TOKENS:, :], spare_x).then_inc(spare_stored, 16)
            sp.dma_start(rows[TOKENS:, :], spare_rows).then_inc(spare_stored, 16)
            with sp.Fori(1, E) as e:
                for k in range(KD):
                    sp.wait_ge(w_low, 2 * e + k - 1)
                    sp.dma_start(staged[k][:, :], w1[bass.ds(e, 1), k * P:(k + 1) * P, :]
                                 .rearrange("e p n -> (e p) n")).then_inc(w_loaded[k], 16)

            def second_layer(u):
                place = second_place(u)
                if u >= len(weights_in):
                    second_split(sp, u - len(weights_in))
                elif place < KD:
                    sp.wait_ge(w_low, 2 * E - KD + place + 1)
                else:
                    for half in range(2):
                        n, _, _ = x_use("wc", place - KD, half)
                        sp.wait_ge(x_done, n + 1)
                sp.dma_start(loaded_half(u), second_half(w2.rearrange("e (k p) n -> p e k n", p=P), u)).then_inc(w_loaded[place], 16)

            def store_x(c):
                for half in halves(c):
                    x_left(sp, "wc", c, half)
                sp.dma_start(dram_rows(out, c), chunk_rows(c)).then_inc(x_stored, 16)

            def store_rows(c):
                sp.wait_ge(x3_high, c + 1)
                sp.wait_ge(x3_low, c + 1)
                if c == WHOLE - 1:
                    sp.wait_ge(rows_stored, 16 * c)
                sp.dma_start(dram_rows(rows, c), row_parts(c)).then_inc(rows_stored, 16)

            second_layer(0)
            second_layer(1)
            store_x(0)
            second_layer(2)
            second_layer(4)
            second_layer(5)
            second_layer(3)
            store_x(1)
            store_rows(0)
            second_layer(6)
            store_x(2)
            sp.dma_start(route_sb[:, :], route_c).then_inc(route_loaded, 16)
            sp.dma_start(rank_sb[:, :], rank_m).then_inc(route_loaded, 16)
            store_rows(1)
            store_x(3)
            second_layer(7)
            store_x(4)
            store_rows(2)
            store_rows(3)
            store_rows(4)
            for u in range(8, 2 * E):
                second_layer(u)
            for u in range(2 * E - len(weights_in), 2 * E):
                second_split(sp, u)
            sp.dma_start(b2_sb[:, :, :].rearrange("p e n -> p (e n)"),
                         b2.rearrange("e n -> (e n)").partition_broadcast(P)).then_inc(b2_loaded, 16)
            def transpose_block(two, o):
                have, used = at(sp, 16 * two + 16), at(sp, 4 * two + 2 * o - 2)
                sp.wait_ge(x0_loaded, 32)
                sp.wait_ge(gathered[o], have)
                sp.wait_ge(first_done, used)
                sp.dma_start_transpose(xgT[o][:, :, :, :].rearrange("p h k s -> p (h k) s"), xg[o][:, :]).then_inc(xg_transposed[o], 16)

            with sp.Fori(1, NB // 2) as two:
                transpose_block(two, 0)
                transpose_block(two, 1)
            transpose_block(NB // 2, 0)
            sp.wait_ge(spare_stored, 32)
            sp.wait_ge(x_stored, 16 * NP)
            sp.wait_ge(rows_stored, 16 * NP)
            sp.wait_ge(added, 16 * NB)

        CROSS_LOADS, KEYS_LOADS = 7 * 16, 5 * 16

        @block.gpsimd
        def _(pool):
            nc.gpsimd.memset(minus_half[:, :], -0.5).then_inc(half_set, 1)
            pool.wait_ge(half_set, 1)
            def inverse_deviation(n, stats_done, of):
                c = slice(0, of.stop - of.start)
                stats_done, halved = at(pool, stats_done), at(pool, 3 * n + 2)
                pool.wait_ge(half_set, 1)
                pool.wait_ge(ln_mv, stats_done)
                nc.gpsimd.tensor_scalar(var_eps[:, c], mv[:, of, 1], EPS, None, ALU.add).then_inc(var_ready, 1)
                pool.wait_ge(var_ready, n + 1)
                nc.gpsimd.tensor_tensor(guess[:, c], var_eps[:, c], minus_half[:, c], ALU.pow).then_inc(guess_ready, 1)
                pool.wait_ge(guess_ready, n + 1)
                nc.gpsimd.tensor_tensor(newton[:, 0, c], guess[:, c], guess[:, c], ALU.mult).then_inc(newton_step, 1)
                pool.wait_ge(newton_step, 3 * n + 1)
                nc.gpsimd.tensor_tensor(newton[:, 1, c], newton[:, 0, c], var_eps[:, c], ALU.mult).then_inc(newton_step, 1)
                pool.wait_ge(half_set, 1)
                pool.wait_ge(newton_step, halved)
                nc.gpsimd.tensor_scalar(newton[:, 2, c], newton[:, 1, c], -0.5, 1.5, ALU.mult, ALU.add).then_inc(newton_step, 1)
                pool.wait_ge(newton_step, 3 * n + 3)
                nc.gpsimd.tensor_tensor(rstd[:, of], guess[:, c], newton[:, 2, c], ALU.mult).then_inc(ln_rstd, 1)

            def values(b, o):
                for u in U_V:
                    pool.wait_ge(s1_moved, S1_USES * b + u + 1)
                if not isinstance(b, int) or b >= 2:
                    pool.wait_ge(pv_done, GROUPS * (b - 1) + 1)
                nc.gpsimd.tensor_tensor(v1[o][:, :, :, 0:DH], v_raw[:, :, :].rearrange("p t (h d) -> p t h d", d=DH),
                                        bqkv_sb[:, 2 * D:].rearrange("p (h d) -> p h d", d=DH).unsqueeze(1)
                                        .to_broadcast([P, T, H, DH]), ALU.add).then_inc(v_ready, 1)

            def low_parts(b, k):
                high = at(pool, 2 * b + k + 1)
                pool.wait_ge(half_set, 1)
                pool.wait_ge(w_high, high)
                dst = W1[:, bass.ds(b, 1), k, :, :]
                nc.gpsimd.tensor_tensor(dst[:, 0, 1, :], staged[k][:, :], dst[:, 0, 0, :],
                                        ALU.subtract).then_inc(w_low, 1)

            def add_output_bias(b):
                pool.wait_ge(wo_loaded, 32)
                pool.wait_ge(xn_ready, T * b + T)
                rows = seq_rows(b)
                nc.gpsimd.tensor_tensor(rows, rows, bo_sb[:, :].unsqueeze(1).to_broadcast([P, T, D]),
                                        ALU.add).then_inc(xb_ready, 1)

            def rotate(b, t):
                pool.wait_ge(s1_moved, S1_USES * b + U_QK[t] + 1)
                nc.gpsimd.tensor_tensor(
                    rot_c[:, t, :].rearrange("p (h d) -> p h d", d=DH),
                    qk[:, t, :].rearrange("p (h d) -> p h d", d=DH),
                    cos_sb[:, t, :].unsqueeze(1).to_broadcast([P, 2 * H, DH]), ALU.mult).then_inc(rot_c_ready, 1)
                pool.wait_ge(rot_c_ready, T * b + t + 1)
                pool.wait_ge(rot_s_ready, T * b + t + 1)
                nc.gpsimd.tensor_tensor(roped[:, t, :], rot_c[:, t, :], rot_s[:, t, :], ALU.add).then_inc(roped_ready, 1)

            def low_stacks(b, o, t):
                heads = roped[:, t, :].rearrange("p (w h d) -> p w h d", w=2, d=DH)
                qs, ks = q_stack[o][:, t], k_stack[:, t]
                high = at(pool, 2 * T * b + 2 * t + 2)
                pool.wait_ge(half_set, 1)
                pool.wait_ge(hi_ready, high)
                nc.gpsimd.memset(qs[:, :, ROW_MAX:ROW_MAX + 1], 0.0).then_inc(lo_ready, 1)
                nc.gpsimd.tensor_tensor(qs[:, :, 48:64], heads[:, 0], qs[:, :, 0:16], ALU.subtract).then_inc(lo_ready, 1)
                nc.gpsimd.tensor_tensor(ks[:, :, 16:32], heads[:, 1], ks[:, :, 0:16], ALU.subtract).then_inc(lo_ready, 1)

            def shift(b, o, t):
                last_two = [s2_slot(b, U_SC[g]) for g in (PAIRS * t + PAIRS - 2, PAIRS * t + PAIRS - 1)]
                moved = [at(pool, n + 1) for _, n in last_two]
                pool.wait_ge(half_set, 1)
                for (bank, _), n in zip(last_two, moved):
                    pool.wait_ge(s2_moved[bank], n)
                nc.gpsimd.tensor_scalar(q_stack[o][:, t, :, ROW_MAX], mx[:, t, :], -1.0, None,
                                        ALU.mult).then_inc(negm_ready, 1)

            def ratios(c):
                for m in range(KD):
                    pool.wait_ge(cum_moved, KD * c + m + 1)
                    nc.gpsimd.tensor_tensor(kv[:, c, m, :], k_exp[c % 2][:, m, :], kv[:, c, m, :],
                                            ALU.mult).then_inc(ratio_ready, 1)

            def chunk_deviation(which, c):
                n, before, of = ln_use(which, c)
                inverse_deviation(LN0 + n, XN0 + before + PIECES[c][1], of)

            def add_cross_bias(c):
                pool.wait_ge(cross_loaded, CROSS_LOADS)
                pool.wait_ge(xc_normed, tiles_to(c))
                nc.gpsimd.tensor_tensor(chunk_rows(c), chunk_rows(c), bxc_sb[:, :].unsqueeze(1).to_broadcast([P, PIECES[c][1], D]),
                                        ALU.add).then_inc(xc_ready, 1)

            def mix(c):
                for m in range(KD):
                    pool.wait_ge(q_heads_ready, KD * c + m + 1)
                    nc.gpsimd.tensor_tensor(mixture(c, m), q_exp[:, m, tokens_beside(c)], mixture(c, m),
                                            ALU.mult).then_inc(mixed_ready, 1)

            def second_low(u):
                pool.wait_ge(w_high, 2 * E + u + 1)
                nc.gpsimd.tensor_tensor(second_half(W2[:, :, :, 1, :], u), loaded_half(u), second_half(W2[:, :, :, 0, :], u),
                                        ALU.subtract).then_inc(w_low, 1)

            def low_rows(c):
                pool.wait_ge(x3_high, c + 1)
                rows_of = row_parts(c)
                nc.gpsimd.tensor_tensor(rows_of[:, :, D:], normalised(3, c), rows_of[:, :, 0:D], ALU.subtract).then_inc(x3_low, 1)

            def step(j, o, stages, also):
                also(0)
                if stages[1]:
                    values(j + 1, 1 - o)
                    low_parts(j + 1, 1)
                if stages[0]:
                    rotate(j + 2, 0)
                    low_stacks(j + 2, o, 0)
                if stages[1]:
                    shift(j + 1, 1 - o, 0)
                if stages[0]:
                    rotate(j + 2, 1)
                    add_output_bias(j + 2)
                also(1)
                if stages[0]:
                    low_stacks(j + 2, o, 1)
                also(2)
                if stages[1]:
                    shift(j + 1, 1 - o, 1)
                if stages[0]:
                    inverse_deviation(j + 3, T * (j + 3) + T, slice(0, T))
                also(3)
                if stages[0]:
                    low_parts(j + 2, 0)

            def first_keys(n):
                if n == 2:
                    ratios(0)
                if n == 3:
                    ratios(1)

            def last_keys(n):
                if n == 2:
                    ratios(2)
                if n == 3:
                    ratios(3)

            def first_mixing(n):
                if n == 0:
                    chunk_deviation(2, 0)
                    chunk_deviation(2, 1)
                    add_cross_bias(0)
                if n == 2:
                    mix(0)
                if n == 3:
                    chunk_deviation(2, 2)
                    add_cross_bias(1)

            def last_mixing(n):
                if n == 0:
                    mix(1)
                    chunk_deviation(2, 3)
                if n == 1:
                    add_cross_bias(2)
                    second_low(0)
                if n == 2:
                    chunk_deviation(3, 0)
                    add_cross_bias(3)
                    mix(2)
                    chunk_deviation(3, 1)
                if n == 3:
                    second_low(2)

            for stack in (*q_stack, k_stack):
                nc.gpsimd.memset(stack[:, :, :, ROW_MAX:ROW_MAX + DH], 0.0).then_inc(stacks_cleared, 1)
            pool.wait_ge(stacks_cleared, 3)
            nc.gpsimd.memset(k_stack[:, :, :, ROW_MAX:ROW_MAX + 1], 1.0).then_inc(consts_set, 1)
            for i in range(2):
                nc.gpsimd.memset(v1[i][:, :, :, DH:], 1.0).then_inc(consts_set, 1)
            pool.wait_ge(consts_set, 3)
            inverse_deviation(0, T, slice(0, T))
            pool.wait_ge(wqkv_loaded, 64)
            iterations(pool, step, (first_keys, last_keys), (first_mixing, last_mixing))

            chunk_deviation(2, 4)
            low_rows(0)
            add_cross_bias(4)
            mix(3)
            chunk_deviation(3, 2)
            mix(4)
            low_rows(1)
            chunk_deviation(3, 3)
            chunk_deviation(3, 4)
            low_rows(2)
            low_rows(3)
            low_rows(4)
            for u in range(4, 12):
                second_low(u)

            pool.wait_ge(rows_stored, 16 * NP)
            pool.wait_ge(x_stored, 16 * NP)
            pool.wait_ge(spare_stored, 32)
            pool.wait_ge(experts_ready, 2)
            pool.wait_ge(ids_ready, 1)

            def gather(i, o, turn, copies):
                if not isinstance(i, int) or i >= 4:
                    rows_read = at(pool, 16 * turn - 16)
                    pool.wait_ge(half_set, 1)
                    pool.wait_ge(xg_transposed[o], rows_read)
                elif i >= 2:
                    pool.wait_ge(xgT_moved, i - 1)
                nc.gpsimd.tensor_copy(gather_ids[o][:, :], block_rows[:, bass.ds(i, 1)]).then_inc(ids_copied, 1)
                copied = at(pool, copies + 1)
                pool.wait_ge(half_set, 1)
                pool.wait_ge(ids_copied, copied)
                nc.gpsimd.indirect_dma_start(xg[o][:, :], None, rows, bass.IndirectOffsetOnAxis(ap=gather_ids[o][:, :], axis=0)
                                             ).then_inc(gathered[o], 16)

            def gate_b2(i, o):
                e = pool.value_load(block_expert[0:1, bass.ds(i, 1)], min_val=0, max_val=E - 1)
                if not isinstance(i, int) or i >= 2:
                    pool.wait_ge(half_set, 1)
                    pool.wait_ge(y_ready, at(pool, i - 1))
                nc.gpsimd.tensor_tensor(gated_b2[o][:, :].unsqueeze(1), b2_sb[:, bass.ds(e, 1), :],
                                        block_gates[:, bass.ds(i, 1)].unsqueeze(2).to_broadcast([P, 1, D]),
                                        ALU.mult).then_inc(gated_b2_ready, 1)

            def add(i, o, copies):
                nc.gpsimd.tensor_copy(add_ids[o][:, :], block_rows[:, bass.ds(i, 1)]).then_inc(ids_copied, 1)
                copied, have, before = at(pool, copies + 1), at(pool, i + 1), at(pool, 16 * i)
                pool.wait_ge(half_set, 1)
                pool.wait_ge(ids_copied, copied)
                pool.wait_ge(y_ready, have)
                pool.wait_ge(added, before)
                nc.gpsimd.indirect_dma_start(out, bass.IndirectOffsetOnAxis(ap=add_ids[o][:, :], axis=0), y[o][:, :], None,
                                             compute_op=ALU.add).then_inc(added, 16)

            def block_step(two, o, ahead, e):
                i = 2 * two + o
                if ahead >= 3:
                    gather(i + 3, 1 - o, two + 1 + o, 3 + 2 * i)
                if isinstance(i, int) and i == 0:
                    pool.wait_ge(b2_loaded, 16)
                    pool.wait_ge(ids_ready, 3)
                gate_b2(i, o)
                add(i, o, 2 * i + 4 if ahead >= 3 else i + NB)

            for i in range(3):
                gather(i, i % 2, i // 2, i)
            blocks_in_turn(pool, block_step)

        @block.scalar
        def _(act):
            act.wait_ge(x0_loaded, 32)
            nc.scalar.copy(id16[:, :], id_sb[:, :]).then_inc(id16_ready, 1)

            def move_xnT(b):
                act.wait_ge(s1_done, S1_USES * b + U_XNT + 1)
                nc.scalar.copy(xnT[:, :, :], s1_ps[:, :].rearrange("p (k s) -> p k s", k=KD)).then_inc(s1_moved, 1)

            def move_v(b, t):
                act.wait_ge(s1_done, S1_USES * b + U_V[t] + 1)
                if t == 0 and (not isinstance(b, int) or b >= 1):
                    act.wait_ge(v_ready, b)
                nc.scalar.copy(v_raw[:, t, :], s1_ps[:, 0:D]).then_inc(s1_moved, 1)

            def high_parts(b, o, t):
                act.wait_ge(roped_ready, T * b + t + 1)
                heads = roped[:, t, :].rearrange("p (w h d) -> p w h d", w=2, d=DH)
                for w, dst in ((0, q_stack[o][:, t, :, 0:32].rearrange("p h (r d) -> p h r d", d=DH)),
                               (1, k_stack[:, t, :, :].rearrange("p h (r d) -> p h r d", d=DH)[:, :, 0:4:3, :])):
                    nc.scalar.copy(dst, heads[:, w].unsqueeze(2).to_broadcast([P, H, 2, DH])).then_inc(hi_ready, 1)

            def move_even_kT(b, o, r):
                bank, _ = s2_slot(b, U_KT[r])
                act.wait_ge(s2_done, S2_USES * b + U_KT[r] + 1)
                src = s2_ps[bank][:, :].bitcast(F16).rearrange("p (a s) -> p a s", s=SEQ)
                dst = kT[o][:, 8 * r:8 * r + 8, :].rearrange("p (a two) s -> p a two s", two=2)
                nc.scalar.copy(dst[0:64, :, 0, :], src[0:64]).then_inc(even_kT_moved, 1)

            def move_qmT(b, o, t):
                bank, _ = s2_slot(b, U_RT[t])
                act.wait_ge(s2_done, S2_USES * b + U_RT[t] + 1)
                src = s2_ps[bank][:, :].bitcast(F16).rearrange("p (a s) -> p a s", s=P)
                nc.scalar.copy(qmT[:, :, t * P:(t + 1) * P], src).then_inc(s2_moved[bank], 1)

            def exponentials(b, g):
                act.wait_ge(scores_ready, GROUPS * b + g + 1)
                if g >= 2:
                    act.wait_ge(pv_done, GROUPS * b + g - 1)
                nc.scalar.activation(probs[g % 2][:, :, :], s_ps[g % 2][:, :, :], ACT.Exp,
                                     scale=SCALE).then_inc(exp_done, 1)

            def first_layer(b, k):
                act.wait_ge(w_loaded[k], 16 * b + 16)
                nc.scalar.activation(staged[k][:, :], staged[k][:, :], ACT.Copy, scale=WSCALE).then_inc(w_scaled, 1)
                scaled = at(act, 2 * b + k + 1)
                act.wait_ge(consts_set, 3)
                act.wait_ge(w_scaled, scaled)
                nc.scalar.copy(W1[:, bass.ds(b, 1), k, 0, :], staged[k][:, :].unsqueeze(1)).then_inc(w_high, 1)

            def second_layer(u):
                place = second_place(u)
                high = second_half(W2[:, :, :, 0, :], u)
                act.wait_ge(w_loaded[place], 16 * second_loads(u))
                if u in DVE_HALVES:
                    nc.scalar.activation(high, loaded_half(u), ACT.Copy, scale=WSCALE).then_inc(w_high, 1)
                else:
                    nc.scalar.activation(loaded_half(u), loaded_half(u), ACT.Copy, scale=WSCALE).then_inc(w_scaled, 1)
                    act.wait_ge(w_scaled, 2 * E + pool_halves(u) + 1)
                    nc.scalar.copy(high, loaded_half(u)).then_inc(w_high, 1)

            def elu_parts(src, bias, exp, relu):
                nc.scalar.activation(exp, src, ACT.Exp, bias=bias)
                return nc.scalar.activation(relu, src, ACT.Relu, bias=bias)

            def key_parts(c):
                for m in range(KD):
                    act.wait_ge(k_done, KD * c + m + 1)
                    if c >= 2:
                        act.wait_ge(ratio_ready, KD * (c - 1))
                    elu_parts(key_ps[c % 2][m], bxk_sb[:, m:m + 1], k_exp[c % 2][:, m, :], k_relu[c % 2][:, m, :]).then_inc(k_moved, 1)

            def move_xT(c):
                for k in range(KD):
                    src, moved = x_arrived(act, "xT", c, k)
                    if c == 0 and k == 0:
                        act.wait_ge(lo_ready, 3 * T * BATCH)
                    nc.scalar.copy(xT[:, k, tokens_beside(c)], src[:, 0:PIECES[c][1] * P]).then_inc(moved, 1)

            def query_parts(c):
                act.wait_ge(cross_loaded, CROSS_LOADS)
                for m in range(KD):
                    src, moved = x_arrived(act, "q", c, m)
                    if c > 0:
                        act.wait_ge(mixed_ready, KD * c)
                    own = tokens_beside(c)
                    elu_parts(src[:, 0:PIECES[c][1] * P], bxq_sb[:, m:m + 1], q_exp[:, m, own], q_relu[:, m, own]).then_inc(moved, 1)

            def move_x3T(c):
                for k in range(KD):
                    src, moved = x_arrived(act, "x3T", c, k)
                    if c > 0 and k == 0:
                        x_arrived(act, "logits", c - 1)
                    nc.scalar.copy(x3T[:, k, tokens_beside(c)], src[:, 0:PIECES[c][1] * P]).then_inc(moved, 1)

            def high_rows(c):
                act.wait_ge(x3_normed, tiles_to(c))
                if c == WHOLE - 1:
                    act.wait_ge(q_heads_ready, KD * NP)
                elif c > 0:
                    act.wait_ge(rows_stored, 16 * min(c, WHOLE - 1))
                nc.scalar.copy(row_parts(c)[:, :, 0:D], normalised(3, c)).then_inc(x3_high, 1)

            def step(j, o, stages, also):
                def probabilities(*groups):
                    for g in groups:
                        if stages[2]:
                            exponentials(j, g)
                        also(g + 1)

                also(0)
                if stages[1]:
                    move_even_kT(j + 1, 1 - o, 1)
                if stages[0]:
                    move_xnT(j + 2)
                probabilities(0, 1)
                if stages[0]:
                    first_layer(j + 2, 0)
                probabilities(2, 3, 4)
                if stages[0]:
                    high_parts(j + 2, o, 0)
                probabilities(5, 6, 7)
                if stages[0]:
                    high_parts(j + 2, o, 1)
                if stages[1]:
                    move_qmT(j + 1, 1 - o, 0)
                if stages[0]:
                    move_v(j + 2, 0)
                    move_v(j + 2, 1)
                    first_layer(j + 2, 1)
                also(9)
                if stages[1]:
                    move_qmT(j + 1, 1 - o, 1)
                if stages[0]:
                    move_even_kT(j + 2, o, 0)
                also(10)

            def first_keys(n):
                if n == 3:
                    key_parts(0)
                if n == 6:
                    key_parts(1)

            def last_keys(n):
                if n == 0:
                    key_parts(2)
                if n == 8:
                    key_parts(3)

            def first_mixing(n):
                if n == 3:
                    move_xT(0)
                if n == 5:
                    query_parts(0)
                if n == 8:
                    move_xT(1)
                if n == 10:
                    query_parts(1)

            def last_mixing(n):
                if n == 2:
                    move_xT(2)
                if n == 4:
                    act.wait_ge(v_ready, BATCH)
                    second_layer(0)
                if n == 5:
                    second_layer(1)
                if n == 6:
                    query_parts(2)
                if n == 9:
                    move_x3T(0)
                if n == 10:
                    second_layer(2)
                    high_rows(0)

            act.wait_ge(consts_set, 3)
            iterations(act, step, (first_keys, last_keys), (first_mixing, last_mixing))

            act.wait_ge(o_moved, 1 + O_USES * BATCH)
            move_xT(3)
            query_parts(3)
            move_xT(4)
            query_parts(4)
            move_x3T(1)
            high_rows(1)
            second_layer(3)
            second_layer(4)
            move_x3T(2)
            high_rows(2)
            move_x3T(3)
            high_rows(3)
            move_x3T(4)
            high_rows(4)
            second_layer(5)
            act.wait_ge(gap_ready, 1)
            nc.scalar.activation(v_exp[:, :], v_gap[:, :], ACT.Exp).then_inc(gap_exp, 1)
            for u in range(6, 2 * E):
                second_layer(u)

            nc.scalar.activation(gelu_table[:, :], b1_sb[:, 0:1], ACT.Gelu_apprx_tanh)
            act.wait_ge(experts_ready, 2)

            def hidden(i, o):
                e = act.value_load(block_expert[0:1, bass.ds(i, 1)], min_val=0, max_val=E - 1)
                for m in range(KF):
                    have = at(act, 2 * i + m // (KF // 2) + 1)
                    split = at(act, 2 * i - 2)
                    act.wait_ge(consts_set, 3)
                    act.wait_ge(first_done, have)
                    if m == 0 and (not isinstance(i, int) or i >= 2):
                        act.wait_ge(lo_split, split)
                    nc.scalar.activation(hid[o][:, m, :], hid_ps[o][:, m, :], ACT.Gelu_apprx_tanh,
                                         bias=b1_sb[:, bass.ds(e * KF + m, 1)], scale=1 / WSCALE).then_inc(gelu_done, 1)

            def block_step(two, o, ahead, e):
                if ahead >= 1:
                    hidden(2 * two + o + 1, 1 - o)

            hidden(0, 0)
            blocks_in_turn(act, block_step)

        @block.vector
        def _(dve):
            def statistics(b):
                rows = seq_rows(b)
                if not isinstance(b, int) or b > 0:
                    dve.wait_ge(x_loaded, 16)
                for t in range(T):
                    nc.vector.bn_stats(stats[:, t, :], rows[:, t, :]).then_inc(ln_stats, 1)
                for t in range(T):
                    have = at(dve, T * b + t + 1)
                    dve.wait_ge(x0_loaded, 32)
                    dve.wait_ge(ln_stats, have)
                    nc.vector.bn_aggr(mv[:, t, :], stats[:, t, :]).then_inc(ln_mv, 1)

            def normalise(b):
                rows = seq_rows(b)
                dve.wait_ge(ln_rstd, b + 1)
                for t in range(T):
                    nc.vector.tensor_scalar(xn[:, t, :], rows[:, t, :], mv[:, t, 0:1], rstd[:, t:t + 1],
                                            ALU.subtract, ALU.mult).then_inc(xn_ready, 1)

            def add_bias(b, t):
                dve.wait_ge(s1_done, S1_USES * b + U_QK[t] + 1)
                nc.vector.tensor_tensor(qk[:, t, :], s1_ps[:, :], bqkv_sb[:, 0:2 * D], ALU.add).then_inc(s1_moved, 1)

            def rotate_swapped(b, t):
                dve.wait_ge(s1_moved, S1_USES * b + U_QK[t] + 1)
                src = qk[:, t, :].rearrange("p (h two e) -> p h two e", two=2, e=DH // 2)
                dst = rot_s[:, t, :].rearrange("p (h two e) -> p h two e", two=2, e=DH // 2)
                sn = sin_sb[:, t, :].rearrange("p (two e) -> p two e", two=2)
                for half in range(2):
                    last = nc.vector.tensor_tensor(
                        dst[:, :, half, :], src[:, :, 1 - half, :],
                        sn[:, half, :].unsqueeze(1).to_broadcast([P, 2 * H, DH // 2]), ALU.mult)
                last.then_inc(rot_s_ready, 1)

            def move_qT(b, r):
                bank, _ = s2_slot(b, U_QT[r])
                dve.wait_ge(s2_done, S2_USES * b + U_QT[r] + 1)
                src = s2_ps[bank][:, :].bitcast(F16).rearrange("p (a s) -> p a s", s=SEQ)
                nc.vector.tensor_copy(qT[:, 4 * r:4 * r + 4, :], src).then_inc(s2_moved[bank], 1)

            def move_odd_kT(b, o, r):
                bank, _ = s2_slot(b, U_KT[r])
                dve.wait_ge(s2_done, S2_USES * b + U_KT[r] + 1)
                src = s2_ps[bank][:, :].bitcast(F16).rearrange("p (a s) -> p a s", s=SEQ)
                dst = kT[o][:, 8 * r:8 * r + 8, :].rearrange("p (a two) s -> p a two s", two=2)
                nc.vector.tensor_copy(dst[64:128, :, 1, :], src[64:128]).then_inc(s2_moved[bank], 1)

            def maxima(b, first, count):
                for g in range(first, first + count):
                    t, pair = divmod(g, PAIRS)
                    bank, _ = s2_slot(b, U_SC[g])
                    dve.wait_ge(s2_done, S2_USES * b + U_SC[g] + 1)
                    nc.vector.reduce_max(mx[:, t, 2 * pair:2 * pair + 2],
                                         s2_ps[bank][:, :].rearrange("p (h s) -> p h s", h=2), AX.X).then_inc(s2_moved[bank], 1)

            def divide(b, half):
                dve.wait_ge(pv_done, GROUPS * b + 4 * half + 4)
                if half > 0:
                    dve.wait_ge(oT_ready, 2 * b + half)
                nc.vector.transpose(o_rows[:, :, :].rearrange("p c r -> p (c r)"), o_ps[:, :]).then_inc(o_moved, 1)
                dve.wait_ge(o_moved, 1 + O_USES * b + half + 1)
                nc.vector.reciprocal(rsums[:, :], o_rows[:, :, DH]).then_inc(rsums_ready, 1)
                dve.wait_ge(rsums_ready, 2 * b + half + 1)
                nc.vector.tensor_tensor(o_rows[:, :, 0:DH], o_rows[:, :, 0:DH],
                                        rsums[:, :].unsqueeze(2).to_broadcast([P, 2 * SEQ // 32, DH]),
                                        ALU.mult).then_inc(o_scaled, 1)
                dve.wait_ge(o_scaled, 2 * b + half + 1)
                nc.vector.transpose(oT[:, 2 * half:2 * half + 2, :].rearrange("p q s -> p (q s)"),
                                    o_rows[:, :, :].rearrange("p c r -> p (c r)")).then_inc(oT_ready, 1)

            def residual(b):
                dve.wait_ge(wo_done, b + 1)
                dve.wait_ge(xb_ready, b + 1)
                rows = seq_rows(b)
                nc.vector.tensor_tensor(rows, o_ps[:, :].rearrange("p (t d) -> p t d", t=T), rows,
                                        ALU.add).then_inc(o_moved, 1)

            def second_low(u):
                dve.wait_ge(w_high, 2 * E + u + 1)
                nc.vector.scalar_tensor_tensor(second_half(W2[:, :, :, 1, :], u), loaded_half(u), WSCALE,
                                               second_half(W2[:, :, :, 0, :], u), ALU.mult,
                                               ALU.subtract).then_inc(second_low_dve, 1)

            def key_heads(c):
                for m in range(KD):
                    dve.wait_ge(k_moved, KD * c + m + 1)
                    nc.vector.scalar_tensor_tensor(k_exp[c % 2][:, m, :], k_exp[c % 2][:, m, :], 1.0, k_relu[c % 2][:, m, :],
                                                   ALU.min, ALU.add).then_inc(k_heads_ready, 1)

            def inverse_sums(c, m):
                dve.wait_ge(cum_done, KD * c + m + 1)
                nc.vector.reciprocal(kv[:, c, m, :], key_ps[c % 2][m]).then_inc(cum_moved, 1)

            def weighted_values(c):
                for m in range(KD):
                    dve.wait_ge(v_done, KD * c + m + 1)
                    dve.wait_ge(ratio_ready, KD * c + m + 1)
                    nc.vector.scalar_tensor_tensor(kv[:, c, m, :], key_ps[c % 2][m], bxv_sb[:, m:m + 1], kv[:, c, m, :],
                                                   ALU.add, ALU.mult).then_inc(v_moved, 1)

            def chunk_statistics(which, c):
                _, before, of = ln_use(which, c)
                if which == 3:
                    for half in halves(c):
                        x_left(dve, "wc", c, half)
                for t in range(PIECES[c][1]):
                    nc.vector.bn_stats(stats[:, t, :], chunk_rows(c)[:, t, :]).then_inc(ln_stats, 1)
                for t in range(PIECES[c][1]):
                    dve.wait_ge(ln_stats, XN0 + before + t + 1)
                    nc.vector.bn_aggr(mv[:, of.start + t, :], stats[:, t, :]).then_inc(ln_mv, 1)

            def normalise_chunk(which, c):
                n, _, of = ln_use(which, c)
                dst, normed = normalised(which, c), (xc_normed if which == 2 else x3_normed)
                if which == 2 and c == 0:
                    dve.wait_ge(s1_done, S1_USES * BATCH)
                elif which == 2:
                    x_arrived(dve, "xT", min(c, WHOLE) - 1, KD - 1)
                elif c == WHOLE - 1:
                    x_arrived(dve, "xT", NP - 1, KD - 1)
                elif c > 0:
                    last = 0 if c == 1 else 1
                    x_arrived(dve, "x3T", last, KD - 1)
                    dve.wait_ge(x3_low, last + 1)
                dve.wait_ge(ln_rstd, LN0 + n + 1)
                for t in range(PIECES[c][1]):
                    i = of.start + t
                    nc.vector.tensor_scalar(dst[:, t, :], chunk_rows(c)[:, t, :], mv[:, i, 0:1], rstd[:, i:i + 1],
                                            ALU.subtract, ALU.mult).then_inc(normed, 1)

            def query_heads(c):
                for m in range(KD):
                    x_left(dve, "q", c, m)
                    nc.vector.scalar_tensor_tensor(q_exp[:, m, tokens_beside(c)], q_exp[:, m, tokens_beside(c)], 1.0, q_relu[:, m, tokens_beside(c)],
                                                   ALU.min, ALU.add).then_inc(q_heads_ready, 1)

            def cross_residual(c):
                dve.wait_ge(xc_ready, c + 1)
                for half in halves(c):
                    src, moved = x_arrived(dve, "wc", c, half)
                    part = chunk_rows(c)[:, 2 * half:2 * half + 2, :]
                    nc.vector.tensor_tensor(part, src.rearrange("p (t d) -> p t d", t=2), part, ALU.add).then_inc(moved, 1)

            def choose(c):
                src, moved = x_arrived(dve, "logits", c)
                first, n = PIECES[c]
                nc.vector.tensor_tensor(lg[:, 0:n, :], src[:, 0:n * E].rearrange("p (t e) -> p t e", e=E),
                                        br_sb[:, :].unsqueeze(1).to_broadcast([P, n, E]), ALU.add).then_inc(moved, 1)
                x_left(dve, "logits", c)
                for t in range(n):
                    nc.vector.max(best_v[:, t, :], lg[:, t, :]).then_inc(best_found, 1)
                for t in range(n):
                    dve.wait_ge(best_found, 2 * first + t + 1)
                    nc.vector.max_index(best_e[:, t, :], best_v[:, t, :], lg[:, t, :]).then_inc(best_found, 1)
                dve.wait_ge(best_found, 2 * first + 2 * n)
                tiles = slice(first, first + n)
                nc.vector.tensor_copy(top_v[:, :, tiles], best_v[:, 0:n, 0:TOP].rearrange("p t k -> p k t")).then_inc(best_kept, 1)
                nc.vector.tensor_copy(top_e[:, :, tiles], best_e[:, 0:n, 0:TOP].rearrange("p t k -> p k t")).then_inc(best_kept, 1)

            def step(j, o, stages, also):
                def s2_max(first, count):
                    if stages[1]:
                        maxima(j + 1, first, count)

                also(0)
                if stages[1]:
                    move_odd_kT(j + 1, 1 - o, 1)
                s2_max(0, 2)
                also(1)
                if stages[0]:
                    add_bias(j + 2, 0)
                s2_max(2, 2)
                if stages[0]:
                    rotate_swapped(j + 2, 0)
                also(2)
                s2_max(4, 3)
                also(3)
                if stages[2]:
                    divide(j, 0)
                s2_max(7, 1)
                also(4)
                if stages[0]:
                    add_bias(j + 2, 1)
                s2_max(8, 1)
                also(5)
                s2_max(9, 1)
                if stages[0]:
                    rotate_swapped(j + 2, 1)
                s2_max(10, 3)
                also(6)
                s2_max(13, 1)
                if stages[2]:
                    divide(j, 1)
                s2_max(14, 2)
                also(7)
                if stages[0]:
                    statistics(j + 3)
                also(8)
                if stages[0]:
                    move_qT(j + 2, 0)
                    normalise(j + 3)
                if stages[2]:
                    residual(j)
                also(9)
                if stages[0]:
                    move_qT(j + 2, 1)
                    move_odd_kT(j + 2, o, 0)
                also(10)

            def first_keys(n):
                if n == 5:
                    key_heads(0)
                if n == 6:
                    key_heads(1)
                    inverse_sums(0, 0)
                    inverse_sums(0, 1)
                if n == 7:
                    inverse_sums(1, 0)
                if n == 8:
                    weighted_values(0)
                if n == 9:
                    inverse_sums(1, 1)

            def last_keys(n):
                if n == 0:
                    weighted_values(1)
                    key_heads(2)
                if n == 2:
                    inverse_sums(2, 0)
                if n == 4:
                    key_heads(3)
                    inverse_sums(2, 1)
                if n == 5:
                    inverse_sums(3, 0)
                if n == 6:
                    inverse_sums(3, 1)
                    weighted_values(2)
                if n == 10:
                    weighted_values(3)

            def first_mixing(n):
                if n == 0:
                    chunk_statistics(2, 0)
                if n == 1:
                    normalise_chunk(2, 0)
                    chunk_statistics(2, 1)
                if n == 3:
                    normalise_chunk(2, 1)
                if n == 6:
                    query_heads(0)
                if n == 8:
                    chunk_statistics(2, 2)
                if n == 9:
                    normalise_chunk(2, 2)
                if n == 10:
                    query_heads(1)

            def last_mixing(n):
                if n == 0:
                    dve.wait_ge(o_moved, 1 + O_USES * (BATCH - 1))
                    chunk_statistics(2, 3)
                if n == 3:
                    cross_residual(0)
                    normalise_chunk(2, 3)
                if n == 4:
                    chunk_statistics(3, 0)
                    normalise_chunk(3, 0)
                if n == 6:
                    query_heads(2)
                if n == 7:
                    cross_residual(1)
                if n == 8:
                    second_low(1)
                    chunk_statistics(3, 1)

            for i in range(2):
                heads = kT[i][:, :, :].rearrange("p h s -> p (h s)").bitcast(F32).rearrange("p (a two s) -> p a two s", two=2, a=PAIRS)
                nc.vector.memset(heads[0:64, :, 1, :], 0.0).then_inc(keys_cleared, 1)
                nc.vector.memset(heads[64:128, :, 0, :], 0.0).then_inc(keys_cleared, 1)
            dve.sem_inc(o_moved, 1)
            dve.wait_ge(x0_loaded, 32)
            statistics(0)
            normalise(0)
            dve.wait_ge(wqkv_loaded, 64)
            dve.wait_ge(consts_set, 3)
            iterations(dve, step, (first_keys, last_keys), (first_mixing, last_mixing))

            dve.wait_ge(o_moved, 1 + O_USES * BATCH)
            chunk_statistics(2, 4)
            choose(0)
            query_heads(3)
            normalise_chunk(2, 4)
            cross_residual(2)
            chunk_statistics(3, 2)
            normalise_chunk(3, 1)
            query_heads(4)
            normalise_chunk(3, 2)
            cross_residual(3)
            chunk_statistics(3, 3)
            choose(1)
            second_low(3)
            cross_residual(4)
            chunk_statistics(3, 4)
            normalise_chunk(3, 3)
            choose(2)
            normalise_chunk(3, 4)
            choose(3)
            choose(4)

            dve.wait_ge(route_loaded, 32)
            dve.wait_ge(best_kept, 2 * NP)
            dve.wait_ge(x3_low, WHOLE)
            by_choice = [P, TOP, NT, E]
            nc.vector.tensor_tensor(v_gap[:, :], top_v[:, 1, :], top_v[:, 0, :], ALU.subtract).then_inc(gap_ready, 1)
            nc.vector.memset(oh_any[:, NT, :], 0.0).then_inc(choices_ready, 1)
            nc.vector.tensor_tensor(oh[:, :, :, :], top_e[:, :, :].unsqueeze(3).to_broadcast(by_choice),
                                    const("experts").unsqueeze(1).unsqueeze(1).to_broadcast(by_choice),
                                    ALU.is_equal).then_inc(routed, 1)
            dve.wait_ge(routed, 1)
            nc.vector.tensor_tensor(oh_any[:, 0:NT, :], oh[:, 0], oh[:, 1], ALU.add).then_inc(choices_ready, 1)
            dve.wait_ge(gap_exp, 1)
            nc.vector.tensor_scalar(v_sum[:, :], v_exp[:, :], 1.0, None, ALU.add).then_inc(routed, 1)
            dve.wait_ge(routed, 2)
            nc.vector.reciprocal(gates[:, 0, :], v_sum[:, :]).then_inc(routed, 1)
            dve.wait_ge(routed, 3)
            nc.vector.tensor_tensor(gates[:, 1, :], v_exp[:, :], gates[:, 0, :], ALU.mult).then_inc(routed, 1)
            all_gates = gates[:, :, :].rearrange("p k t -> p (k t)")
            dve.wait_ge(routed, 4)
            nc.vector.tensor_scalar(gate_parts[:, 0, :], all_gates, GSCALE, None, ALU.mult).then_inc(gates_split, 1)
            dve.wait_ge(gates_split, 1)
            nc.vector.scalar_tensor_tensor(gate_parts[:, 1, :], all_gates, GSCALE, gate_parts[:, 0, :],
                                           ALU.mult, ALU.subtract).then_inc(gates_split, 1)
            dve.wait_ge(ranks_done, 1)
            floors = [P, E, TOKENS // P]
            nc.vector.tensor_tensor(above[:, :, :], rank_ps[:, NT, :].unsqueeze(2).to_broadcast(floors),
                                    const("block_floors").unsqueeze(1).to_broadcast(floors), ALU.is_gt).then_inc(routed, 1)
            dve.wait_ge(routed, 5)
            nc.vector.reduce_sum(expert_blocks[:, :], above[:, :, :], AX.X).then_inc(routed, 1)
            dve.wait_ge(routed, 6)
            nc.vector.tensor_tensor(bounds_of[:, :, :], const("before").rearrange("p (w e) -> p w e", e=E),
                                    expert_blocks[:, :].unsqueeze(1).to_broadcast([P, 2 * E, E]), ALU.mult).then_inc(routed, 1)
            dve.wait_ge(routed, 7)
            nc.vector.reduce_sum(bounds[:, :], bounds_of[:, :, :], AX.X).then_inc(routed, 1)
            dve.wait_ge(routed, 8)
            nc.vector.scalar_tensor_tensor(place_of[:, :, :], bounds[:, 0:E].unsqueeze(1).to_broadcast([P, NT, E]), float(P),
                                           rank_ps[:, 0:NT, :], ALU.mult, ALU.add).then_inc(routed, 1)
            dve.wait_ge(routed, 9)
            nc.vector.tensor_tensor(oh_place[:, :, :, :], oh[:, :, :, :], place_of[:, :, :].unsqueeze(1).to_broadcast(by_choice),
                                    ALU.mult).then_inc(routed, 1)
            dve.wait_ge(routed, 10)
            nc.vector.reduce_sum(place[:, :], oh_place[:, :, :, :].rearrange("p k t e -> p (k t) e"), AX.X).then_inc(routed, 1)
            dve.wait_ge(routed, 11)
            nc.vector.tensor_copy(place_i[:, :], place[:, :]).then_inc(routed, 1)
            dve.wait_ge(routed, 12)
            nc.vector.tensor_scalar(block_i[:, :], place_i[:, :], P.bit_length() - 1, None,
                                    ALU.logical_shift_right).then_inc(routed, 1)
            dve.wait_ge(routed, 13)
            nc.vector.tensor_copy(block_f[:, :], block_i[:, :]).then_inc(routed, 1)
            dve.wait_ge(routed, 14)
            nc.vector.scalar_tensor_tensor(pos[:, :], block_f[:, :], float(-P), place[:, :], ALU.mult, ALU.add).then_inc(routed, 1)
            by_block = [P, TOP * NT, NB]
            nc.vector.tensor_tensor(table[:, :, 0, :], const("blocks")[:, 0:NB].unsqueeze(1).to_broadcast(by_block),
                                    block_f[:, :].unsqueeze(2).to_broadcast(by_block), ALU.is_equal).then_inc(routed, 1)
            dve.wait_ge(x_stored, 16 * NP)
            dve.wait_ge(routed, 16)

            def position_rows(q):
                j = slice(q * 8, q * 8 + 8)
                nc.vector.tensor_tensor(pos_oh[q], const("positions").unsqueeze(1).to_broadcast([P, 8, P]),
                                        pos[:, j].unsqueeze(2).to_broadcast([P, 8, P]), ALU.is_equal).then_inc(pos_ready, 1)

            dve.wait_ge(gates_split, 2)
            for w in range(2):
                nc.vector.tensor_tensor(table[:, :, 1 + w, :], table[:, :, 0, :],
                                        gate_parts[:, w, :].unsqueeze(2).to_broadcast(by_block), ALU.mult).then_inc(table_ready, 1)
            dve.wait_ge(table_ready, 2)
            for k in range(TOP):
                tiles = table[:, k * NT:(k + 1) * NT, 0, :]
                nc.vector.tensor_tensor(tiles, tiles, const("tokens").unsqueeze(2).to_broadcast([P, NT, NB]),
                                        ALU.mult).then_inc(table_ready, 1)
            for q in range(TOP * NT // 8):
                position_rows(q)
            by_expert = [P, NB + 1, E]
            dve.wait_ge(rows_stored, 16 * NP)
            nc.vector.tensor_tensor(reached[:, :, :], const("blocks").unsqueeze(2).to_broadcast(by_expert),
                                    bounds[:, E:].unsqueeze(1).to_broadcast(by_expert), ALU.is_ge).then_inc(routed, 1)
            dve.wait_ge(routed, 17)
            nc.vector.reduce_sum(owner[:, :], reached[:, :, :], AX.X).then_inc(routed, 1)
            dve.wait_ge(routed, 18)
            nc.vector.tensor_scalar(owner[:, :], owner[:, :], float(E - 1), None, ALU.min).then_inc(routed, 1)
            dve.wait_ge(routed, 19)
            nc.vector.tensor_copy(block_expert[:, :], owner[:, :]).then_inc(experts_ready, 1)
            two_by_two = owner[:, :].rearrange("p (b two) -> p b two", two=2)
            nc.vector.scalar_tensor_tensor(expert_pairs[:, :], two_by_two[:, :, 1], float(E), two_by_two[:, :, 0],
                                           ALU.mult, ALU.add).then_inc(experts_ready, 1)
            dve.wait_ge(table_done, 1)
            nc.vector.tensor_scalar(spare_ids[:, :], table_ps[:, 0:NB], 0.0, const("spare_row"), ALU.is_ge,
                                    ALU.mult).then_inc(routed, 1)
            dve.wait_ge(routed, 20)
            nc.vector.scalar_tensor_tensor(block_rows[:, :], table_ps[:, 0:NB], float(TOKENS), spare_ids[:, :],
                                           ALU.add, ALU.add).then_inc(ids_ready, 1)
            nc.vector.tensor_scalar(block_gates[:, :], table_ps[:, NB:2 * NB], 1 / GSCALE, None, ALU.mult).then_inc(high_gates, 1)
            dve.wait_ge(high_gates, 1)
            nc.vector.scalar_tensor_tensor(block_gates[:, :], table_ps[:, 2 * NB:], 1 / GSCALE, block_gates[:, :],
                                           ALU.mult, ALU.add).then_inc(ids_ready, 1)
            dve.wait_ge(ids_ready, 2)
            nc.vector.tensor_scalar(block_scales[:, :], block_gates[:, :], 1 / WSCALE, None, ALU.mult).then_inc(ids_ready, 1)

            dve.wait_ge(ids_ready, 3)
            dve.wait_ge(experts_ready, 2)
            dve.wait_ge(w_low, 2 * E)

            def copy_w1(i, o, e):
                done = at(dve, 2 * i - 2)
                if not isinstance(i, int) or i >= 2:
                    dve.wait_ge(x0_loaded, 32)
                    dve.wait_ge(first_done, done)
                nc.vector.tensor_copy(w1_now[o], W1[:, bass.ds(e, 1), :, :, :].rearrange("p e k h n -> p (e k) h n")
                                      ).then_inc(w1_copied, 1)

            def move_xgT(i, o):
                dve.wait_ge(first_xg_transposed, i + 1)
                nc.vector.tensor_copy(xgT[o][:, :, :, :], xgT_ps[o]).then_inc(xgT_moved, 1)

            def split_hidden(i, o, half):
                m = slice(half * KF // 2, (half + 1) * KF // 2)
                dve.wait_ge(gelu_done, KF * i + m.stop)
                nc.vector.tensor_copy(hid_hi[o][:, m, :], hid[o][:, m, :]).then_inc(hi_split, 1)
                dve.wait_ge(hi_split, 2 * i + half + 1)
                nc.vector.tensor_tensor(hid_lo[o][:, m, :], hid[o][:, m, :], hid_hi[o][:, m, :],
                                        ALU.subtract).then_inc(lo_split, 1)

            def gated_output(i, o):
                have, before = at(dve, i + 1), at(dve, 16 * i - 16)
                dve.wait_ge(x0_loaded, 32)
                dve.wait_ge(second_done, have)
                dve.wait_ge(gated_b2_ready, have)
                if not isinstance(i, int) or i >= 2:
                    dve.wait_ge(added, before)
                nc.vector.scalar_tensor_tensor(y[o][:, :], y_ps[o], block_scales[:, bass.ds(i, 1)], gated_b2[o][:, :],
                                               ALU.mult, ALU.add).then_inc(y_ready, 1)

            def block_step(two, o, ahead, e):
                i = 2 * two + o
                if ahead >= 2:
                    copy_w1(i + 2, o, e)
                if ahead >= 1:
                    split_hidden(i + 1, 1 - o, 0)
                if ahead >= 1:
                    split_hidden(i + 1, 1 - o, 1)
                gated_output(i, o)

            for i, e in enumerate(expert_pair(dve, 0)):
                copy_w1(i, i, e)
            second_low(12)
            move_xgT(0, 0)
            second_low(13)
            move_xgT(1, 1)
            second_low(14)
            second_low(15)
            split_hidden(0, 0, 0)
            split_hidden(0, 0, 1)
            blocks_in_turn(dve, block_step, experts_of=2)

        @block.tensor
        def _(pe):
            def s1_free(b, u):
                pe.wait_ge(s1_moved, S1_USES * b + u)

            def s2_free(b, u):
                bank, n = s2_slot(b, u)
                pe.wait_ge(s2_moved[bank], n)
                return bank

            def s2_arrived(b, u):
                bank, n = s2_slot(b, u)
                pe.wait_ge(s2_moved[bank], n + 1)

            def transpose_xn(b):
                pe.wait_ge(xn_ready, T * b + T)
                s1_free(b, U_XNT)
                for k in range(KD):
                    for t in range(T):
                        last = nc.tensor.transpose(s1_ps[:, k * SEQ + t * P:k * SEQ + (t + 1) * P],
                                                   xn[:, t, k * P:(k + 1) * P], id_sb[:, :])
                last.then_inc(s1_done, 1)

            def project(b, u, t, lo, n):
                pe.wait_ge(wqkv_loaded, 64)
                s1_free(b, u)
                for k in range(KD):
                    last = nc.tensor.matmul(s1_ps[:, 0:n], xnT[:, k, t * P:(t + 1) * P],
                                            wqkv_sb[:, k, lo:lo + n], start=(k == 0), stop=(k == KD - 1))
                last.then_inc(s1_done, 1)

            def transpose_stack(b, stack, u, r):
                bank = s2_free(b, u)
                dst = s2_ps[bank][:, :].bitcast(F16).rearrange("p (a s) -> p a s", s=SEQ)
                for a in range(4):
                    for t in range(T):
                        pair = 4 * r + a
                        last = nc.tensor.transpose(
                            dst[:, a, t * P:(t + 1) * P],
                            stack[:, t, 2 * pair:2 * pair + 2, :].rearrange("p h r -> p (h r)"), id16[:, :])
                last.then_inc(s2_done, 1)

            def transpose_shifted(b, o, t):
                pe.wait_ge(negm_ready, T * b + t + 1)
                bank = s2_free(b, U_RT[t])
                dst = s2_ps[bank][:, :].bitcast(F16).rearrange("p (a s) -> p a s", s=P)
                for pair in range(PAIRS):
                    last = nc.tensor.transpose(
                        dst[:, pair, :], q_stack[o][:, t, 2 * pair:2 * pair + 2, :].rearrange("p h r -> p (h r)"), id16[:, :])
                last.then_inc(s2_done, 1)

            def row_scores(b, o, first, count):
                for g in range(first, first + count):
                    t, pair = divmod(g, PAIRS)
                    if g in (0, PAIRS // 2):
                        s2_arrived(b, U_QT[g // (PAIRS // 2)])
                        s2_arrived(b, U_KT[g // (PAIRS // 2)])
                    bank = s2_free(b, U_SC[g])
                    if g < 2:
                        pe.wait_ge(even_kT_moved, 2 * b + g + 1)
                    for h in range(2):
                        last = nc.tensor.matmul(s2_ps[bank][:, h * SEQ:(h + 1) * SEQ], qT[:, pair, t * P:(t + 1) * P],
                                                kT[o][:, 2 * pair + h, :], start=True, stop=True)
                    last.then_inc(s2_done, 1)

            def key_scores(b, o, g):
                quad, kt = divmod(g, T)
                if g == 0:
                    for u in U_RT:
                        s2_arrived(b, u)
                    pe.wait_ge(v_moved, KD * NC)
                if g >= 2:
                    pe.wait_ge(exp_done, GROUPS * b + g - 1)
                for n in range(4):
                    h = 4 * quad + n
                    last = nc.tensor.matmul(s_ps[g % 2][:, n, :], kT[o][:, h, kt * P:(kt + 1) * P],
                                            qmT[:, h // 2, :], start=True, stop=True)
                last.then_inc(scores_ready, 1)

            def weigh_values(b, o, g):
                quad, kt = divmod(g, T)
                col = (quad % 2) * SEQ
                if g == 0:
                    pe.wait_ge(v_ready, b + 1)
                if g % 4 == 0:
                    pe.wait_ge(o_moved, 1 + O_USES * b + quad // 2)
                pe.wait_ge(exp_done, GROUPS * b + g + 1)
                for n in range(4):
                    last = nc.tensor.matmul(o_ps[32 * n:32 * n + 32, col:col + SEQ], v1[o][:, kt, 4 * quad + n, :],
                                            probs[g % 2][:, n, :], start=(kt == 0), stop=(kt == T - 1))
                last.then_inc(pv_done, 1)

            def project_out(b, t):
                if t == 0:
                    pe.wait_ge(wo_loaded, 32)
                    pe.wait_ge(oT_ready, 2 * b + 2)
                    pe.wait_ge(o_moved, 1 + O_USES * b + U_WO)
                for quad in range(QUADS):
                    last = nc.tensor.matmul(o_ps[:, t * D:(t + 1) * D], oT[:, quad, t * P:(t + 1) * P],
                                            wo_sb[:, quad, :], start=(quad == 0), stop=(quad == QUADS - 1))
                if t == T - 1:
                    last.then_inc(wo_done, 1)

            def project_features(dst, m, w, rhs):
                for k in range(KD):
                    last = nc.tensor.matmul(dst, w[:, k, m * P:(m + 1) * P], rhs[:, k, :], start=(k == 0), stop=(k == KD - 1))
                return last

            def project_keys(c):
                pe.wait_ge(keys_loaded, KEYS_LOADS)
                pe.wait_ge(ctx_loaded[c], 16)
                for m in range(KD):
                    if c >= 2:
                        pe.wait_ge(v_moved, KD * (c - 2) + m + 1)
                    project_features(key_ps[c % 2][m], m, wxkv_sb[:, 0], ctx_sb[c]).then_inc(k_done, 1)

            def sum_keys(c):
                for m in range(KD):
                    pe.wait_ge(k_heads_ready, KD * c + m + 1)
                    for k in range(m + 1):
                        last = nc.tensor.matmul(key_ps[c % 2][m], cum_sb[:, k, m * P:(m + 1) * P], k_exp[c % 2][:, k, :],
                                                start=(k == 0), stop=(k == m))
                    last.then_inc(cum_done, 1)

            def project_values(c):
                for m in range(KD):
                    pe.wait_ge(cum_moved, KD * c + m + 1)
                    project_features(key_ps[c % 2][m], m, wxkv_sb[:, 1], ctx_sb[c]).then_inc(v_done, 1)

            def x_bank(what, c, part=0):
                _, bank, before = x_use(what, c, part)
                if before > 0:
                    pe.wait_ge(x_moved[bank], before)
                elif bank == 0:
                    pe.wait_ge(s1_moved, S1_USES * BATCH)
                elif bank <= 2:
                    pe.wait_ge(s2_moved[bank - 1], S2_USES // 2 * BATCH)
                else:
                    pe.wait_ge(exp_done, GROUPS * BATCH)
                return x_ps[bank]

            def transpose_rows(what, c, k):
                src, normed = normalised(2 if what == "xT" else 3, c), (xc_normed if what == "xT" else x3_normed)
                pe.wait_ge(normed, tiles_to(c))
                bank = x_bank(what, c, k)
                for t in range(PIECES[c][1]):
                    last = nc.tensor.transpose(bank[:, t * P:(t + 1) * P], src[:, t, k * P:(k + 1) * P], id_sb[:, :])
                last.then_inc(x_done, 1)

            def project_queries(c, m):
                pe.wait_ge(cross_loaded, CROSS_LOADS)
                for k in range(KD):
                    x_left(pe, "xT", c, k)
                project_features(x_bank("q", c, m)[:, 0:PIECES[c][1] * P], m, wxq_sb, xT[:, :, tokens_beside(c)]).then_inc(x_done, 1)

            def project_mixture(c, half):
                pe.wait_ge(mixed_ready, KD * c + KD)
                bank = x_bank("wc", c, half)
                for t in range(2):
                    rows_of = slice((2 * half + t) * P, (2 * half + t + 1) * P)
                    for k in range(KD):
                        last = nc.tensor.matmul(bank[:, t * D:(t + 1) * D], mixture(c, k)[:, rows_of], wxc_sb[:, k, :],
                                                start=(k == 0), stop=(k == KD - 1))
                last.then_inc(x_done, 1)

            def router_values(c):
                for k in range(KD):
                    x_left(pe, "x3T", c, k)
                bank = x_bank("logits", c)
                rows_of = x3T[:, :, tokens_beside(c)]
                for t in range(PIECES[c][1]):
                    for k in range(KD):
                        last = nc.tensor.matmul(bank[:, t * E:(t + 1) * E], rows_of[:, k, t * P:(t + 1) * P],
                                                wr_sb[:, k, :], start=(k == 0), stop=(k == KD - 1))
                last.then_inc(x_done, 1)

            def step(j, o, stages, also):
                s1, s2, s3 = stages

                def probabilities(g):
                    if s3:
                        weigh_values(j, o, g)
                        if g + 2 < GROUPS:
                            key_scores(j, o, g + 2)
                    also(g + 1)

                def s2_scores(first, count):
                    if s2:
                        row_scores(j + 1, 1 - o, first, count)

                if s2:
                    transpose_stack(j + 1, k_stack, U_KT[1], 1)
                also(0)
                if s1:
                    transpose_xn(j + 2)
                s2_scores(0, 1)
                if s3:
                    key_scores(j, o, 0)
                    key_scores(j, o, 1)
                s2_scores(1, 1)
                if s1:
                    project(j + 2, U_QK[0], 0, 0, 2 * D)
                probabilities(0)
                s2_scores(2, 2)
                probabilities(1)
                s2_scores(4, 2)
                probabilities(2)
                s2_scores(6, 1)
                probabilities(3)
                s2_scores(7, 2)
                if s1:
                    project(j + 2, U_QK[1], 1, 0, 2 * D)
                probabilities(4)
                s2_scores(9, 2)
                probabilities(5)
                s2_scores(11, 2)
                probabilities(6)
                s2_scores(13, 1)
                probabilities(7)
                if s2:
                    transpose_shifted(j + 1, 1 - o, 0)
                if s1:
                    project(j + 2, U_V[0], 0, 2 * D, D)
                s2_scores(14, 2)
                if s1:
                    project(j + 2, U_V[1], 1, 2 * D, D)
                also(9)
                if s1:
                    pe.wait_ge(lo_ready, 3 * T * (j + 2) + 3 * T)
                if s3:
                    project_out(j, 0)
                if s2:
                    transpose_shifted(j + 1, 1 - o, 1)
                if s1:
                    transpose_stack(j + 2, q_stack[o], U_QT[0], 0)
                if s3:
                    project_out(j, 1)
                if s1:
                    transpose_stack(j + 2, q_stack[o], U_QT[1], 1)
                    transpose_stack(j + 2, k_stack, U_KT[0], 0)
                also(10)

            def first_keys(n):
                if n == 2:
                    project_keys(0)
                if n == 4:
                    project_keys(1)
                if n == 8:
                    sum_keys(0)
                    sum_keys(1)
                if n == 9:
                    project_values(0)
                if n == 10:
                    project_values(1)
                    project_keys(2)

            def last_keys(n):
                if n == 2:
                    sum_keys(2)
                if n == 3:
                    project_keys(3)
                if n == 5:
                    sum_keys(3)
                if n == 7:
                    project_values(2)
                if n == 9:
                    project_values(3)

            def first_mixing(n):
                if n == 1:
                    transpose_rows("xT", 0, 0)
                if n == 2:
                    transpose_rows("xT", 0, 1)
                if n == 4:
                    project_queries(0, 0)
                if n == 5:
                    project_queries(0, 1)
                if n == 6:
                    transpose_rows("xT", 1, 0)
                if n == 7:
                    transpose_rows("xT", 1, 1)
                if n == 9:
                    project_queries(1, 0)
                if n == 10:
                    project_queries(1, 1)

            def last_mixing(n):
                if n == 1:
                    transpose_rows("xT", 2, 0)
                    transpose_rows("xT", 2, 1)
                if n == 2:
                    project_mixture(0, 0)
                if n == 3:
                    project_mixture(0, 1)
                if n == 4:
                    project_queries(2, 0)
                if n == 5:
                    project_queries(2, 1)
                if n == 6:
                    project_mixture(1, 0)
                if n == 7:
                    project_mixture(1, 1)
                if n == 8:
                    transpose_rows("x3T", 0, 0)
                    transpose_rows("x3T", 0, 1)
                if n == 10:
                    transpose_rows("xT", 3, 0)
                    transpose_rows("xT", 3, 1)

            pe.wait_ge(keys_cleared, 4)
            pe.wait_ge(x0_loaded, 32)
            pe.wait_ge(id16_ready, 1)
            pe.wait_ge(consts_set, 3)
            iterations(pe, step, (first_keys, last_keys), (first_mixing, last_mixing))

            def transpose_both(what, c):
                for k in range(KD):
                    transpose_rows(what, c, k)

            def project_both(project, c):
                for part in halves(c) if project == project_mixture else range(KD):
                    project(c, part)

            router_values(0)
            project_both(project_queries, 3)
            project_both(project_mixture, 2)
            transpose_both("xT", 4)
            project_both(project_queries, 4)
            transpose_both("x3T", 1)
            project_both(project_mixture, 3)
            router_values(1)
            project_both(project_mixture, 4)
            transpose_both("x3T", 2)
            router_values(2)
            transpose_both("x3T", 3)
            router_values(3)
            transpose_both("x3T", 4)
            router_values(4)

            pe.wait_ge(route_loaded, 32)
            pe.wait_ge(choices_ready, 2)
            any_flat = oh_any[:, :, :].rearrange("p t e -> p (t e)")
            rank_flat = s2_ps[0][:, 0:(NT + 1) * E]
            nc.tensor.matmul(rank_flat, rank_sb[:, 0:P], any_flat, start=True, stop=False)
            for t in range(1, NT + 1):
                last = nc.tensor.matmul(rank_flat[:, t * E:], rank_sb[:, P:], any_flat[:, 0:(NT + 1 - t) * E],
                                        start=False, stop=(t == NT))
            last.then_inc(ranks_done, 1)
            pe.wait_ge(table_ready, 2 + TOP)
            for j in range(TOP * NT):
                if j % 8 == 0:
                    pe.wait_ge(pos_ready, j // 8 + 1)
                last = nc.tensor.matmul(table_ps, pos_oh[j // 8][:, j % 8, :], table[:, j, :, :].rearrange("p w b -> p (w b)"),
                                        start=(j == 0), stop=(j == TOP * NT - 1))
            last.then_inc(table_done, 1)

            pe.wait_ge(experts_ready, 2)
            PASSES = ((0, 0), (0, 1), (1, 0))

            def transpose_block(o):
                pe.wait_ge(gathered[o], 16)
                if o == 0:
                    pe.wait_ge(ids_ready, 3)
                for h in range(2):
                    for k in range(KD):
                        last = nc.tensor.transpose(xgT_ps[o][:, h, k, :], xg[o][:, (h * KD + k) * P:(h * KD + k + 1) * P], id16[:, :])
                last.then_inc(first_xg_transposed, 1)

            def first_layer(i, o, turn):
                if isinstance(i, int) and i < 2:
                    pe.wait_ge(xgT_moved, i + 1)
                else:
                    pe.wait_ge(xg_transposed[o], at(pe, 16 * turn))
                pe.wait_ge(w1_copied, i + 1)
                if not isinstance(i, int) or i >= 2:
                    pe.wait_ge(gelu_done, KF * (i - 1))
                for m in range(KF):
                    for n, (wp, xp) in enumerate(PASSES):
                        for k in range(KD):
                            last = nc.tensor.matmul(hid_ps[o][:, m, :], w1_now[o][:, k, wp, m * P:(m + 1) * P], xgT[o][:, xp, k, :],
                                                    start=(n + k == 0), stop=(n == 2 and k == KD - 1))
                    if m % (KF // 2) == KF // 2 - 1:
                        last.then_inc(first_done, 1)

            def second_layer(i, o, e):
                w = W2[:, bass.ds(e, 1), :, :, :]
                if not isinstance(i, int) or i >= 2:
                    pe.wait_ge(y_ready, i - 1)
                for k in range(KF):
                    if k % (KF // 2) == 0:
                        pe.wait_ge(lo_split, 2 * i + k // (KF // 2) + 1)
                    for n, (wp, hp) in enumerate(PASSES):
                        last = nc.tensor.matmul(y_ps[o], (hid_hi, hid_lo)[hp][o][:, k, :], w[:, 0, k, wp, :],
                                                start=(k + n == 0), stop=(n == 2 and k == KF - 1))
                last.then_inc(second_done, 1)

            def block_step(two, o, ahead, e):
                i = 2 * two + o
                if ahead >= 1:
                    first_layer(i + 1, 1 - o, two + o)
                second_layer(i, o, e)

            transpose_block(0)
            transpose_block(1)
            first_layer(0, 0, 0)
            second_split(pe, DVE_HALVES[-1])
            second_split(pe, max(u for u in range(2 * E) if u not in DVE_HALVES))
            blocks_in_turn(pe, block_step, experts_of=0)


def head_halves():
    return np.concatenate([h * DH + np.concatenate([np.arange(0, DH, 2), np.arange(1, DH, 2)]) for h in range(H)])


def quad_rows(w):
    padded = np.zeros((H, 32, w.shape[1]), w.dtype)
    padded[:, :DH] = w.reshape(H, DH, -1)
    return padded.reshape(H * 32, -1)


def kernel(**inputs):
    import concourse.bacc as bacc
    from concourse.bass_utils import run_bass_kernel_spmd

    a = {k: np.asarray(v) for k, v in inputs.items()}
    halves = head_halves()
    cos, sin = rope_tables()
    laid = {
        "x": a["x"].reshape(BATCH * SEQ, D),
        "ctxT": a["ctx_1024"].reshape(BATCH * SEQ, D).T,
        "w_qkv": np.concatenate([a["L0_attn_Wq"].T[:, halves], a["L0_attn_Wk"].T[:, halves], a["L0_attn_Wv"].T], 1),
        "b_qkv": np.concatenate([a["L0_attn_bq"][halves], a["L0_attn_bk"][halves], a["L0_attn_bv"]]),
        "w_o": quad_rows(a["L0_attn_Wo"].T),
        "b_o": a["L0_attn_bo"],
        "wx_q": a["L0_xattn_wq_w"], "wx_k": a["L0_xattn_wk_w"], "wx_v": a["L0_xattn_wv_w"], "wx_c": a["L0_xattn_wc_w"],
        "bx_q": a["L0_xattn_wq_b"], "bx_k": a["L0_xattn_wk_b"], "bx_v": a["L0_xattn_wv_b"], "bx_c": a["L0_xattn_wc_b"],
        "wr": a["L0_ffn_Wr"], "br": a["L0_ffn_br"], "w1": a["L0_ffn_W1"], "b1": a["L0_ffn_b1"].reshape(-1),
        "w2": a["L0_ffn_W2"], "b2": a["L0_ffn_b2"],
        "rank_m": rank_matrices(), "route_c": np.concatenate(list(routing_constants().values()), 1),
        "spare_x": np.zeros((ROWS - TOKENS, D), np.float32), "spare_rows": np.zeros((ROWS - TOKENS, 2 * D), np.float16),
        "cos": cos, "sin": sin, "cumsum_m": head_cumsum_matrix(), "ident": np.eye(P, dtype=np.float32),
    }
    nc = bacc.Bacc("TRN2", target_bir_lowering=False, num_devices=1)
    arrays, args = {}, {}
    for name, value in laid.items():
        value = np.ascontiguousarray(value)
        arrays[f"in_{name}"] = value
        args[name] = nc.dram_tensor(f"in_{name}", value.shape, mybir.dt.from_np(value.dtype), kind="ExternalInput").ap()
    rows = nc.dram_tensor("rows", (ROWS, 2 * D), F16, kind="Internal").ap()
    out = nc.dram_tensor("out_0", (ROWS, D), F32, kind="ExternalOutput").ap()
    build(nc, rows=rows, out=out, **args)
    got = run_bass_kernel_spmd(nc, [arrays], core_ids=[0]).results[0]["out_0"]
    return got[:TOKENS].reshape(BATCH, SEQ, D)
```
